# Optimizing a Trainium2 kernel written in Bass

```python
import numpy as np
import jax
import jax.numpy as jnp

def _softmax(x, axis=-1):
    return jax.nn.softmax(x, axis=axis)

def _gelu(x):
    return jax.nn.gelu(x, approximate=True)

def _silu(x):
    return jax.nn.silu(x)

def _sigmoid(x):
    return jax.nn.sigmoid(x)

def _layernorm(x, axis=-1, eps=1e-05):
    m = jnp.mean(x, axis=axis, keepdims=True)
    v = jnp.var(x, axis=axis, keepdims=True)
    return (x - m) / jnp.sqrt(v + eps)

def _scatter_add(tgt, idx, src, axis=0):
    return tgt.at[idx].add(src)

def _segment_sum(src, seg, n):
    return jax.ops.segment_sum(src, seg, n)
kernel_name = 'mk_seq_preln_d1_jaxref_r4_a6b784'

def setup_inputs(seed: int=0):
    np.random.seed(seed)
    _w = jnp.asarray

    def _L0_attn_setup():
        import jax, jax.numpy as jnp
        import numpy as np
        D = 256
        K = 4
        H = 2
        BITS = 9
        BUCKETS = 128
        ASSOC = 2
        KEY_DIM = 32
        MEM_DIM = 32
        CONV_K = 4

        def _rms_norm(x, eps=1e-06):
            return x * jax.lax.rsqrt(jnp.mean(x * x, axis=-1, keepdims=True) + eps)
        key = jax.random.key(seed)
        ks = jax.random.split(key, 20)

        def w(k, shape, fan_in):
            return jax.random.normal(k, shape, jnp.float32) / np.sqrt(float(fan_in))
        B, T, d = (4, 128, D)
        hidden = 4 * d
        return {'x': jax.random.normal(ks[0], (B, T, d), jnp.float32), 'conv_w': w(ks[1], (d, CONV_K), CONV_K), 'gate_w': w(ks[2], (d, d), d), 'gate_b': jnp.zeros((d,), jnp.float32), 'mlp_up_w': w(ks[3], (hidden, d), d), 'mlp_up_b': jnp.zeros((hidden,), jnp.float32), 'mlp_down_w': w(ks[4], (d, hidden), hidden), 'mlp_down_b': jnp.zeros((d,), jnp.float32), 'state_in_w': w(ks[5], (K * d, d), d), 'state_out_w': w(ks[6], (d, K * d), K * d), 'state_decay_logit': jax.random.normal(ks[7], (K,), jnp.float32) + 2.0, 'read_bits_w': w(ks[8], (H * BITS, d), d), 'write_bits_w': w(ks[9], (H * BITS, d), d), 'qkey_w': w(ks[10], (KEY_DIM, d), d), 'wkey_w': w(ks[11], (KEY_DIM, d), d), 'value_w': w(ks[12], (MEM_DIM, d), d), 'mem_out_w': w(ks[13], (d, MEM_DIM), MEM_DIM), 'write_gate_w': w(ks[14], (1, d), d), 'write_gate_b': jnp.zeros((1,), jnp.float32), 'gate_long_w': w(ks[15], (1, d), d), 'gate_long_b': jnp.zeros((1,), jnp.float32), 'gate_mem_w': w(ks[16], (1, d), d), 'gate_mem_b': jnp.zeros((1,), jnp.float32)}
    _L0_attn_in = _L0_attn_setup()

    def _L0_ffn_setup():
        import jax, jax.numpy as jnp
        import numpy as np
        DIM = 256
        DEPTH = 2
        HEADS = 8
        DIM_HEAD = 64
        WINDOW = 128
        INNER = HEADS * DIM_HEAD
        HID = int(DIM * 4 * 2 / 3)
        B, N = (2, 2048)
        QK_SCALE = 8.0

        def shift_token(t):
            t1, t2 = jnp.split(t, 2, axis=-1)
            t2 = jnp.pad(t2, ((0, 0), (1, 0), (0, 0)))[:, :-1]
            return jnp.concatenate([t1, t2], axis=-1)

        def l2norm(t):
            return t / jnp.clip(jnp.linalg.norm(t, axis=-1, keepdims=True), 1e-12)

        def rotate_half(x):
            x1, x2 = jnp.split(x, 2, axis=-1)
            return jnp.concatenate([-x2, x1], axis=-1)

        def rotary_xpos(q, k):
            n = q.shape[-2]
            half_idx = jnp.arange(0, DIM_HEAD, 2, dtype=jnp.float32)
            inv_freq = 1.0 / 10000.0 ** (half_idx / DIM_HEAD)
            t = jnp.arange(n, dtype=jnp.float32)
            freqs = t[:, None] * inv_freq[None, :]
            freqs = jnp.concatenate([freqs, freqs], axis=-1)
            base = (half_idx + 0.4 * DIM_HEAD) / (1.4 * DIM_HEAD)
            power = (t - n // 2) / float(WINDOW // 2)
            scale = base[None, :] ** power[:, None]
            scale = jnp.concatenate([scale, scale], axis=-1)
            cos, sin = (jnp.cos(freqs), jnp.sin(freqs))
            q = q * cos * scale + rotate_half(q) * sin * scale
            k = k * cos / scale + rotate_half(k) * sin / scale
            return (q, k)

        def local_attention(q, k, v):
            b, h, n, d = q.shape
            w = n // WINDOW
            bq = q.reshape(b, h, w, WINDOW, d) * QK_SCALE
            bk = k.reshape(b, h, w, WINDOW, d)
            bv = v.reshape(b, h, w, WINDOW, d)

            def look_around(t):
                p = jnp.pad(t, ((0, 0), (0, 0), (1, 0), (0, 0), (0, 0)))
                return jnp.concatenate([p[:, :, :w], p[:, :, 1:]], axis=3)
            bk, bv = (look_around(bk), look_around(bv))
            bt = jnp.arange(n).reshape(w, WINDOW)
            btp = jnp.pad(bt, ((1, 0), (0, 0)), constant_values=-1)
            btk = jnp.concatenate([btp[:w], btp[1:]], axis=1)
            sim = jnp.einsum('bhwid,bhwjd->bhwij', bq, bk)
            i = bt[:, :, None]
            j = btk[:, None, :]
            mask = (i < j) | (i > j + WINDOW) | (j == -1)
            sim = jnp.where(mask, -jnp.finfo(sim.dtype).max, sim)
            attn = jax.nn.softmax(sim, axis=-1)
            out = jnp.einsum('bhwij,bhwjd->bhwid', attn, bv)
            return out.reshape(b, h, n, d)

        def _layer(x, wqkv, qs, ksc, wo, lg, lb, w1, b1, w2, b2):
            b, n, _ = x.shape
            h = shift_token(x)
            qkv = h @ wqkv
            q, k, v = jnp.split(qkv, 3, axis=-1)
            to_heads = lambda t: t.reshape(b, n, HEADS, DIM_HEAD).transpose(0, 2, 1, 3)
            q, k, v = (to_heads(q), to_heads(k), to_heads(v))
            q = l2norm(q) * qs
            k = l2norm(k) * ksc
            q, k = rotary_xpos(q, k)
            o = local_attention(q, k, v)
            o = o.transpose(0, 2, 1, 3).reshape(b, n, INNER)
            x = x + o @ wo
            h = shift_token(x)
            mu = h.mean(-1, keepdims=True)
            var = h.var(-1, keepdims=True)
            h = (h - mu) / jnp.sqrt(var + 1e-05) * lg + lb
            h = h @ w1 + b1
            a, g = jnp.split(h, 2, axis=-1)
            h = a * jax.nn.gelu(g, approximate=False)
            x = x + h @ w2 + b2
            return x
        key = jax.random.key(seed)
        ks = jax.random.split(key, 6)
        return {'x': jax.random.normal(ks[0], (B, N, DIM), jnp.float32), 'wqkv': jax.random.normal(ks[1], (DEPTH, DIM, 3 * INNER), jnp.float32) * 0.02, 'q_scale': jnp.ones((DEPTH, DIM_HEAD), jnp.float32), 'k_scale': jnp.ones((DEPTH, DIM_HEAD), jnp.float32), 'wo': jax.random.normal(ks[2], (DEPTH, INNER, DIM), jnp.float32) * 0.02, 'ln_g': jnp.ones((DEPTH, DIM), jnp.float32), 'ln_b': jnp.zeros((DEPTH, DIM), jnp.float32), 'w1': jax.random.normal(ks[3], (DEPTH, DIM, 2 * HID), jnp.float32) * 0.02, 'b1': jnp.zeros((DEPTH, 2 * HID), jnp.float32), 'w2': jax.random.normal(ks[4], (DEPTH, HID, DIM), jnp.float32) * 0.02, 'b2': jnp.zeros((DEPTH, DIM), jnp.float32)}
    _L0_ffn_in = _L0_ffn_setup()
    _d = {'L0_attn_x': _L0_attn_in['x'], 'L0_attn_conv_w': _L0_attn_in['conv_w'], 'L0_attn_gate_w': _L0_attn_in['gate_w'], 'L0_attn_gate_b': _L0_attn_in['gate_b'], 'L0_attn_mlp_up_w': _L0_attn_in['mlp_up_w'], 'L0_attn_mlp_up_b': _L0_attn_in['mlp_up_b'], 'L0_attn_mlp_down_w': _L0_attn_in['mlp_down_w'], 'L0_attn_mlp_down_b': _L0_attn_in['mlp_down_b'], 'L0_attn_state_in_w': _L0_attn_in['state_in_w'], 'L0_attn_state_out_w': _L0_attn_in['state_out_w'], 'L0_attn_state_decay_logit': _L0_attn_in['state_decay_logit'], 'L0_attn_read_bits_w': _L0_attn_in['read_bits_w'], 'L0_attn_write_bits_w': _L0_attn_in['write_bits_w'], 'L0_attn_qkey_w': _L0_attn_in['qkey_w'], 'L0_attn_wkey_w': _L0_attn_in['wkey_w'], 'L0_attn_value_w': _L0_attn_in['value_w'], 'L0_attn_mem_out_w': _L0_attn_in['mem_out_w'], 'L0_attn_write_gate_w': _L0_attn_in['write_gate_w'], 'L0_attn_write_gate_b': _L0_attn_in['write_gate_b'], 'L0_attn_gate_long_w': _L0_attn_in['gate_long_w'], 'L0_attn_gate_long_b': _L0_attn_in['gate_long_b'], 'L0_attn_gate_mem_w': _L0_attn_in['gate_mem_w'], 'L0_attn_gate_mem_b': _L0_attn_in['gate_mem_b'], 'L0_ffn_wqkv': _L0_ffn_in['wqkv'], 'L0_ffn_q_scale': _L0_ffn_in['q_scale'], 'L0_ffn_k_scale': _L0_ffn_in['k_scale'], 'L0_ffn_wo': _L0_ffn_in['wo'], 'L0_ffn_ln_g': _L0_ffn_in['ln_g'], 'L0_ffn_ln_b': _L0_ffn_in['ln_b'], 'L0_ffn_w1': _L0_ffn_in['w1'], 'L0_ffn_b1': _L0_ffn_in['b1'], 'L0_ffn_w2': _L0_ffn_in['w2'], 'L0_ffn_b2': _L0_ffn_in['b2']}
    _x0 = _d['L0_attn_x']
    _d['L0_attn_x'] = jax.random.normal(jax.random.fold_in(jax.random.key(seed), 1), (4, 1024, 256), dtype=_x0.dtype)
    del _x0
    return _d

def reference(L0_attn_x, L0_attn_conv_w, L0_attn_gate_w, L0_attn_gate_b, L0_attn_mlp_up_w, L0_attn_mlp_up_b, L0_attn_mlp_down_w, L0_attn_mlp_down_b, L0_attn_state_in_w, L0_attn_state_out_w, L0_attn_state_decay_logit, L0_attn_read_bits_w, L0_attn_write_bits_w, L0_attn_qkey_w, L0_attn_wkey_w, L0_attn_value_w, L0_attn_mem_out_w, L0_attn_write_gate_w, L0_attn_write_gate_b, L0_attn_gate_long_w, L0_attn_gate_long_b, L0_attn_gate_mem_w, L0_attn_gate_mem_b, L0_ffn_wqkv, L0_ffn_q_scale, L0_ffn_k_scale, L0_ffn_wo, L0_ffn_ln_g, L0_ffn_ln_b, L0_ffn_w1, L0_ffn_b1, L0_ffn_w2, L0_ffn_b2):

    def _L0_attn_ref(x, conv_w, gate_w, gate_b, mlp_up_w, mlp_up_b, mlp_down_w, mlp_down_b, state_in_w, state_out_w, state_decay_logit, read_bits_w, write_bits_w, qkey_w, wkey_w, value_w, mem_out_w, write_gate_w, write_gate_b, gate_long_w, gate_long_b, gate_mem_w, gate_mem_b):
        import jax, jax.numpy as jnp
        import numpy as np
        D = 256
        K = 4
        H = 2
        BITS = 9
        BUCKETS = 128
        ASSOC = 2
        KEY_DIM = 32
        MEM_DIM = 32
        CONV_K = 4

        def _rms_norm(x, eps=1e-06):
            return x * jax.lax.rsqrt(jnp.mean(x * x, axis=-1, keepdims=True) + eps)
        B, T, d = x.shape
        xn = _rms_norm(x)
        xp = jnp.pad(xn, ((0, 0), (CONV_K - 1, 0), (0, 0)))
        h = sum((xp[:, j:j + T, :] * conv_w[:, j] for j in range(CONV_K)))
        u = jax.nn.silu(h) * jax.nn.sigmoid(xn @ gate_w.T + gate_b)
        inp = (u @ state_in_w.T).reshape(B, T, K, d)
        decay = jax.nn.sigmoid(state_decay_logit)[:, None]

        def ssm_step(s, it):
            s = decay * s + it
            return (s, s)
        _, s_seq = jax.lax.scan(ssm_step, jnp.zeros((B, K, d), x.dtype), jnp.swapaxes(inp, 0, 1))
        long = (s_seq.reshape(T, B, K * d) @ state_out_w.T).swapaxes(0, 1)
        bit_pows = (2 ** jnp.arange(BITS)).astype(jnp.int32)

        def route(z):
            return jnp.sum((z > 0).astype(jnp.int32) * bit_pows, axis=-1)
        ridx = route((u @ read_bits_w.T).reshape(B, T, H, BITS))
        widx = route((u @ write_bits_w.T).reshape(B, T, H, BITS))
        qk = u @ qkey_w.T
        wk = u @ wkey_w.T
        wv = u @ value_w.T
        wg = jax.nn.sigmoid(u @ write_gate_w.T + write_gate_b)
        bI = jnp.arange(B)[:, None]
        hI = jnp.arange(H)[None, :]
        scale = np.float32(1.0 / np.sqrt(KEY_DIM))

        def mem_step(carry, xs):
            mem_k, mem_v, mem_last = carry
            ri, wi, q, k_, v_, g_ = xs
            keys = mem_k[bI, hI, ri]
            vals = mem_v[bI, hI, ri]
            scores = jnp.einsum('bhak,bk->bha', keys, q) * scale
            attn = jax.nn.softmax(scores.reshape(B, H * ASSOC), axis=-1).reshape(B, H, ASSOC)
            read = jnp.einsum('bha,bham->bm', attn, vals)
            slot = (mem_last[bI, hI, wi] + 1) % ASSOC
            g3 = g_[:, :, None]
            old_k = mem_k[bI, hI, wi, slot]
            old_v = mem_v[bI, hI, wi, slot]
            new_k = old_k + g3 * (k_[:, None, :] - old_k)
            new_v = old_v + g3 * (v_[:, None, :] - old_v)
            mem_k = mem_k.at[bI, hI, wi, slot].set(new_k)
            mem_v = mem_v.at[bI, hI, wi, slot].set(new_v)
            mem_last = mem_last.at[bI, hI, wi].set(slot)
            return ((mem_k, mem_v, mem_last), read)
        carry0 = (jnp.zeros((B, H, BUCKETS, ASSOC, KEY_DIM), x.dtype), jnp.zeros((B, H, BUCKETS, ASSOC, MEM_DIM), x.dtype), jnp.full((B, H, BUCKETS), -1, jnp.int32))
        xs = (jnp.swapaxes(ridx, 0, 1), jnp.swapaxes(widx, 0, 1), jnp.swapaxes(qk, 0, 1), jnp.swapaxes(wk, 0, 1), jnp.swapaxes(wv, 0, 1), jnp.swapaxes(wg, 0, 1))
        _, reads = jax.lax.scan(mem_step, carry0, xs)
        mem_read = (reads @ mem_out_w.T).swapaxes(0, 1)
        gl = jax.nn.sigmoid(u @ gate_long_w.T + gate_long_b)
        gm = jax.nn.sigmoid(u @ gate_mem_w.T + gate_mem_b)
        y = x + gl * long + gm * mem_read
        yn = _rms_norm(y)
        out = y + (jax.nn.silu(yn @ mlp_up_w.T + mlp_up_b) @ mlp_down_w.T + mlp_down_b)
        return out

    def _L0_ffn_ref(x, wqkv, q_scale, k_scale, wo, ln_g, ln_b, w1, b1, w2, b2):
        import jax, jax.numpy as jnp
        import numpy as np
        DIM = 256
        DEPTH = 2
        HEADS = 8
        DIM_HEAD = 64
        WINDOW = 128
        INNER = HEADS * DIM_HEAD
        HID = int(DIM * 4 * 2 / 3)
        B, N = (2, 2048)
        QK_SCALE = 8.0

        def shift_token(t):
            t1, t2 = jnp.split(t, 2, axis=-1)
            t2 = jnp.pad(t2, ((0, 0), (1, 0), (0, 0)))[:, :-1]
            return jnp.concatenate([t1, t2], axis=-1)

        def l2norm(t):
            return t / jnp.clip(jnp.linalg.norm(t, axis=-1, keepdims=True), 1e-12)

        def rotate_half(x):
            x1, x2 = jnp.split(x, 2, axis=-1)
            return jnp.concatenate([-x2, x1], axis=-1)

        def rotary_xpos(q, k):
            n = q.shape[-2]
            half_idx = jnp.arange(0, DIM_HEAD, 2, dtype=jnp.float32)
            inv_freq = 1.0 / 10000.0 ** (half_idx / DIM_HEAD)
            t = jnp.arange(n, dtype=jnp.float32)
            freqs = t[:, None] * inv_freq[None, :]
            freqs = jnp.concatenate([freqs, freqs], axis=-1)
            base = (half_idx + 0.4 * DIM_HEAD) / (1.4 * DIM_HEAD)
            power = (t - n // 2) / float(WINDOW // 2)
            scale = base[None, :] ** power[:, None]
            scale = jnp.concatenate([scale, scale], axis=-1)
            cos, sin = (jnp.cos(freqs), jnp.sin(freqs))
            q = q * cos * scale + rotate_half(q) * sin * scale
            k = k * cos / scale + rotate_half(k) * sin / scale
            return (q, k)

        def local_attention(q, k, v):
            b, h, n, d = q.shape
            w = n // WINDOW
            bq = q.reshape(b, h, w, WINDOW, d) * QK_SCALE
            bk = k.reshape(b, h, w, WINDOW, d)
            bv = v.reshape(b, h, w, WINDOW, d)

            def look_around(t):
                p = jnp.pad(t, ((0, 0), (0, 0), (1, 0), (0, 0), (0, 0)))
                return jnp.concatenate([p[:, :, :w], p[:, :, 1:]], axis=3)
            bk, bv = (look_around(bk), look_around(bv))
            bt = jnp.arange(n).reshape(w, WINDOW)
            btp = jnp.pad(bt, ((1, 0), (0, 0)), constant_values=-1)
            btk = jnp.concatenate([btp[:w], btp[1:]], axis=1)
            sim = jnp.einsum('bhwid,bhwjd->bhwij', bq, bk)
            i = bt[:, :, None]
            j = btk[:, None, :]
            mask = (i < j) | (i > j + WINDOW) | (j == -1)
            sim = jnp.where(mask, -jnp.finfo(sim.dtype).max, sim)
            attn = jax.nn.softmax(sim, axis=-1)
            out = jnp.einsum('bhwij,bhwjd->bhwid', attn, bv)
            return out.reshape(b, h, n, d)

        def _layer(x, wqkv, qs, ksc, wo, lg, lb, w1, b1, w2, b2):
            b, n, _ = x.shape
            h = shift_token(x)
            qkv = h @ wqkv
            q, k, v = jnp.split(qkv, 3, axis=-1)
            to_heads = lambda t: t.reshape(b, n, HEADS, DIM_HEAD).transpose(0, 2, 1, 3)
            q, k, v = (to_heads(q), to_heads(k), to_heads(v))
            q = l2norm(q) * qs
            k = l2norm(k) * ksc
            q, k = rotary_xpos(q, k)
            o = local_attention(q, k, v)
            o = o.transpose(0, 2, 1, 3).reshape(b, n, INNER)
            x = x + o @ wo
            h = shift_token(x)
            mu = h.mean(-1, keepdims=True)
            var = h.var(-1, keepdims=True)
            h = (h - mu) / jnp.sqrt(var + 1e-05) * lg + lb
            h = h @ w1 + b1
            a, g = jnp.split(h, 2, axis=-1)
            h = a * jax.nn.gelu(g, approximate=False)
            x = x + h @ w2 + b2
            return x
        for l in range(DEPTH):
            x = _layer(x, wqkv[l], q_scale[l], k_scale[l], wo[l], ln_g[l], ln_b[l], w1[l], b1[l], w2[l], b2[l])
        return x
    x = L0_attn_x
    x = x + _L0_attn_ref(_layernorm(x, axis=-1), L0_attn_conv_w, L0_attn_gate_w, L0_attn_gate_b, L0_attn_mlp_up_w, L0_attn_mlp_up_b, L0_attn_mlp_down_w, L0_attn_mlp_down_b, L0_attn_state_in_w, L0_attn_state_out_w, L0_attn_state_decay_logit, L0_attn_read_bits_w, L0_attn_write_bits_w, L0_attn_qkey_w, L0_attn_wkey_w, L0_attn_value_w, L0_attn_mem_out_w, L0_attn_write_gate_w, L0_attn_write_gate_b, L0_attn_gate_long_w, L0_attn_gate_long_b, L0_attn_gate_mem_w, L0_attn_gate_mem_b)
    x = x + _L0_ffn_ref(_layernorm(x, axis=-1), L0_ffn_wqkv, L0_ffn_q_scale, L0_ffn_k_scale, L0_ffn_wo, L0_ffn_ln_g, L0_ffn_ln_b, L0_ffn_w1, L0_ffn_b1, L0_ffn_w2, L0_ffn_b2)
    return x

_drawn_inputs = setup_inputs


def setup_inputs(seed=0):
    import zlib

    import numpy as np

    out = dict(_drawn_inputs(seed))
    spreads = {'L0_attn_gate_b': (0.0, 0.634),
     'L0_attn_mlp_up_b': (0.0, 0.292),
     'L0_attn_mlp_down_b': (0.0, 0.1),
     'L0_ffn_q_scale': (1.0, 0.6),
     'L0_ffn_k_scale': (1.0, 0.6),
     'L0_ffn_ln_g': (1.0, 0.6),
     'L0_ffn_ln_b': (0.0, 0.8),
     'L0_ffn_b1': (0.0, 0.8),
     'L0_ffn_b2': (0.0, 0.313)}
    factors = {'L0_attn_read_bits_w': 7.734,
     'L0_attn_write_bits_w': 3.957,
     'L0_attn_qkey_w': 8.0,
     'L0_attn_wkey_w': 8.0,
     'L0_attn_value_w': 5.738,
     'L0_attn_mem_out_w': 5.833,
     'L0_attn_write_gate_w': 8.0,
     'L0_attn_gate_mem_w': 8.0,
     'L0_ffn_wqkv': 3.256,
     'L0_ffn_wo': 3.082,
     'L0_ffn_w1': 3.625,
     'L0_ffn_w2': 3.605}
    for name, (base, spread) in spreads.items():
        noise = np.random.default_rng([zlib.crc32(name.encode()), seed]).standard_normal(out[name].shape)
        drawn = base * np.exp(spread * noise) if base else spread * noise
        out[name] = jnp.asarray(drawn.astype(out[name].dtype))
    for name, factor in factors.items():
        out[name] = (out[name] * factor).astype(out[name].dtype)
    return out
```

```python
from contextlib import ExitStack

import numpy as np

import concourse.bass as bass
from concourse import mybir

F32 = mybir.dt.float32
ALU = mybir.AluOpType
ACT = mybir.ActivationFunctionType
AX = mybir.AxisListType.X

P = 128
B, T, D = 4, 1024, 256
NW = T // P
NC = D // P
DEPTH, HEADS, DH = 2, 8, 64
INNER = HEADS * DH
NHP = HEADS // 2
HID = int(D * 4 * 2 / 3)
NM = -(-HID // P)
QK_SCALE = 8.0
LN_EPS = 1e-5
MASKED = -1e30
GT = 512
WPG = GT // P
NG = T // GT


def rows(m):
    return min(P, HID - m * P)


def head_of(unit, i):
    return 4 * (unit // 2) + 2 * i + unit % 2


def bcast(ap, at, n):
    names = [f"d{i}" for i in range(len(ap.shape) - 1)]
    out = names[:at] + ["o"] + names[at:]
    src = names[:at] + [f"(o {names[at]})"] + names[at + 1:] if at < len(names) else names[:-1] + [f"({names[-1]} o)"]
    r = ap.rearrange(f"p {' '.join(src)} -> p {' '.join(out)}", o=1)
    shape = list(r.shape)
    shape[at + 1] = n
    return r.to_broadcast(shape)


def ffn_units():
    order = [("A", "xT", 0), ("A", "xT", 1)]
    for w in range(NW):
        order += [("A", "qT", w), ("A", "kT", w), ("D", "sim", w, 0), ("D", "sim", w, 1)]
        if w + 2 < NW:
            order.append(("A", "xT", w + 2))
        order += [("D", "sim", w, 2), ("D", "sim", w, 3)]
        if w >= 1:
            order += [("A", "oT", w - 1), ("D", "wo", w - 1)]
        order += [("A", "pT", w, hp) for hp in range(NHP)]
    order += [("A", "zT", w) for w in range(WPG)]
    order += [("A", "oT", NW - 1), ("D", "wo", NW - 1)]
    for g in range(NG):
        if g:
            order += [("A", "zT", w) for w in range(g * WPG, (g + 1) * WPG)]
        for m in range(NM):
            order += [("A", "gate", g, m), ("D", "up", g, m)]
        order += [("D", "down", w) for w in range(g * WPG, (g + 1) * WPG)]
    index = {"A": {}, "D": {}}
    for ring, *key in order:
        index[ring][tuple(key)] = len(index[ring])
    return index["A"], index["D"]


def build_ffn(nc, x2, x1, y0, out, wqkv, wo, w1, w2, pvec, qs2, b2, tabc, tabs, ident, maskd):
    A, Dn = ffn_units()
    NA, ND = len(A), len(Dn)
    with ExitStack() as ctx:
        def sb(name, shape, dt=F32):
            return ctx.enter_context(nc.sbuf_tensor(name, shape, dt))

        def psum(name, shape):
            return ctx.enter_context(nc.psum_tensor(name, shape, F32))

        def sem(name):
            return ctx.enter_context(nc.semaphore(name))

        Wqkv = [sb(f"Wqkv{i}", [P, NC, 3 * INNER]) for i in range(DEPTH)]
        Wo = [sb(f"Wo{i}", [P, NHP, D]) for i in range(DEPTH)]
        W1 = [sb(f"W1{i}", [P, NC, 2 * HID]) for i in range(DEPTH)]
        W2 = [sb(f"W2{i}", [P, NM, D]) for i in range(DEPTH)]
        Pv = sb("Pv", [P, DEPTH, 2 * NM + 2 * NC])
        Qs = sb("Qs", [P, DEPTH, 2, 2, DH])
        B2 = sb("B2", [P, DEPTH, D])
        TabC = sb("TabC", [P, NW, 2, DH])
        TabS = sb("TabS", [P, NW, 2, DH])
        Cs = sb("Cs", [P, NW, 2, DH])
        Ss = sb("Ss", [P, NW, 2, DH])
        Id = sb("Id", [P, P])
        Mk = sb("Mk", [P, 2, P])
        Half = sb("Half", [P, 2 * HEADS])
        X = sb("X", [P, NW, D])
        X1 = sb("X1", [P, NW, D])
        XS = sb("XS", [P, NW, P])
        XT = sb("XT", [P, NC, T + 1])
        QKr = sb("QKr", [P, 2, 2, HEADS, DH])
        T2 = sb("T2", [P, 2, HEADS, DH])
        Sq = sb("Sq", [P, 2 * HEADS, DH])
        Ssum = sb("Ssum", [P, 2 * HEADS])
        Rn = sb("Rn", [P, 2 * HEADS])
        V = sb("V", [P, 4, INNER])
        KT = sb("KT", [P, 4, NHP, P])
        QT = sb("QT", [P, NHP, P])
        SM = sb("SM", [P, NHP, 2, 2, P])
        Mx = sb("Mx", [P, HEADS])
        Nb = sb("Nb", [P, HEADS])
        Rs = sb("Rs", [P, 2, HEADS])
        Ri = sb("Ri", [P, HEADS])
        PT = sb("PT", [P, NHP, 2, 2, P])
        On = sb("On", [P, HEADS, DH])
        OT = sb("OT", [P, NHP, P])
        Bn = sb("Bn", [P, 2, 6])
        Mv = sb("Mv", [P, NW, 2])
        Ve = sb("Ve", [P, NW])
        Rd = sb("Rd", [P, NW])
        Z = sb("Z", [P, NW, D])
        ZT = sb("ZT", [P, NC, T])
        G = sb("G", [P, 2, GT])
        HT = sb("HT", [P, NM, GT])

        qkv_ps = psum("qkv_ps", [P, 3, 512])
        a_ps = psum("a_ps", [P, 2, 512])
        d_ps = psum("d_ps", [P, 2, 512])
        o_ps = psum("o_ps", [P, 512])

        s_wt = [sem(f"wt{i}") for i in range(DEPTH)]
        s_cst = sem("cst")
        s_set = sem("set")
        s_x = [sem(f"x_in{w}") for w in range(NW)]
        s_sh = [sem(f"shift{w}") for w in range(NW)]
        s_st = [sem(f"stored{w}") for w in range(NW)]
        a_ready, a_free = sem("a_ready"), sem("a_free")
        d_ready, d_free = sem("d_ready"), sem("d_free")
        qkv_ready = sem("qkv_ready")
        qkv_read_act, qkv_read_dve = sem("qkv_read_act"), sem("qkv_read_dve")
        sq_done = sem("sq_done")
        ssum_done = sem("ssum_done")
        rot_terms = sem("rot_terms")
        rn_done = sem("rn_done")
        qkr_sum = sem("qkr_sum")
        qk_rot = sem("qk_rot")
        tabs_done = sem("tabs_done")
        nb_done = sem("nb_done")
        exp_done = sem("exp_done")
        o_ready, o_norm = sem("o_ready"), sem("o_norm")
        xmid = sem("xmid")
        ve_done = sem("ve_done")
        rd_done = sem("rd_done")
        z_done = sem("z_done")
        b2_added = sem("b2_added")
        gelu_done = sem("gelu_done")
        ht_done = sem("ht_done")
        fin_done = sem("fin_done")
        v_chain = sem("v_chain")
        bn_seen = sem("bn_seen")

        stages = [(x2, y0), (y0, out)]

        with nc.Block() as block:

            @block.sync
            def _(sp):
                for dst, src in ((Id[:], ident), (TabC[:], tabc.rearrange("(w p) a d -> p w a d", p=P)),
                                 (TabS[:], tabs.rearrange("(w p) a d -> p w a d", p=P)), (Mk[:], maskd),
                                 (Pv[:], pvec), (Qs[:], qs2), (B2[:], b2)):
                    sp.dma_start(dst, src).then_inc(s_cst, 16)
                for i in range(DEPTH):
                    sp.dma_start(Wqkv[i][:], wqkv[i].rearrange("(c p) n -> p c n", p=P)).then_inc(s_wt[i], 16)
                    sp.dma_start(Wo[i][:], wo[i].rearrange("(c p) n -> p c n", p=P)).then_inc(s_wt[i], 16)
                    sp.dma_start(W1[i][:], w1[i].rearrange("(c p) n -> p c n", p=P)).then_inc(s_wt[i], 16)
                    full = (NM - 1) * P
                    sp.dma_start(W2[i][:, 0:NM - 1, :], w2[i, 0:full].rearrange("(c p) n -> p c n", p=P)).then_inc(s_wt[i], 16)
                    sp.dma_start(W2[i][0:HID - full, NM - 1, :], w2[i, full:HID]).then_inc(s_wt[i], 16)
                for layer, (src, _dst) in enumerate(stages):
                    with sp.Fori(0, B) as b:
                        it = b + layer * B
                        for w in range(NW):
                            sp.wait_ge(s_st[w], it * 16 + 16)
                            sp.dma_start(X[:, w, :], src[b, w * P:(w + 1) * P, :]).then_inc(s_x[w], 16)
                            if layer == DEPTH - 1:
                                sp.dma_start(X1[:, w, :], x1[b, w * P:(w + 1) * P, :]).then_inc(s_x[w], 16)
                        for w in range(NW):
                            sp.wait_ge(xmid, it * NW + w + 1)
                            sp.dma_start(XS[1:P, w, :], X[0:P - 1, w, P:D]).then_inc(s_sh[w], 16)
                            if w + 1 < NW:
                                sp.dma_start(XS[0:1, w + 1, :], X[P - 1:P, w, P:D]).then_inc(s_sh[w + 1], 16)

            def x_landed(eng, layer, b, w):
                if layer == DEPTH - 1:
                    eng.wait_ge(s_x[w], b * 32 + (layer * B * 16 + 32))
                else:
                    eng.wait_ge(s_x[w], b * 16 + (layer * B * 16 + 16))

            @block.tensor
            def _(pe):
                pe.wait_ge(s_cst, 7 * 16)
                pe.wait_ge(s_set, 3)
                for layer in range(DEPTH):
                    pe.wait_ge(s_wt[layer], 5 * 16)
                    with pe.Fori(0, B) as b:
                        it = b + layer * B

                        def a_unit(*key):
                            pe.wait_ge(a_free, it * NA + A[key] + 1)
                            return a_ps[:, A[key] % 2, :]

                        def d_unit(*key):
                            pe.wait_ge(d_free, it * ND + Dn[key] + 1)
                            return d_ps[:, Dn[key] % 2, :]

                        def x_transposed(w):
                            x_landed(pe, layer, b, w)
                            bank = a_unit("xT", w)
                            for c in range(NC):
                                last = nc.tensor.transpose(bank[:, c * P:(c + 1) * P], X[:, w, c * P:(c + 1) * P], Id[:])
                            last.then_inc(a_ready, 1)

                        def project_qkv(w):
                            pe.wait_ge(a_free, it * NA + A["xT", w] + 3)
                            pe.wait_ge(qkv_read_act, it * NW + w + 1)
                            pe.wait_ge(qkv_read_dve, it * NW + w + 1)
                            lhs = [XT[:, 0, 1 + w * P:1 + (w + 1) * P], XT[:, 1, w * P:(w + 1) * P]]
                            for part in range(3):
                                for c in range(NC):
                                    last = nc.tensor.matmul(qkv_ps[:, part, :], lhs[c],
                                                            Wqkv[layer][:, c, part * INNER:(part + 1) * INNER],
                                                            start=(c == 0), stop=(c == NC - 1))
                            last.then_inc(qkv_ready, 1)

                        def qk_transposed(w):
                            pe.wait_ge(qk_rot, it * NW + w + 2)
                            for a, name in enumerate(("qT", "kT")):
                                bank = a_unit(name, w)
                                for hp in range(NHP):
                                    src = QKr[:, w % 2, a, 2 * hp:2 * hp + 2, :].rearrange("p h d -> p (h d)")
                                    last = nc.tensor.transpose(bank[:, hp * P:(hp + 1) * P], src, Id[:])
                                last.then_inc(a_ready, 1)

                        def scores(w, a):
                            banks = [d_unit("sim", w, 2 * a + r) for r in range(2)]
                            if a == 0:
                                pe.wait_ge(a_free, it * NA + A["kT", w] + 3)
                            own = [(i, blk) for i in range(2) for blk in range(2) if w or blk]
                            for i, blk in own:
                                for r in range(2):
                                    half = slice(r * DH, (r + 1) * DH)
                                    mm = nc.tensor.matmul(banks[r][:, (2 * i + blk) * P:(2 * i + blk + 1) * P],
                                                          QT[half, 2 * a + i, :], KT[half, (w - 1 + blk) % 4, 2 * a + i, :],
                                                          start=True, stop=True)
                                    if (i, blk) == own[-1]:
                                        mm.then_inc(d_ready, 1)

                        def project_out(w):
                            pe.wait_ge(o_norm, it * NW + w + 2)
                            bank = a_unit("oT", w)
                            for hp in range(NHP):
                                last = nc.tensor.transpose(bank[:, hp * P:(hp + 1) * P],
                                                           On[:, 2 * hp:2 * hp + 2, :].rearrange("p h d -> p (h d)"), Id[:])
                            last.then_inc(a_ready, 1)
                            bank = d_unit("wo", w)
                            pe.wait_ge(a_free, it * NA + A["oT", w] + 3)
                            for hp in range(NHP):
                                last = nc.tensor.matmul(bank[:, 0:D], OT[:, hp, :], Wo[layer][:, hp, :],
                                                        start=(hp == 0), stop=(hp == NHP - 1))
                            last.then_inc(d_ready, 1)

                        def probs_transposed(w, hp):
                            pe.wait_ge(exp_done, (it * NW + w) * NHP + hp + 1)
                            bank = a_unit("pT", w, hp)
                            for h in range(2):
                                for blk in range(2):
                                    if w == 0 and blk == 0:
                                        continue
                                    i = 2 * h + blk
                                    last = nc.tensor.transpose(bank[:, i * P:(i + 1) * P], SM[:, hp, h, blk, :], Id[:])
                            last.then_inc(a_ready, 1)

                        def attend(w, hp):
                            if hp == 0:
                                pe.wait_ge(o_norm, it * NW + w + 1)
                            pe.wait_ge(a_free, it * NA + A["pT", w, hp] + 3)
                            for h in range(2):
                                head = head_of(hp, h)
                                for blk in range(2):
                                    if w == 0 and blk == 0:
                                        continue
                                    last = nc.tensor.matmul(o_ps[:, head * DH:(head + 1) * DH], PT[:, hp, h, blk, :],
                                                            V[:, (w - 1 + blk) % 4, head * DH:(head + 1) * DH],
                                                            start=(blk == 0 or w == 0), stop=(blk == 1))
                            if hp == NHP - 1:
                                last.then_inc(o_ready, 1)

                        def z_transposed(w):
                            pe.wait_ge(z_done, it * NW + w + 1)
                            bank = a_unit("zT", w)
                            for c in range(NC):
                                last = nc.tensor.transpose(bank[:, c * P:(c + 1) * P], Z[:, w, c * P:(c + 1) * P], Id[:])
                            last.then_inc(a_ready, 1)

                        for w in range(2):
                            x_transposed(w)
                            project_qkv(w)
                        for w in range(NW):
                            qk_transposed(w)
                            scores(w, 0)
                            if w + 2 < NW:
                                x_transposed(w + 2)
                                project_qkv(w + 2)
                            scores(w, 1)
                            if w >= 1:
                                project_out(w - 1)
                            for hp in range(NHP):
                                probs_transposed(w, hp)
                                if hp:
                                    attend(w, hp - 1)
                            attend(w, NHP - 1)
                        for w in range(WPG):
                            z_transposed(w)
                        project_out(NW - 1)
                        for g in range(NG):
                            if g:
                                for w in range(g * WPG, (g + 1) * WPG):
                                    z_transposed(w)
                            pe.wait_ge(a_free, it * NA + A["zT", (g + 1) * WPG - 1] + 3)
                            toks = slice(g * GT, (g + 1) * GT)
                            for m in range(NM):
                                n = rows(m)
                                for ring, name, first, ready in ((a_unit, "gate", HID + m * P, a_ready),
                                                                 (d_unit, "up", m * P, d_ready)):
                                    bank = ring(name, g, m)
                                    for c in range(NC):
                                        last = nc.tensor.matmul(bank[0:n, :], W1[layer][:, c, first:first + n],
                                                                ZT[:, c, toks], start=(c == 0), stop=(c == NC - 1))
                                    last.then_inc(ready, 1)
                            pe.wait_ge(ht_done, it * (NG * NM) + (g + 1) * NM + 2)
                            for w in range(g * WPG, (g + 1) * WPG):
                                bank = d_unit("down", w)
                                t0 = (w % WPG) * P
                                for m in range(NM):
                                    n = rows(m)
                                    last = nc.tensor.matmul(bank[:, 0:D], HT[0:n, m, t0:t0 + P],
                                                            W2[layer][0:n, m, :], start=(m == 0), stop=(m == NM - 1))
                                last.then_inc(d_ready, 1)

            @block.scalar
            def _(act):
                act.sem_inc(a_free, 2)
                act.sem_inc(qkv_read_act, 1)
                for w in range(NW):
                    act.sem_inc(s_st[w], 16)
                act.wait_ge(s_cst, 7 * 16)
                act.wait_ge(s_set, 3)
                for layer in range(DEPTH):
                    with act.Fori(0, B) as b:
                        it = b + layer * B

                        def a_full(*key):
                            act.wait_ge(a_ready, it * NA + A[key] + 1)
                            return a_ps[:, A[key] % 2, :]

                        def evacuate(dst, bank):
                            nc.scalar.activation(dst, bank, ACT.Copy).then_inc(a_free, 1)

                        def x_evacuated(w):
                            bank = a_full("xT", w)
                            evacuate(XT[:, :, 1 + w * P:1 + (w + 1) * P],
                                     bank[:, 0:D].rearrange("p (c t) -> p c t", c=NC))

                        def squares(w):
                            act.wait_ge(qkv_ready, it * NW + w + 1)
                            act.wait_ge(ssum_done, it * NW + w + 1)
                            nc.scalar.activation(Sq[:], qkv_ps[:, 0:2, :].rearrange("p a (h d) -> p (a h) d", d=DH),
                                                 ACT.Square).then_inc(sq_done, 1)
                            nc.scalar.activation(V[:, w % 4, :], qkv_ps[:, 2, :], ACT.Copy).then_inc(qkv_read_act, 1)

                        def exponentials(w, hp):
                            act.wait_ge(nb_done, (it * NW + w) * NHP + hp + 1)
                            for h in range(2):
                                head = head_of(hp, h)
                                s = SM[:, hp, h, :, :] if w else SM[:, hp, h, 1:2, :]
                                last = nc.scalar.activation(s, s, ACT.Exp, bias=Nb[:, 2 * hp + h:2 * hp + h + 1], scale=QK_SCALE,
                                                            accum_out=Rs[:, w % 2, head:head + 1])
                            last.then_inc(exp_done, 1)

                        for w in range(2):
                            x_evacuated(w)
                            squares(w)
                        for w in range(NW):
                            for name, dst in (("qT", QT[:]), ("kT", KT[:, w % 4])):
                                evacuate(dst, a_full(name, w).rearrange("p (a t) -> p a t", a=NHP))
                            if w + 2 < NW:
                                x_evacuated(w + 2)
                            exponentials(w, 0)
                            exponentials(w, 1)
                            if w + 2 < NW:
                                squares(w + 2)
                            exponentials(w, 2)
                            if w >= 1:
                                evacuate(OT[:], a_full("oT", w - 1).rearrange("p (a t) -> p a t", a=NHP))
                            exponentials(w, 3)
                            for hp in range(NHP):
                                bank = a_full("pT", w, hp).rearrange("p (h k t) -> p h k t", h=2, k=2)
                                k = slice(0, 2) if w else slice(1, 2)
                                evacuate(PT[:, hp, :, k, :], bank[:, :, k, :])

                        def z_evacuated(w):
                            bank = a_full("zT", w)
                            for c in range(NC):
                                g0 = 2 * NM
                                last = nc.scalar.activation(ZT[:, c, w * P:(w + 1) * P], bank[:, c * P:(c + 1) * P],
                                                            ACT.Identity, scale=Pv[:, layer, g0 + c:g0 + c + 1],
                                                            bias=Pv[:, layer, g0 + NC + c:g0 + NC + c + 1])
                            last.then_inc(a_free, 1)

                        for w in range(WPG):
                            z_evacuated(w)
                        evacuate(OT[:], a_full("oT", NW - 1).rearrange("p (a t) -> p a t", a=NHP))
                        for g in range(NG):
                            if g:
                                for w in range(g * WPG, (g + 1) * WPG):
                                    z_evacuated(w)
                            for m in range(NM):
                                n = rows(m)
                                i = g * NM + m
                                bank = a_full("gate", g, m)
                                act.wait_ge(ht_done, it * (NG * NM) + i + 1)
                                nc.scalar.activation(G[0:n, i % 2, :], bank[0:n, :], ACT.Gelu,
                                                     bias=Pv[0:n, layer, NM + m:NM + m + 1]).then_inc(a_free, 1)
                        for w in range(NW):
                            act.wait_ge(fin_done, it * NW + w + 1)
                            act.dma_start(stages[layer][1][b, w * P:(w + 1) * P, :], X[:, w, :]).then_inc(s_st[w], 16)
                for w in range(NW):
                    act.wait_ge(s_st[w], (DEPTH * B + 1) * 16)

            @block.gpsimd
            def _(pool):
                nc.gpsimd.memset(Half[:], -0.5).then_inc(s_set, 1)
                nc.gpsimd.memset(XT[:, 1, 0:1], 0.0).then_inc(s_set, 1)
                nc.gpsimd.memset(XS[0:1, 0, :], 0.0).then_inc(s_set, 1)
                pool.sem_inc(qk_rot, 1)
                pool.wait_ge(s_set, 3)
                pool.wait_ge(s_cst, 7 * 16)
                for layer in range(DEPTH):
                    with pool.Fori(0, B) as b:
                        it = b + layer * B

                        def rotate(w):
                            pool.wait_ge(ssum_done, it * NW + w + 2)
                            nc.gpsimd.tensor_tensor(Rn[:], Ssum[:], Half[:], ALU.pow).then_inc(rn_done, 1)
                            pool.wait_ge(rot_terms, it * NW + w + 1)
                            q = QKr[:, w % 2].rearrange("p a h d -> p (a h) d")
                            nc.gpsimd.tensor_tensor(q, q, T2[:].rearrange("p a h d -> p (a h) d"), ALU.add).then_inc(qkr_sum, 1)
                            pool.wait_ge(qkr_sum, it * NW + w + 1)
                            pool.wait_ge(rn_done, it * NW + w + 1)
                            nc.gpsimd.tensor_tensor(q, q, bcast(Rn[:], 1, DH), ALU.mult).then_inc(qk_rot, 1)

                        def rsqrt_var(w):
                            pool.wait_ge(ve_done, it * NW + w + 1)
                            nc.gpsimd.tensor_tensor(Rd[:, w:w + 1], Ve[:, w:w + 1], Half[:, 0:1], ALU.pow).then_inc(rd_done, 1)

                        rotate(0)
                        rotate(1)
                        for w in range(NW):
                            if w >= 2:
                                rsqrt_var(w - 2)
                            if w + 2 < NW:
                                rotate(w + 2)
                        rsqrt_var(NW - 2)
                        rsqrt_var(NW - 1)
                        for w in range(NW):
                            pool.wait_ge(z_done, it * NW + w + 1)
                            pool.wait_ge(s_sh[w], it * (16 if w == 0 else 32) + (16 if w == 0 else 32))
                            if w + 1 < NW:
                                pool.wait_ge(s_sh[w + 1], it * 32 + 32)
                            if layer == DEPTH - 1:
                                x_landed(pool, layer, b, w)
                                nc.gpsimd.tensor_tensor(X[:, w, :], X[:, w, :], X1[:, w, :], ALU.add).then_inc(b2_added, 1)
                                pool.wait_ge(b2_added, b * (2 * NW) + (layer * B * NW + 2 * w + 1))
                                nc.gpsimd.tensor_tensor(X[:, w, :], X[:, w, :], B2[:, layer, :], ALU.add).then_inc(b2_added, 1)
                            else:
                                nc.gpsimd.tensor_tensor(X[:, w, :], X[:, w, :], B2[:, layer, :], ALU.add).then_inc(b2_added, 1)

            @block.vector
            def _(dve):
                dve.sem_inc(d_free, 2)
                dve.sem_inc(qkv_read_dve, 1)
                dve.sem_inc(ssum_done, 1)
                dve.sem_inc(o_norm, 1)
                dve.sem_inc(ht_done, 2)
                dve.wait_ge(s_cst, 7 * 16)
                for layer in range(DEPTH):
                    for swap, (dst, tab) in enumerate(((Cs, TabC), (Ss, TabS))):
                        nc.vector.tensor_tensor(dst[:], tab[:], bcast(Qs[:, layer, swap], 0, NW), ALU.mult).then_inc(tabs_done, 1)
                    dve.wait_ge(tabs_done, 2 * (layer + 1))
                    with dve.Fori(0, B) as b:
                        it = b + layer * B
                        steps = [0]

                        def written(ins):
                            steps[0] += 1
                            ins.then_inc(v_chain, 1)
                            dve.wait_ge(v_chain, it * V_STEPS + steps[0])

                        def d_full(*key):
                            dve.wait_ge(d_ready, it * ND + Dn[key] + 1)
                            return d_ps[:, Dn[key] % 2, :]

                        def rotary_terms(w):
                            dve.wait_ge(qkv_ready, it * NW + w + 1)
                            if w >= 2:
                                dve.wait_ge(a_ready, it * NA + A["kT", w - 2] + 1)
                            dve.wait_ge(qk_rot, it * NW + w + 1)
                            dve.wait_ge(sq_done, it * NW + w + 1)
                            qk = qkv_ps[:, 0:2, :].rearrange("p a (h d) -> p a h d", d=DH)
                            nc.vector.tensor_tensor(QKr[:, w % 2], qk, bcast(Cs[:, w], 1, HEADS), ALU.mult)
                            lo, hi = slice(0, DH // 2), slice(DH // 2, DH)
                            nc.vector.tensor_tensor(T2[:, :, :, lo], qk[:, :, :, hi], bcast(Ss[:, w, :, lo], 1, HEADS), ALU.mult)
                            nc.vector.tensor_tensor(T2[:, :, :, hi], qk[:, :, :, lo], bcast(Ss[:, w, :, hi], 1, HEADS),
                                                    ALU.mult).then_inc(rot_terms, 1)
                            dve.wait_ge(rot_terms, it * NW + w + 1)
                            dve.sem_inc(qkv_read_dve, 1)
                            written(nc.vector.reduce_sum(Ssum[:], Sq[:], AX))
                            nc.vector.tensor_scalar(Ssum[:], Ssum[:], 1e-24, None, ALU.max).then_inc(ssum_done, 1)

                        def mask_and_max(w, hp):
                            bank = d_full("sim", w, hp).rearrange("p (h k t) -> p h k t", h=2, k=2)
                            k = slice(0, 2) if w else slice(1, 2)
                            nk = 2 if w else 1
                            if w:
                                dve.wait_ge(a_ready, it * NA + A["pT", w - 1, hp] + 1)
                            ins = nc.vector.tensor_tensor(SM[:, hp, :, k, :], bank[:, :, k, :], bcast(Mk[:, k, :], 0, 2), ALU.add)
                            ins.then_inc(d_free, 1)
                            dve.wait_ge(d_free, it * ND + Dn["sim", w, hp] + 3)
                            written(nc.vector.reduce_max(Mx[:, 2 * hp:2 * hp + 2], SM[:, hp, :, k, :].rearrange("p h k t -> p h (k t)"), AX))
                            nc.vector.tensor_scalar(Nb[:, 2 * hp:2 * hp + 2], Mx[:, 2 * hp:2 * hp + 2], -QK_SCALE, None,
                                                    ALU.mult).then_inc(nb_done, 1)

                        def normalise(w):
                            dve.wait_ge(exp_done, (it * NW + w + 1) * NHP)
                            written(nc.vector.reciprocal(Ri[:], Rs[:, w % 2, :]))
                            dve.wait_ge(o_ready, it * NW + w + 1)
                            if w:
                                dve.wait_ge(a_ready, it * NA + A["oT", w - 1] + 1)
                            nc.vector.tensor_tensor(On[:], o_ps[:].rearrange("p (h d) -> p h d", d=DH), bcast(Ri[:], 1, DH),
                                                    ALU.mult).then_inc(o_norm, 1)

                        def add_attention(w):
                            bank = d_full("wo", w)
                            nc.vector.tensor_tensor(X[:, w, :], bank[:, 0:D], X[:, w, :], ALU.add).then_inc(d_free, 1)
                            dve.wait_ge(d_free, it * ND + Dn["wo", w] + 3)
                            dve.sem_inc(xmid, 1)

                        def variance(w):
                            n = 16 if w == 0 else 32
                            dve.wait_ge(s_sh[w], it * n + n)
                            nc.vector.bn_stats(Bn[:, 0, :], X[:, w, 0:P])
                            written(nc.vector.bn_stats(Bn[:, 1, :], XS[:, w, :]))
                            dve.sem_inc(bn_seen, 1)
                            written(nc.vector.bn_aggr(Mv[:, w, :], Bn[:].rearrange("p a b -> p (a b)")))
                            nc.vector.tensor_scalar(Ve[:, w:w + 1], Mv[:, w, 1:2], LN_EPS, None, ALU.add).then_inc(ve_done, 1)

                        def layernorm(w):
                            dve.wait_ge(rd_done, it * NW + w + 1)
                            nc.vector.tensor_scalar(Z[:, w, 0:P], X[:, w, 0:P], Mv[:, w, 0:1], Rd[:, w:w + 1], ALU.subtract, ALU.mult)
                            nc.vector.tensor_scalar(Z[:, w, P:D], XS[:, w, :], Mv[:, w, 0:1], Rd[:, w:w + 1],
                                                    ALU.subtract, ALU.mult).then_inc(z_done, 1)

                        rotary_terms(0)
                        rotary_terms(1)
                        for w in range(NW):
                            for hp in range(NHP):
                                mask_and_max(w, hp)
                            if w >= 1:
                                add_attention(w - 1)
                            if w + 2 < NW:
                                rotary_terms(w + 2)
                            if w >= 3:
                                layernorm(w - 3)
                            if w >= 2:
                                variance(w - 2)
                            normalise(w)
                        layernorm(NW - 3)
                        variance(NW - 2)
                        add_attention(NW - 1)
                        layernorm(NW - 2)
                        variance(NW - 1)
                        layernorm(NW - 1)
                        for g in range(NG):
                            for m in range(NM):
                                n = rows(m)
                                i = g * NM + m
                                bank = d_full("up", g, m)
                                dve.wait_ge(a_free, it * NA + A["gate", g, m] + 3)
                                nc.vector.scalar_tensor_tensor(HT[0:n, m, :], bank[0:n, :], Pv[0:n, layer, m:m + 1],
                                                               G[0:n, i % 2, :], ALU.add, ALU.mult).then_inc(ht_done, 1)
                                dve.wait_ge(ht_done, it * (NG * NM) + i + 3)
                                dve.sem_inc(d_free, 1)
                            for w in range(g * WPG, (g + 1) * WPG):
                                bank = d_full("down", w)
                                per = 2 if layer == DEPTH - 1 else 1
                                dve.wait_ge(b2_added, b * (per * NW) + (layer * B * NW + per * (w + 1)))
                                nc.vector.tensor_tensor(X[:, w, :], bank[:, 0:D], X[:, w, :], ALU.add).then_inc(d_free, 1)
                                dve.wait_ge(d_free, it * ND + Dn["down", w] + 3)
                                dve.sem_inc(fin_done, 1)
                        assert steps[0] == V_STEPS, steps[0]


V_STEPS = NW * (1 + NHP + 1 + 2)


def ffn_constants():
    f = np.float32
    half = np.arange(0, DH, 2, dtype=f)
    inv = (f(1.0) / np.power(f(10000.0), half / f(DH))).astype(f)
    t = np.arange(T, dtype=f)
    fr = (t[:, None] * inv[None]).astype(f)
    fr = np.concatenate([fr, fr], -1)
    base = ((half + f(0.4 * DH)) / f(1.4 * DH)).astype(f)
    power = ((t - T // 2) / f(P // 2)).astype(f)
    sc = (base[None].astype(f) ** power[:, None]).astype(f)
    sc = np.concatenate([sc, sc], -1)
    sign = np.where(np.arange(DH) < DH // 2, f(-1), f(1))
    cos, sin = np.cos(fr), np.sin(fr) * sign
    tabc = np.stack([cos * sc, cos / sc], 1).astype(f)
    tabs = np.stack([sin * sc, sin / sc], 1).astype(f)
    i, j = np.arange(P)[:, None], np.arange(P)[None]
    mask = np.stack([np.where(j >= i, 0, MASKED), np.where(j <= i, 0, MASKED)], 1).astype(f)
    return tabc, tabs, np.eye(P, dtype=f), mask


def ffn_arrays(inp):
    f = np.float32
    b1, lg, lb = inp["L0_ffn_b1"], inp["L0_ffn_ln_g"], inp["L0_ffn_ln_b"]
    pv = np.zeros((P, DEPTH, 2 * NM + 2 * NC), f)
    for i in range(DEPTH):
        for m in range(NM):
            pv[:rows(m), i, m] = b1[i, m * P:m * P + rows(m)]
            pv[:rows(m), i, NM + m] = b1[i, HID + m * P:HID + m * P + rows(m)]
        for c in range(NC):
            pv[:, i, 2 * NM + c] = lg[i, c * P:(c + 1) * P]
            pv[:, i, 2 * NM + NC + c] = lb[i, c * P:(c + 1) * P]
    qk = np.stack([inp["L0_ffn_q_scale"], inp["L0_ffn_k_scale"]], 1)
    swapped = np.concatenate([qk[..., DH // 2:], qk[..., :DH // 2]], -1)
    qs = np.broadcast_to(np.stack([qk, swapped], 1)[None], (P, DEPTH, 2, 2, DH))
    b2 = np.broadcast_to(inp["L0_ffn_b2"][None], (P, DEPTH, D))
    tabc, tabs, ident, mask = ffn_constants()
    return {"wqkv": inp["L0_ffn_wqkv"], "wo": inp["L0_ffn_wo"], "w1": inp["L0_ffn_w1"], "w2": inp["L0_ffn_w2"],
            "pvec": pv, "qs2": qs, "b2": b2, "tabc": tabc, "tabs": tabs, "ident": ident, "maskd": mask}



BF16 = mybir.dt.bfloat16
DT_, K = 256, 4
H, BITS, BUCKETS, ASSOC = 2, 9, 128, 2
KD = 32
CONV_K = 4
UP = 4 * D
NU = UP // P
ZR, ZW, ZQ, ZK = 0, H * BITS, 2 * H * BITS, 2 * H * BITS + KD
ZG = ZK + 2 * KD
NZ = ZG + 3
RMS_EPS = 1e-6
SCALE = float(np.float32(1.0 / np.sqrt(KD)))
PAD = CONV_K - 1
ZW3 = 3


def bcast1(ap, n):
    return ap.to_broadcast([P, n])


def z_windows(i):
    return range(i * ZW3, min((i + 1) * ZW3, NW))


NZU = -(-NW // ZW3)


def attn_units():
    order = [("A", "xnT", w) for w in range(NW)]
    order += [("A", "gate", c, g) for g in range(NG) for c in range(NC)]
    order += [("A", "z", i) for i in range(NZU)]
    for w in range(NW):
        order.append(("A", "rows", w))
    order += [("A", "keep", g) for g in range(NG)]
    for h in range(H):
        order += [("D", "slot_row", h, g) for g in range(NG)] + [("D", "slot_col", h)]
    order += [("A", "long", w) for w in range(NW)]
    order += [("A", "rvT", g) for g in range(NG)]
    order += [("D", "mem", w) for w in range(NW)]
    order += [("A", "ynT", w) for w in range(NW)]
    for g in range(NG):
        order += [("A", "up", g, m) for m in range(NU)]
        order += [("D", "down", w) for w in range(g * WPG, (g + 1) * WPG)]
    index = {"A": {}, "D": {}}
    for ring, *key in order:
        index[ring][tuple(key)] = len(index[ring])
    return index["A"], index["D"]


AV_STEPS = 1 + 1 + (CONV_K - 1) * NC + 2 + 2 * H + 2 * H + 3 * H * NW + 8 + 3 * NW
AP_STEPS = 5


def build_attn(nc, x, x1, x2, gate_wt, conv_w, cols, wcat, state_in, state_out_t, mem_out_t, up_wt, down_wt, rowsv, ident):
    A, Dn = attn_units()
    NA, ND = len(A), len(Dn)
    PRE = 2 * K
    with ExitStack() as ctx:
        def sb(name, shape, dt=F32):
            return ctx.enter_context(nc.sbuf_tensor(name, shape, dt))

        def psum(name, shape):
            return ctx.enter_context(nc.psum_tensor(name, shape, F32))

        def sem(name):
            return ctx.enter_context(nc.semaphore("m_" + name))

        GateT = sb("GateT", [P, NC, D])
        ConvW = sb("ConvW", [P, NC, CONV_K])
        Cols = sb("Cols", [P, NC + NU])
        Wcat = sb("Wcat", [P, NC, NZ])
        Comb = sb("Comb", [P, K, NC, D])
        MemO = sb("MemO", [KD, D])
        UpT = sb("UpT", [P, NC, UP])
        DownT = sb("DownT", [P, NU, D])
        Rv = sb("Rv", [P, 2 * H * BITS + K + 3 + D + 1])
        Pow = Rv[:, 0:2 * H * BITS]
        r0 = 2 * H * BITS
        DecL, GateB, DownB, Iota = Rv[:, r0:r0 + K], Rv[:, r0 + K:r0 + K + 3], Rv[:, r0 + K + 3:r0 + K + 3 + D], Rv[:, r0 + K + 3 + D:r0 + K + 4 + D]
        Id = sb("Id_", [P, P])
        Ones = sb("Ones", [P, P])
        OnesB = sb("OnesB", [P, P], BF16)
        Half = sb("Half_", [P, NW])
        Dec = sb("Dec", [P, K])
        Eps = sb("Eps", [P, 2, NW])

        X = sb("X_", [P, NW, D])
        XA = sb("XA", [P, NW, D])
        XN = sb("XN", [P, NW, D])
        XNT = sb("XNT", [P, NC, PAD + T])
        Bn = sb("Bn_", [P, NW, 6])
        Mv = sb("Mv_", [P, NW, 2])
        Rd = sb("Rd_", [P, NW])
        Rr = sb("Rr", [P, NW])
        HC = sb("HC", [P, NC, T])
        SG = sb("SG", [P, NG * NC, GT])
        UT = sb("UT", [P, NC, T])
        Z = sb("Z_", [P, NW, NZ])
        Bits = sb("Bits", [P, NW, 2 * H * BITS])
        Idx = sb("Idx", [P, NW, 2 * H])
        Gt = sb("Gt", [P, 3, NW])
        Keep = sb("Keep", [P, NW])
        DG = sb("DG", [P, 2 * H, P])
        DO = sb("DO", [P, 2, P])
        Row = sb("Row", [P, 2 * H, T])
        KeepRow = sb("KeepRow", [P, T])
        OW = sb("OW", [P, T])
        Par = sb("Par", [P, T])
        OWP = sb("OWP", [P, H, T], BF16)
        SlotC = sb("SlotC", [P, H, 2, NW])
        CellC = sb("CellC", [P, H, NW])
        KVM = sb("KVM", [P, H, NW, ASSOC, 2 * KD])
        A0 = OW
        D1 = sb("D1", [P, T])
        S = sb("S", [P, 1 + T])
        W = sb("W", [P, 2, T])
        RD = sb("RD", [P, NW, H * ASSOC, 2 * KD])
        Sc = sb("Sc", [P, NW, H * ASSOC])
        Sm = sb("Sm", [P, NW])
        At = sb("At", [P, NW, H * ASSOC])
        Rdv = sb("Rdv", [P, NW, KD])
        RVT = sb("RVT", [KD, T])
        SS = sb("SS", [P, K, NC, T])
        flat = SS[:].rearrange("p k c t -> p (k c t)")
        StIn = flat[:, 0:2 * K * D].rearrange("p (a n) -> p a n", n=D)
        StOut = flat[:, 2 * K * D:4 * K * D].rearrange("p (a n) -> p a n", n=D)
        PR = HC[:].rearrange("p c t -> p (c t)")[:, 0:NW * H * ASSOC * KD].rearrange("p (w a d) -> p w a d", w=NW, d=KD)
        Hm = Row[:].rearrange("p a t -> p (a t)").rearrange("p (m t) -> p m t", t=GT)

        a_ps = psum("a_ps_", [P, 2, 512])
        d_ps = psum("d_ps_", [P, 2, 512])
        rd_ps = psum("rd_ps", [P, H, NW, P])

        s_c = sem("const"); s_w0 = sem("state_maps"); s_set = sem("set")
        s_x = [sem(f"x{w}") for w in range(NW)]
        a_ready, a_free, d_ready, d_free = sem("a_ready"), sem("a_free"), sem("d_ready"), sem("d_free")
        dec_done = sem("dec_done"); mv_done = sem("mv_done"); rr_done = sem("rr_done")
        xn_done = sem("xn_done"); conv_done = sem("conv_done"); silu_done = sem("silu_done"); sg_done = sem("sg_done")
        ut_done = sem("ut_done"); z_copied = sem("z_copied"); idx_done = sem("idx_done"); gt_done = sem("gt_done")
        keep_done = sem("keep_done"); dg_done = sem("dg_done"); do_done = sem("do_done")
        ss_done = sem("ss_done"); owp_done = sem("owp_done"); slotc_done = sem("slotc_done"); kvm_done = sem("kvm_done")
        w_done = sem("w_done"); w_used = sem("w_used"); rd_ready = sem("rd_ready"); rd_copied = sem("rd_copied")
        sc_done = sem("sc_done"); ex_done = sem("ex_done"); rdv_done = sem("rdv_done")
        long_done = sem("long_done"); yl_added = sem("yl_added"); y_done = sem("y_done"); ysq_done = sem("ysq_done")
        yv_done = sem("yv_done"); yr_done = sem("yr_done"); yn_done = sem("yn_done"); res_done = sem("res_done")
        x1_done = sem("x1_done"); mv1_done = sem("mv1_done"); rd1_done = sem("rd1_done"); x2_done = sem("x2_done")
        x1_st, x2_st = [sem(f"x1st{w}") for w in range(NW)], [sem(f"x2st{w}") for w in range(NW)]
        v_chain, p_chain, seen = sem("v_chain"), sem("p_chain"), sem("seen")
        seen_bn = sem("seen_bn")
        NCONST = 10

        with nc.Block() as block:

            @block.sync
            def _(sp):
                sp.dma_start(StIn, state_in.rearrange("(a p) n -> p a n", p=P)).then_inc(s_w0, 16)
                sp.dma_start(StOut, state_out_t.rearrange("(a p) n -> p a n", p=P)).then_inc(s_w0, 16)
                for dst, src in ((Rv[:], rowsv), (Id[:], ident), (ConvW[:], conv_w), (Cols[:], cols),
                                 (GateT[:], gate_wt.rearrange("(c p) n -> p c n", p=P)),
                                 (Wcat[:], wcat.rearrange("(c p) n -> p c n", p=P)), (MemO[:], mem_out_t),
                                 (UpT[:], up_wt.rearrange("(c p) n -> p c n", p=P)),
                                 (DownT[:], down_wt.rearrange("(c p) n -> p c n", p=P))):
                    sp.dma_start(dst, src).then_inc(s_c, 16)
                for w in range(NW):
                    sp.sem_inc(x1_st[w], 16)
                    sp.sem_inc(x2_st[w], 16)
                with sp.Fori(0, B) as b:
                    for w in range(NW):
                        sp.wait_ge(res_done, b * NW + w + 1)
                        sp.dma_start(X[:, w, :], x[b, w * P:(w + 1) * P, :]).then_inc(s_x[w], 16)
                    for w in range(NW):
                        sp.wait_ge(x1_done, b * NW + w + 1)
                        sp.dma_start(x1[b, w * P:(w + 1) * P, :], XA[:, w, :]).then_inc(x1_st[w], 16)
                        sp.wait_ge(x2_done, b * NW + w + 1)
                        sp.dma_start(x2[b, w * P:(w + 1) * P, :], XN[:, w, :]).then_inc(x2_st[w], 16)
                for w in range(NW):
                    sp.wait_ge(x1_st[w], (B + 1) * 16)
                    sp.wait_ge(x2_st[w], (B + 1) * 16)

            @block.tensor
            def _(pe):
                pe.wait_ge(s_w0, 32)
                for i in range(PRE):
                    k, c = divmod(i, NC)
                    pe.wait_ge(a_free, i + 1)
                    for dt in range(NC):
                        last = nc.tensor.matmul(a_ps[:, i % 2, 0:D], StIn[:, k * NC + dt, c * P:(c + 1) * P],
                                                StOut[:, k * NC + dt, :], start=(dt == 0), stop=(dt == NC - 1))
                    last.then_inc(a_ready, 1)
                pe.wait_ge(s_c, 9 * 16)
                pe.wait_ge(s_set, 8)
                with pe.Fori(0, B) as b:
                    def a_unit(*key):
                        pe.wait_ge(a_free, b * NA + (PRE + A[key] + 1))
                        return a_ps[:, A[key] % 2, :]

                    def a_emptied(*key):
                        pe.wait_ge(a_free, b * NA + (PRE + A[key] + 3))

                    def d_unit(*key):
                        pe.wait_ge(d_free, b * ND + (Dn[key] + 1))
                        return d_ps[:, Dn[key] % 2, :]

                    def transposed(name, w, src, done, n):
                        pe.wait_ge(done, n)
                        bank = a_unit(name, w)
                        for c in range(NC):
                            last = nc.tensor.transpose(bank[:, c * P:(c + 1) * P], src[:, w, c * P:(c + 1) * P], Id[:])
                        last.then_inc(a_ready, 1)

                    for w in range(NW):
                        transposed("xnT", w, XN, xn_done, b * NW + w + 1)
                    for g in range(NG):
                        a_emptied("xnT", (g + 1) * WPG - 1)
                        for c in range(NC):
                            bank = a_unit("gate", c, g)
                            for ci in range(NC):
                                last = nc.tensor.matmul(bank, GateT[:, ci, c * P:(c + 1) * P],
                                                        XNT[:, ci, PAD + g * GT:PAD + (g + 1) * GT],
                                                        start=(ci == 0), stop=(ci == NC - 1))
                            last.then_inc(a_ready, 1)
                    pe.wait_ge(ut_done, (b + 1) * (NG * NC) + 1)
                    for i in range(NZU):
                        bank = a_unit("z", i)
                        for j, w in enumerate(z_windows(i)):
                            for c in range(NC):
                                last = nc.tensor.matmul(bank[:, j * NZ:(j + 1) * NZ], UT[:, c, w * P:(w + 1) * P],
                                                        Wcat[:, c, :], start=(c == 0), stop=(c == NC - 1))
                        last.then_inc(a_ready, 1)
                    for w in range(NW):
                        pe.wait_ge(dg_done, b * NW + w + 1)
                        bank = a_unit("rows", w)
                        nc.tensor.matmul(bank, Ones[:], DG[:].rearrange("p a t -> p (a t)"),
                                         start=True, stop=True).then_inc(a_ready, 1)
                    for g in range(NG):
                        bank = a_unit("keep", g)
                        for i in range(WPG):
                            w = g * WPG + i
                            pe.wait_ge(do_done, b * NW + w + 1)
                            nc.tensor.matmul(bank[:, i * P:(i + 1) * P], Ones[:], DO[:, w % 2, :],
                                             start=True, stop=True).then_inc(a_ready if i == WPG - 1 else seen, 1)
                    for h in range(H):
                        pe.wait_ge(owp_done, b * H + h + 1)
                        for g in range(NG):
                            bank = d_unit("slot_row", h, g)
                            nc.tensor.matmul(bank, OnesB[:], OWP[:, h, g * GT:(g + 1) * GT],
                                             start=True, stop=True).then_inc(d_ready, 1)
                        bank = d_unit("slot_col", h)
                        for w in range(NW):
                            last = nc.tensor.matmul(bank[:, w:w + 1], OWP[:, h, w * P:(w + 1) * P], OnesB[:, 0:1],
                                                    start=True, stop=True)
                        last.then_inc(d_ready, 1)
                    pe.wait_ge(ss_done, (b + 1) * (K * NC))
                    for w in range(NW):
                        bank = a_unit("long", w)
                        for i in range(K * NC):
                            k, c = divmod(i, NC)
                            last = nc.tensor.matmul(bank[:, 0:D], SS[:, k, c, w * P:(w + 1) * P], Comb[:, k, c, :],
                                                    start=(i == 0), stop=(i == K * NC - 1))
                        last.then_inc(a_ready, 1)
                    for h in range(H):
                        pe.wait_ge(kvm_done, b * (H * ASSOC) + (h + 1) * ASSOC)
                        pe.wait_ge(rd_copied, b * H + h + 1)
                        for i in range(NW):
                            pe.wait_ge(w_done, b * (H * NW) + (h * NW + i + 1))
                            for w in range(i, NW):
                                last = nc.tensor.matmul(rd_ps[:, h, w, :], W[:, i % 2, (w - i) * P:(w - i + 1) * P],
                                                        KVM[:, h, i].rearrange("p a d -> p (a d)"),
                                                        start=(i == 0 and w % 4 == 0), stop=(i == w), skip_group_check=True)
                            last.then_inc(w_used, 1)
                        pe.wait_ge(w_used, b * (H * NW) + (h + 1) * NW)
                        pe.sem_inc(rd_ready, 1)
                    pe.wait_ge(rdv_done, b + 1)
                    for g in range(NG):
                        bank = a_unit("rvT", g)
                        for i in range(WPG):
                            last = nc.tensor.transpose(bank[0:KD, i * P:(i + 1) * P], Rdv[:, g * WPG + i, :], Id[:])
                        last.then_inc(a_ready, 1)
                    a_emptied("rvT", NG - 1)
                    for w in range(NW):
                        bank = d_unit("mem", w)
                        nc.tensor.matmul(bank[:, 0:D], RVT[:, w * P:(w + 1) * P], MemO[:], start=True, stop=True).then_inc(d_ready, 1)
                    for w in range(NW):
                        transposed("ynT", w, XN, yn_done, b * NW + w + 1)
                    for g in range(NG):
                        a_emptied("ynT", (g + 1) * WPG - 1)
                        for m in range(NU):
                            bank = a_unit("up", g, m)
                            for c in range(NC):
                                last = nc.tensor.matmul(bank, UpT[:, c, m * P:(m + 1) * P],
                                                        XNT[:, c, PAD + g * GT:PAD + (g + 1) * GT],
                                                        start=(c == 0), stop=(c == NC - 1))
                            last.then_inc(a_ready, 1)
                        a_emptied("up", g, NU - 1)
                        for w in range(g * WPG, (g + 1) * WPG):
                            bank = d_unit("down", w)
                            t0 = (w % WPG) * P
                            for m in range(NU):
                                last = nc.tensor.matmul(bank[:, 0:D], Hm[:, m, t0:t0 + P], DownT[:, m, :],
                                                        start=(m == 0), stop=(m == NU - 1))
                            last.then_inc(d_ready, 1)

            @block.scalar
            def _(act):
                act.sem_inc(a_free, 2)
                act.sem_inc(rd_copied, 1)
                for i in range(PRE):
                    k, c = divmod(i, NC)
                    act.wait_ge(a_ready, i + 1)
                    nc.scalar.activation(Comb[:, k, c, :], a_ps[:, i % 2, 0:D], ACT.Copy).then_inc(a_free, 1)
                act.wait_ge(s_c, 9 * 16)
                act.wait_ge(s_set, 8)
                nc.scalar.activation(Dec[:], DecL, ACT.Sigmoid).then_inc(dec_done, 1)
                with act.Fori(0, B) as b:
                    def a_full(*key):
                        act.wait_ge(a_ready, b * NA + (PRE + A[key] + 1))
                        return a_ps[:, A[key] % 2, :]

                    def evacuate(dst, bank, func=ACT.Copy, **kw):
                        return nc.scalar.activation(dst, bank, func, **kw).then_inc(a_free, 1)

                    for w in range(NW):
                        evacuate(XNT[:, :, PAD + w * P:PAD + (w + 1) * P],
                                 a_full("xnT", w)[:, 0:D].rearrange("p (c t) -> p c t", c=NC))
                    for g in range(NG):
                        for c in range(NC):
                            i = g * NC + c
                            toks = slice(g * GT, (g + 1) * GT)
                            bank = a_full("gate", c, g)
                            act.wait_ge(ut_done, b * (NG * NC) + 1)
                            evacuate(SG[:, i, :], bank, ACT.Sigmoid, bias=Cols[:, c:c + 1])
                            act.wait_ge(a_free, b * NA + (PRE + A["gate", c, g] + 3))
                            act.sem_inc(sg_done, 1)
                    for g in range(NG):
                        for c in range(NC):
                            toks = slice(g * GT, (g + 1) * GT)
                            act.wait_ge(conv_done, (b + 1) * NC)
                            nc.scalar.activation(UT[:, c, toks], HC[:, c, toks], ACT.Silu).then_inc(silu_done, 1)
                    for i in range(NZU):
                        ws = z_windows(i)
                        evacuate(Z[:, ws[0]:ws[-1] + 1, :],
                                 a_full("z", i)[:, 0:len(ws) * NZ].rearrange("p (w n) -> p w n", n=NZ))
                    act.wait_ge(a_free, b * NA + (PRE + A["z", NZU - 1] + 3))
                    act.sem_inc(z_copied, 1)
                    for j in range(3):
                        nc.scalar.activation(Gt[:, j, :], Z[:, :, ZG + j], ACT.Sigmoid, bias=GateB[:, j:j + 1]).then_inc(gt_done, 1)
                    for w in range(NW):
                        evacuate(Row[:, :, w * P:(w + 1) * P], a_full("rows", w).rearrange("p (a t) -> p a t", t=P))
                    for g in range(NG):
                        evacuate(KeepRow[:, g * GT:(g + 1) * GT], a_full("keep", g))
                    act.wait_ge(gt_done, b * 3 + 3)
                    for w in range(NW):
                        evacuate(XN[:, w, :], a_full("long", w)[:, 0:D], ACT.Copy, scale=Gt[:, 1, w:w + 1])
                    for h in range(H):
                        act.wait_ge(rd_ready, b * H + h + 1)
                        nc.scalar.activation(RD[:, :, h * ASSOC:(h + 1) * ASSOC, :],
                                             rd_ps[:, h].rearrange("p w (a d) -> p w a d", a=ASSOC), ACT.Copy).then_inc(rd_copied, 1)
                    act.wait_ge(sc_done, b + 1)
                    nc.scalar.activation(At[:], Sc[:], ACT.Exp, scale=SCALE).then_inc(ex_done, 1)
                    for g in range(NG):
                        evacuate(RVT[:, g * GT:(g + 1) * GT], a_full("rvT", g)[0:KD, :])
                    for w in range(NW):
                        act.wait_ge(y_done, b * NW + w + 1)
                        nc.scalar.activation(SG[:, 0, 0:D], XA[:, w, :], ACT.Square, accum_out=Rr[:, w:w + 1]).then_inc(ysq_done, 1)
                        act.wait_ge(ysq_done, b * NW + w + 1)
                    for w in range(NW):
                        evacuate(XNT[:, :, PAD + w * P:PAD + (w + 1) * P],
                                 a_full("ynT", w)[:, 0:D].rearrange("p (c t) -> p c t", c=NC))
                    for g in range(NG):
                        if g:
                            act.wait_ge(d_ready, b * ND + (Dn["down", g * WPG - 1] + 1))
                        for m in range(NU):
                            evacuate(Hm[:, m, :], a_full("up", g, m), ACT.Silu, bias=Cols[:, NC + m:NC + m + 1])

            @block.gpsimd
            def _(pool):
                nc.gpsimd.memset(Half[:], -0.5).then_inc(s_set, 1)
                nc.gpsimd.memset(XNT[:, :, 0:PAD], 0.0).then_inc(s_set, 1)
                nc.gpsimd.memset(D1[:], 0.0).then_inc(s_set, 1)
                nc.gpsimd.memset(S[:, 0:1], 0.0).then_inc(s_set, 1)
                nc.gpsimd.memset(Ones[:], 1.0).then_inc(s_set, 1)
                nc.gpsimd.memset(OnesB[:], 1.0).then_inc(s_set, 1)
                nc.gpsimd.memset(Eps[:, 0, :], LN_EPS).then_inc(s_set, 1)
                nc.gpsimd.memset(Eps[:, 1, :], RMS_EPS).then_inc(s_set, 1)
                pool.sem_inc(res_done, NW)
                pool.wait_ge(s_set, 8)
                pool.wait_ge(s_c, 9 * 16)
                with pool.Fori(0, B) as b:
                    steps = [0]

                    def written(ins):
                        steps[0] += 1
                        ins.then_inc(p_chain, 1)
                        pool.wait_ge(p_chain, b * AP_STEPS + steps[0])

                    pool.wait_ge(mv_done, b + 1)
                    var = Mv[:, :, 1]
                    written(nc.gpsimd.tensor_tensor(Rr[:], var, Eps[:, 0, :], ALU.add))
                    written(nc.gpsimd.tensor_tensor(Rd[:], Rr[:], Half[:], ALU.pow))
                    written(nc.gpsimd.tensor_tensor(Rr[:], Rd[:], Rd[:], ALU.mult))
                    written(nc.gpsimd.tensor_tensor(Rr[:], Rr[:], var, ALU.mult))
                    written(nc.gpsimd.tensor_tensor(Rr[:], Rr[:], Eps[:, 1, :], ALU.add))
                    nc.gpsimd.tensor_tensor(Rr[:], Rr[:], Half[:], ALU.pow).then_inc(rr_done, 1)
                    pool.wait_ge(idx_done, b + 1)
                    for w in range(NW):
                        pool.wait_ge(a_ready, b * NA + (PRE + A["rows", w]))
                        nc.gpsimd.tensor_tensor(DG[:], bcast(Id[:], 0, 2 * H), bcast(Idx[:, w, :], 1, P), ALU.mult).then_inc(dg_done, 1)
                    pool.wait_ge(keep_done, b + 1)
                    for w in range(NW):
                        if w >= 2:
                            g, i = divmod(w - 2, WPG)
                            n = (g * (WPG - 1) + i + 1) if i < WPG - 1 else None
                            if n is None:
                                pool.wait_ge(a_ready, b * NA + (PRE + A["keep", g] + 1))
                            else:
                                pool.wait_ge(seen, b * (NG * (WPG - 1)) + n)
                        nc.gpsimd.tensor_tensor(DO[:, w % 2, :], Id[:], bcast1(Keep[:, w:w + 1], P), ALU.mult).then_inc(do_done, 1)
                    for h in range(H):
                        pool.wait_ge(slotc_done, b * H + h + 1)
                        for a in range(ASSOC):
                            nc.gpsimd.tensor_tensor(KVM[:, h, :, a, :], Z[:, :, ZK:ZK + 2 * KD], bcast(SlotC[:, h, a, :], 1, 2 * KD),
                                                    ALU.mult).then_inc(kvm_done, 1)
                    for w in range(NW):
                        pool.wait_ge(a_free, b * NA + (PRE + A["long", w] + 3))
                        nc.gpsimd.tensor_tensor(XA[:, w, :], XA[:, w, :], XN[:, w, :], ALU.add).then_inc(yl_added, 1)
                    pool.wait_ge(yv_done, b + 1)
                    nc.gpsimd.tensor_tensor(Rd[:], Rd[:], Half[:], ALU.pow).then_inc(yr_done, 1)
                    for w in range(NW):
                        pool.wait_ge(yn_done, b * NW + w + 1)
                        pool.wait_ge(ysq_done, b * NW + w + 1)
                        nc.gpsimd.tensor_tensor(XA[:, w, :], XA[:, w, :], X[:, w, :], ALU.add).then_inc(res_done, 1)
                    for w in range(NW):
                        pool.wait_ge(mv1_done, b * NW + w + 1)
                        nc.gpsimd.tensor_tensor(Rd[:, w:w + 1], Rd[:, w:w + 1], Half[:, 0:1], ALU.pow).then_inc(rd1_done, 1)
                    assert steps[0] == AP_STEPS, steps[0]

            @block.vector
            def _(dve):
                dve.sem_inc(d_free, 2)
                dve.sem_inc(ut_done, 1)
                dve.wait_ge(s_c, 9 * 16)
                dve.wait_ge(s_set, 8)
                dve.wait_ge(dec_done, 1)
                dve.wait_ge(a_free, PRE + 2)
                with dve.Fori(0, B) as b:
                    steps = [0]

                    def written(ins):
                        steps[0] += 1
                        ins.then_inc(v_chain, 1)
                        dve.wait_ge(v_chain, b * AV_STEPS + steps[0])

                    def d_full(*key):
                        dve.wait_ge(d_ready, b * ND + (Dn[key] + 1))
                        return d_ps[:, Dn[key] % 2, :]

                    def a_emptied(*key):
                        dve.wait_ge(a_free, b * NA + (PRE + A[key] + 3))

                    for w in range(NW):
                        dve.wait_ge(s_x[w], b * 16 + 16)
                        last = nc.vector.bn_stats(Bn[:, w, :], X[:, w, :])
                    written(last)
                    dve.sem_inc(seen_bn, 1)
                    for w in range(NW):
                        last = nc.vector.bn_aggr(Mv[:, w, :], Bn[:, w, :])
                    last.then_inc(mv_done, 1)
                    dve.wait_ge(rr_done, b + 1)
                    for w in range(NW):
                        dve.wait_ge(x1_st[w], b * 16 + 16)
                        dve.wait_ge(x2_st[w], b * 16 + 16)
                        last = nc.vector.tensor_scalar(XA[:, w, :], X[:, w, :], Mv[:, w, 0:1], Rd[:, w:w + 1], ALU.subtract, ALU.mult)
                        if w == NW - 1:
                            written(last)
                    for w in range(NW):
                        nc.vector.tensor_scalar(XN[:, w, :], XA[:, w, :], Rr[:, w:w + 1], None, ALU.mult).then_inc(xn_done, 1)
                    a_emptied("xnT", NW - 1)
                    for j in range(CONV_K):
                        for c in range(NC):
                            src = XNT[:, c, j:j + T]
                            if j == 0:
                                last = nc.vector.tensor_scalar(HC[:, c, :], src, ConvW[:, c, 0:1], None, ALU.mult)
                            else:
                                last = nc.vector.scalar_tensor_tensor(HC[:, c, :], src, ConvW[:, c, j:j + 1], HC[:, c, :], ALU.mult, ALU.add)
                            if j == CONV_K - 1:
                                last.then_inc(conv_done, 1)
                            else:
                                written(last)
                    for g in range(NG):
                        for c in range(NC):
                            i = g * NC + c
                            toks = slice(g * GT, (g + 1) * GT)
                            dve.wait_ge(silu_done, b * (NG * NC) + i + 1)
                            dve.wait_ge(sg_done, b * (NG * NC) + i + 1)
                            nc.vector.tensor_tensor(UT[:, c, toks], UT[:, c, toks], SG[:, i, :], ALU.mult).then_inc(ut_done, 1)
                    dve.wait_ge(z_copied, b + 1)
                    written(nc.vector.scalar_tensor_tensor(Bits[:], Z[:, :, 0:2 * H * BITS], 0.0, bcast(Pow, 0, NW), ALU.is_gt, ALU.mult))
                    written(nc.vector.reduce_sum(Idx[:].rearrange("p w a -> p (w a)"), Bits[:].rearrange("p w (a n) -> p (w a) n", n=BITS), AX))
                    nc.vector.tensor_scalar(Idx[:, :, 0:H], Idx[:, :, 0:H], float(BUCKETS - 1), None, ALU.min).then_inc(idx_done, 1)
                    dve.wait_ge(gt_done, b * 3 + 3)
                    nc.vector.tensor_scalar(Keep[:], Gt[:, 0, :], -1.0, 1.0, ALU.mult, ALU.add).then_inc(keep_done, 1)
                    dve.wait_ge(ut_done, (b + 1) * (NG * NC) + 1)
                    for k in range(K):
                        for c in range(NC):
                            nc.vector.tensor_tensor_scan(SS[:, k, c, :], bcast1(Dec[:, k:k + 1], T), UT[:, c, :], 0.0,
                                                         ALU.mult, ALU.add).then_inc(ss_done, 1)
                    dve.wait_ge(idx_done, b + 1)
                    a_emptied("keep", NG - 1)
                    for h in range(H):
                        if h:
                            dve.wait_ge(owp_done, b * H + h)
                        written(nc.vector.tensor_scalar(OW[:], Row[:, H + h, :], Iota, None, ALU.is_equal))
                        written(nc.vector.tensor_tensor_scan(Par[:], OW[:], bcast1(S[:, 0:1], T), 0.0, ALU.not_equal, ALU.add))
                        nc.vector.tensor_tensor(OWP[:, h, :], OW[:], Par[:], ALU.mult).then_inc(owp_done, 1)
                    for h in range(H):
                        for g in range(NG):
                            row = Row[:, H + h, g * GT:(g + 1) * GT]
                            nc.vector.scalar_tensor_tensor(row, row, 2.0, d_full("slot_row", h, g), ALU.mult, ALU.add).then_inc(d_free, 1)
                        written(nc.vector.tensor_copy(SlotC[:, h, 0, :], d_full("slot_col", h)[:, 0:NW]))
                        dve.sem_inc(d_free, 1)
                        nc.vector.tensor_scalar(SlotC[:, h, 1, :], SlotC[:, h, 0, :], -1.0, 1.0, ALU.mult, ALU.add).then_inc(slotc_done, 1)
                        written(nc.vector.scalar_tensor_tensor(CellC[:, h, :], Idx[:, :, H + h], 2.0, SlotC[:, h, 0, :], ALU.mult, ALU.add))
                    dve.wait_ge(d_free, b * ND + (Dn["slot_col", H - 1] + 3))
                    for h in range(H):
                        for i in range(NW):
                            n = T - i * P
                            t0 = i * P
                            nc.vector.tensor_scalar(D1[:, 0:P], Id[:], Gt[:, 0, i:i + 1], None, ALU.mult)
                            written(nc.vector.scalar_tensor_tensor(A0[:, 0:n], Row[:, H + h, t0:T], CellC[:, h, i:i + 1], KeepRow[:, t0:T],
                                                                   ALU.not_equal, ALU.max))
                            written(nc.vector.tensor_tensor_scan(S[:, 1:1 + n], A0[:, 0:n], D1[:, 0:n], 0.0, ALU.mult, ALU.add))
                            j = h * NW + i
                            if j >= 2:
                                dve.wait_ge(w_used, b * (H * NW) + (j - 1))
                            written(nc.vector.scalar_tensor_tensor(W[:, i % 2, 0:n], Row[:, h, t0:T], Idx[:, i, H + h:H + h + 1], S[:, 0:n],
                                                                   ALU.is_equal, ALU.mult))
                            dve.sem_inc(w_done, 1)
                    dve.wait_ge(rd_copied, b * H + (H + 1))
                    written(nc.vector.tensor_tensor(PR, RD[:, :, :, 0:KD], bcast(Z[:, :, ZQ:ZQ + KD], 1, H * ASSOC), ALU.mult))
                    written(nc.vector.reduce_sum(Sc[:], PR, AX))
                    written(nc.vector.reduce_max(Sm[:], Sc[:], AX))
                    nc.vector.tensor_tensor(Sc[:], Sc[:], bcast(Sm[:], 1, H * ASSOC), ALU.subtract).then_inc(sc_done, 1)
                    dve.wait_ge(ex_done, b + 1)
                    written(nc.vector.reduce_sum(Sm[:], At[:], AX))
                    written(nc.vector.reciprocal(Sm[:], Sm[:]))
                    written(nc.vector.tensor_tensor(Sm[:], Sm[:], Gt[:, 2, :], ALU.mult))
                    written(nc.vector.tensor_tensor(At[:], At[:], bcast(Sm[:], 1, H * ASSOC), ALU.mult))
                    written(nc.vector.tensor_tensor(PR, RD[:, :, :, KD:2 * KD], bcast(At[:], 2, KD), ALU.mult))
                    nc.vector.reduce_sum(Rdv[:], PR.rearrange("p w a d -> p w d a"), AX).then_inc(rdv_done, 1)
                    for w in range(NW):
                        dve.wait_ge(yl_added, b * NW + w + 1)
                        nc.vector.tensor_tensor(XA[:, w, :], d_full("mem", w)[:, 0:D], XA[:, w, :], ALU.add).then_inc(d_free, 1)
                        dve.wait_ge(d_free, b * ND + (Dn["mem", w] + 3))
                        dve.sem_inc(y_done, 1)
                    dve.wait_ge(ysq_done, (b + 1) * NW)
                    nc.vector.tensor_scalar(Rd[:], Rr[:], 1.0 / D, RMS_EPS, ALU.mult, ALU.add).then_inc(yv_done, 1)
                    dve.wait_ge(yr_done, b + 1)
                    for w in range(NW):
                        nc.vector.tensor_scalar(XN[:, w, :], XA[:, w, :], Rd[:, w:w + 1], None, ALU.mult).then_inc(yn_done, 1)
                    for w in range(NW):
                        bank = d_full("down", w)
                        dve.wait_ge(res_done, b * NW + (NW + w + 1))
                        nc.vector.tensor_tensor(XA[:, w, :], bank[:, 0:D], XA[:, w, :], ALU.add).then_inc(d_free, 1)
                        dve.wait_ge(d_free, b * ND + (Dn["down", w] + 3))
                        written(nc.vector.tensor_tensor(XA[:, w, :], XA[:, w, :], DownB, ALU.add))
                        dve.sem_inc(x1_done, 1)
                        written(nc.vector.bn_stats(Bn[:, w, :], XA[:, w, :]))
                        dve.sem_inc(seen_bn, 1)
                        written(nc.vector.bn_aggr(Mv[:, w, :], Bn[:, w, :]))
                        nc.vector.tensor_scalar(Rd[:, w:w + 1], Mv[:, w, 1:2], LN_EPS, None, ALU.add).then_inc(mv1_done, 1)
                        dve.wait_ge(rd1_done, b * NW + w + 1)
                        nc.vector.tensor_scalar(XN[:, w, :], XA[:, w, :], Mv[:, w, 0:1], Rd[:, w:w + 1], ALU.subtract, ALU.mult).then_inc(x2_done, 1)
                    assert steps[0] == AV_STEPS, steps[0]


def attn_arrays(inp):
    f = np.float32
    g = lambda n: inp["L0_attn_" + n]
    convw = np.ascontiguousarray(g("conv_w").reshape(NC, P, CONV_K).transpose(1, 0, 2))
    cols = np.concatenate([g("gate_b").reshape(NC, P).T, g("mlp_up_b").reshape(NU, P).T], 1)
    wcat = np.concatenate([g("read_bits_w"), g("write_bits_w"), g("qkey_w"), g("wkey_w"), g("value_w"),
                           g("write_gate_w"), g("gate_long_w"), g("gate_mem_w")], 0).T
    pw = np.tile(2.0 ** np.arange(BITS), 2 * H).astype(f)
    row = np.concatenate([pw, g("state_decay_logit"), g("write_gate_b"), g("gate_long_b"), g("gate_mem_b"), g("mlp_down_b")])
    rv = np.concatenate([np.broadcast_to(row[None], (P, row.size)), np.arange(P, dtype=f)[:, None]], 1)
    return {"gate_wt": g("gate_w").T, "conv_w": convw, "cols": cols, "wcat": wcat, "state_in": g("state_in_w"),
            "state_out_t": g("state_out_w").T, "mem_out_t": g("mem_out_w").T, "up_wt": g("mlp_up_w").T,
            "down_wt": g("mlp_down_w").T, "rowsv": rv}


def build(nc, d, x1, x2, y0, out):
    build_attn(nc, d["x"], x1, x2, *(d[n] for n in ATTN_NAMES), d["ident"])
    build_ffn(nc, x2, x1, y0, out, *(d[n] for n in FFN_NAMES))


ATTN_NAMES = ("gate_wt", "conv_w", "cols", "wcat", "state_in", "state_out_t", "mem_out_t", "up_wt", "down_wt", "rowsv")
FFN_NAMES = ("wqkv", "wo", "w1", "w2", "pvec", "qs2", "b2", "tabc", "tabs", "ident", "maskd")


def kernel(**inputs):
    import numpy as _np
    import concourse.bacc as _bacc
    from concourse.bass_utils import run_bass_kernel_spmd as _run

    inp = {k: _np.asarray(v) for k, v in inputs.items()}
    arrays = {**attn_arrays(inp), **ffn_arrays(inp), "x": inp["L0_attn_x"]}
    arrays = {k: _np.ascontiguousarray(v) for k, v in arrays.items()}
    nc = _bacc.Bacc("TRN2", target_bir_lowering=False, num_devices=1)
    d = {k: nc.dram_tensor(k, v.shape, F32, kind="ExternalInput").ap() for k, v in arrays.items()}
    scratch = [nc.dram_tensor(n, (B, T, D), F32, kind="Internal").ap() for n in ("x1", "x2", "y0")]
    out = nc.dram_tensor("out", (B, T, D), F32, kind="ExternalOutput").ap()
    build(nc, d, *scratch, out)
    r = _run(nc, [arrays], core_ids=[0])
    return r.results[0]["out"]
```

```python
from contextlib import ExitStack
from itertools import chain

import numpy as np

import concourse.bass as bass
from concourse import mybir

F32 = mybir.dt.float32
ALU = mybir.AluOpType
ACT = mybir.ActivationFunctionType
AX = mybir.AxisListType.X

P = 128
B, T, D = 4, 1024, 256
NW = T // P
NC = D // P
DEPTH, HEADS, DH = 2, 8, 64
INNER = HEADS * DH
NHP = HEADS // 2
HID = int(D * 4 * 2 / 3)
NM = -(-HID // P)
QK_SCALE = 8.0
LN_EPS = 1e-5
MASKED = -1e30
GT = 512
WPG = GT // P
NG = T // GT


OUT_LAG = 2
NORM_LAG = 3
MLP_STEPS = {0: (1, -NW), 1: (2, -NW), 2: (3, -NW), 3: (0, -WPG), 4: (1, -WPG), 5: (2, -WPG), 6: (3, -WPG), 7: (0, 0)}
NONE = range(0)
MLP_WORK = {(0, 0): (range(WPG), NONE, NONE, NONE), (0, 1): (NONE, range(NM), NONE, NONE),
            (1, 0): (NONE, NONE, range(0, 2), NONE), (1, 1): (NONE, NONE, range(2, 4), NONE),
            (2, 0): (NONE, NONE, range(4, NM), NONE), (2, 1): (NONE, NONE, NONE, range(0, 1)),
            (3, 0): (NONE, NONE, NONE, range(1, 3)), (3, 1): (NONE, NONE, NONE, range(3, WPG))}


def rows(m):
    return min(P, HID - m * P)


def head_of(unit, i):
    return 4 * (unit // 2) + 2 * i + unit % 2


def bcast(ap, at, n):
    names = [f"d{i}" for i in range(len(ap.shape) - 1)]
    out = names[:at] + ["o"] + names[at:]
    src = names[:at] + [f"(o {names[at]})"] + names[at + 1:] if at < len(names) else names[:-1] + [f"({names[-1]} o)"]
    r = ap.rearrange(f"p {' '.join(src)} -> p {' '.join(out)}", o=1)
    shape = list(r.shape)
    shape[at + 1] = n
    return r.to_broadcast(shape)


def ahead(s):
    return s + 2 < NW


def mlp_units(step, half):
    quarter, w0 = MLP_STEPS[step]
    turned, gates, ups, downs = MLP_WORK[quarter, half]
    return ([("A", "zT", w0 + i) for i in turned] + [("A", "gate", w0, m) for m in gates]
            + [("D", "up", w0, m) for m in ups] + [("D", "down", w0 + i) for i in downs])


def ffn_units(prev, cur):
    def has(w):
        return cur if w >= 0 else prev

    order = []
    if cur:
        order += [("A", "xT", 0), ("A", "xT", 1)]
    if prev:
        order += [("A", "oT", -OUT_LAG), ("D", "wo", -OUT_LAG)]
        order += [("A", "pT", -1, u) for u in range(NHP)]
        order += mlp_units(0, 0)
    for s in range(NW):
        if cur:
            order += [("A", "qT", s), ("A", "kT", s)]
        if has(MLP_STEPS[s][1]) and ahead(s):
            order += mlp_units(s, 0 if s else 1)
        if cur and ahead(s):
            order.append(("A", "xT", s + 2))
        if s and has(s - OUT_LAG):
            order.append(("A", "oT", s - OUT_LAG))
        if cur:
            order += [("D", "sim", s, 0), ("D", "sim", s, 1)]
        if has(MLP_STEPS[s][1]) and not ahead(s):
            order += mlp_units(s, 0)
        if cur:
            order += [("D", "sim", s, 2), ("D", "sim", s, 3)]
        if s and has(s - OUT_LAG):
            order.append(("D", "wo", s - OUT_LAG))
        if s and cur:
            order += [("A", "pT", s - 1, u) for u in range(NHP)]
        if s and has(MLP_STEPS[s][1]):
            order += mlp_units(s, 1)
    index = {"A": {}, "D": {}}
    for ring, *key in order:
        index[ring][tuple(key)] = len(index[ring])
    return index["A"], index["D"]


def build_ffn(nc, x2, x1, y0, out, wqkv, wo, w1, w2, pvec, qs2, b2, tabc, tabs, ident, maskd):
    FIRST, FULL, LAST = ffn_units(False, True), ffn_units(True, True), ffn_units(True, False)
    with ExitStack() as ctx:
        def sb(name, shape, dt=F32):
            return ctx.enter_context(nc.sbuf_tensor(name, shape, dt))

        def psum(name, shape):
            return ctx.enter_context(nc.psum_tensor(name, shape, F32))

        def sem(name):
            return ctx.enter_context(nc.semaphore(name))

        Wqkv = [sb(f"Wqkv{i}", [P, NC, 3 * INNER]) for i in range(DEPTH)]
        Wo = [sb(f"Wo{i}", [P, NHP, D]) for i in range(DEPTH)]
        W1 = [sb(f"W1{i}", [P, NC, 2 * HID]) for i in range(DEPTH)]
        W2 = [sb(f"W2{i}", [P, NM, D]) for i in range(DEPTH)]
        Pv = sb("Pv", [P, DEPTH, 2 * NM + 2 * NC])
        Qs = sb("Qs", [P, DEPTH, 2, 2, DH])
        B2 = sb("B2", [P, DEPTH, D])
        TabC = sb("TabC", [P, NW, 2, DH])
        TabS = sb("TabS", [P, NW, 2, DH])
        Cs = sb("Cs", [P, NW, 2, DH])
        Ss = sb("Ss", [P, NW, 2, DH])
        Id = sb("Id", [P, P])
        Mk = sb("Mk", [P, 2, P])
        Half = sb("Half", [P, 2 * HEADS])
        X = sb("X", [P, NW, D])
        XM = sb("XM", [P, NW, D])
        X1 = sb("X1", [P, WPG, D])
        XS = sb("XS", [P, NW, P])
        XT = sb("XT", [P, NC, T + 1])
        QKr = sb("QKr", [P, 2, 2, HEADS, DH])
        T2 = sb("T2", [P, 2, HEADS, DH])
        Sq = sb("Sq", [P, 2 * HEADS, DH])
        Ssum = sb("Ssum", [P, 2 * HEADS])
        Rn = sb("Rn", [P, 2 * HEADS])
        V = sb("V", [P, 4, INNER])
        KT = sb("KT", [P, 4, NHP, P])
        QT = sb("QT", [P, NHP, P])
        SM = sb("SM", [P, 2, NHP, 2, 2, P])
        Mx = sb("Mx", [P, HEADS])
        Nb = sb("Nb", [P, 2, HEADS])
        Rs = sb("Rs", [P, 2, HEADS])
        Ri = sb("Ri", [P, 2, HEADS])
        PT = sb("PT", [P, NHP, 2, 2, P])
        On = sb("On", [P, HEADS, DH])
        OT = sb("OT", [P, NHP, P])
        Bn = sb("Bn", [P, 2, 6])
        Mv = sb("Mv", [P, NW, 2])
        Ve = sb("Ve", [P, NW])
        Rd = sb("Rd", [P, NW])
        Z = sb("Z", [P, NW, D])
        ZT = sb("ZT", [P, NC, GT])
        HT = sb("HT", [P, NM, GT])

        qkv_ps = psum("qkv_ps", [P, 3, 512])
        a_ps = psum("a_ps", [P, 2, 512])
        d_ps = psum("d_ps", [P, 2, 512])
        o_ps = psum("o_ps", [P, 512])

        s_wqkv = [sem(f"wqkv_in{i}") for i in range(DEPTH)]
        s_wt = [sem(f"wt{i}") for i in range(DEPTH)]
        s_cst = sem("cst")
        s_set = sem("set")
        s_x = [sem(f"x_in{w}") for w in range(NW)]
        s_x1 = [sem(f"x1_in{i}") for i in range(WPG)]
        s_sh = [sem(f"shift{w}") for w in range(NW)]
        s_st = [sem(f"stored{w}") for w in range(NW)]
        a_ready, a_free = sem("a_ready"), sem("a_free")
        d_ready, d_free = sem("d_ready"), sem("d_free")
        qk_ready, qk_read = sem("qk_ready"), sem("qk_read")
        v_ready, v_copied = sem("v_ready"), sem("v_copied")
        sq_done, sums_done, ssum_done = sem("sq_done"), sem("sums_done"), sem("ssum_done")
        rot_terms, rn_done, qkr_sum, qk_rot = sem("rot_terms"), sem("rn_done"), sem("qkr_sum"), sem("qk_rot")
        tabs_done = sem("tabs_done")
        masked, max_done, nb_done, exp_done = sem("masked"), sem("max_done"), sem("nb_done"), sem("exp_done")
        recip_done, o_ready, o_norm = sem("recip_done"), sem("o_ready"), sem("o_norm")
        xmid = sem("xmid")
        bn_done, bn_seen, mv_done, ve_done, rd_done, z_done = (sem("bn_done"), sem("bn_seen"), sem("mv_done"), sem("ve_done"),
                                                               sem("rd_done"), sem("z_done"))
        x1_added, b2_added = sem("x1_added"), sem("b2_added")
        gelu_done, ht_done, fin_done = sem("gelu_done"), sem("ht_done"), sem("fin_done")

        stages = [(x2, y0), (y0, out)]

        class Pass:

            def __init__(self, it, b, layer, b_prev, layer_prev, units, a_base, d_base):
                self.it, self.b, self.layer, self.b_prev, self.layer_prev = it, b, layer, b_prev, layer_prev
                (self.A, self.D), self.a_base, self.d_base = units, a_base, d_base

            def has(self, w):
                return (self.layer if w >= 0 else self.layer_prev) is not None

            def layer_of(self, w):
                return self.layer if w >= 0 else self.layer_prev

            def seq_of(self, w):
                return self.b if w >= 0 else self.b_prev

            def win(self, w, n=1):
                return self.it * (NW * n) + w * n

        NA1, ND1 = len(FIRST[0]), len(FIRST[1])
        NAF, NDF = len(FULL[0]), len(FULL[1])
        assert NA1 % 2 == ND1 % 2 == NAF % 2 == NDF % 2 == 0

        def passes(eng, body):
            body(Pass(0, 0, 0, None, None, FIRST, 0, 0))
            for layer in range(DEPTH):
                if layer:
                    n = layer * B - 1
                    body(Pass(layer * B, 0, layer, B - 1, layer - 1, FULL, NA1 + n * NAF, ND1 + n * NDF))
                n = layer * B - 1
                with eng.Fori(1, B) as b:
                    body(Pass(b + layer * B, b, layer, b - 1, layer, FULL, b * NAF + (NA1 + n * NAF), b * NDF + (ND1 + n * NDF)))
            n = DEPTH * B - 1
            body(Pass(DEPTH * B, None, None, B - 1, DEPTH - 1, LAST, NA1 + n * NAF, ND1 + n * NDF))

        with nc.Block() as block:

            @block.sync
            def _(sp):
                for dst, src in ((Id[:], ident), (TabC[:], tabc.rearrange("(w p) a d -> p w a d", p=P)),
                                 (TabS[:], tabs.rearrange("(w p) a d -> p w a d", p=P)), (Mk[:], maskd),
                                 (Pv[:], pvec), (Qs[:], qs2), (B2[:], b2)):
                    sp.dma_start(dst, src).then_inc(s_cst, 16)
                sp.dma_start(Wqkv[0][:], wqkv[0].rearrange("(c p) n -> p c n", p=P)).then_inc(s_wqkv[0], 16)

                def body(p):
                    def load_x(w):
                        if p.layer_prev is not None:
                            sp.wait_ge(xmid, p.win(w - NW) + 1)
                        sp.dma_start(X[:, w, :], stages[p.layer][0][p.b, w * P:(w + 1) * P, :]).then_inc(s_x[w], 16)

                    if p.has(0):
                        for w in range(NW - OUT_LAG):
                            load_x(w)
                    for s in range(NW):
                        w = s - OUT_LAG
                        if p.has(w):
                            v = w % NW
                            sp.wait_ge(xmid, p.win(w) + 1)
                            sp.dma_start(XS[1:P, v, :], XM[0:P - 1, v, P:D]).then_inc(s_sh[v], 16)
                            if v + 1 < NW:
                                sp.dma_start(XS[0:1, v + 1, :], XM[P - 1:P, v, P:D]).then_inc(s_sh[v + 1], 16)
                        if s < OUT_LAG and p.has(0):
                            load_x(NW - OUT_LAG + s)
                        quarter, w0 = MLP_STEPS[s]
                        if quarter == 0 and p.has(w0) and p.layer_of(w0) == DEPTH - 1:
                            if not (p.layer_prev != DEPTH - 1 and w0 == 0):
                                sp.wait_ge(b2_added, p.win(w0))
                            for i in range(WPG):
                                t0 = (w0 % NW + i) * P
                                sp.dma_start(X1[:, i, :], x1[p.seq_of(w0), t0:t0 + P, :]).then_inc(s_x1[i], 16)

                passes(sp, body)

            @block.tensor
            def _(pe):
                pe.wait_ge(s_cst, 7 * 16)
                pe.wait_ge(s_set, 3)

                def body(p):
                    def a_unit(*key):
                        pe.wait_ge(a_free, p.a_base + (p.A[key] + 1))
                        return a_ps[:, p.A[key] % 2, :]

                    def a_emptied(*key):
                        pe.wait_ge(a_free, p.a_base + (p.A[key] + 3))

                    def d_unit(*key):
                        pe.wait_ge(d_free, p.d_base + (p.D[key] + 1))
                        return d_ps[:, p.D[key] % 2, :]

                    def transposes(bank, srcs):
                        for i, src in enumerate(srcs):
                            last = nc.tensor.transpose(bank[:, i * P:(i + 1) * P], src, Id[:])
                        return last

                    def x_transposed(w):
                        pe.wait_ge(s_x[w], p.it * 16 + 16)
                        transposes(a_unit("xT", w), [X[:, w, c * P:(c + 1) * P] for c in range(NC)]).then_inc(a_ready, 1)

                    def project(w, parts):
                        lhs = [XT[:, 0, 1 + w * P:1 + (w + 1) * P], XT[:, 1, w * P:(w + 1) * P]]
                        for part in parts:
                            for c in range(NC):
                                last = nc.tensor.matmul(qkv_ps[:, part, :], lhs[c],
                                                        Wqkv[p.layer][:, c, part * INNER:(part + 1) * INNER],
                                                        start=(c == 0), stop=(c == NC - 1))
                        return last

                    def project_qk(w):
                        a_emptied("xT", w)
                        pe.wait_ge(qk_read, p.win(w) + 1)
                        project(w, (0, 1)).then_inc(qk_ready, 1)

                    def project_v(w):
                        pe.wait_ge(v_copied, p.win(w) + 1)
                        project(w, (2,)).then_inc(v_ready, 1)

                    def qk_transposed(w):
                        pe.wait_ge(qk_rot, p.win(w) + 2)
                        for a, name in enumerate(("qT", "kT")):
                            srcs = [QKr[:, w % 2, a, 2 * i:2 * i + 2, :].rearrange("p h d -> p (h d)") for i in range(NHP)]
                            transposes(a_unit(name, w), srcs).then_inc(a_ready, 1)

                    def scores(w, a):
                        banks = [d_unit("sim", w, 2 * a + r) for r in range(2)]
                        if a == 0:
                            a_emptied("kT", w)
                        own = [(i, blk) for i in range(2) for blk in range(2) if w or blk]
                        for i, blk in own:
                            for r in range(2):
                                half = slice(r * DH, (r + 1) * DH)
                                mm = nc.tensor.matmul(banks[r][:, (2 * i + blk) * P:(2 * i + blk + 1) * P],
                                                      QT[half, 2 * a + i, :], KT[half, (w - 1 + blk) % 4, 2 * a + i, :],
                                                      start=True, stop=True)
                                if (i, blk) == own[-1]:
                                    mm.then_inc(d_ready, 1)

                    def blocks(w):
                        return (0, 1) if w % NW else (1,)

                    def probs_transposed(w, u):
                        pe.wait_ge(exp_done, p.win(w, NHP) + u + 1)
                        bank = a_unit("pT", w, u)
                        for i in range(2):
                            for blk in blocks(w):
                                j = 2 * i + blk
                                last = nc.tensor.transpose(bank[:, j * P:(j + 1) * P], SM[:, w % 2, u, i, blk, :], Id[:])
                        last.then_inc(a_ready, 1)

                    def attend(w, u):
                        if u == 0:
                            pe.wait_ge(o_norm, p.win(w) + 1)
                            pe.wait_ge(v_copied, p.win(w) + 2)
                        a_emptied("pT", w, u)
                        for i in range(2):
                            head = head_of(u, i)
                            cols = slice(head * DH, (head + 1) * DH)
                            for blk in blocks(w):
                                last = nc.tensor.matmul(o_ps[:, cols], PT[:, u, i, blk, :], V[:, (w - 1 + blk) % 4, cols],
                                                        start=(blk == blocks(w)[0]), stop=(blk == 1))
                        if u == NHP - 1:
                            last.then_inc(o_ready, 1)

                    def attention(w, w_out=None):
                        probs_transposed(w, 0)
                        probs_transposed(w, 1)
                        if w_out is not None:
                            project_out(w_out)
                        for u in range(2, NHP):
                            attend(w, u - 2)
                            probs_transposed(w, u)
                        attend(w, NHP - 2)
                        attend(w, NHP - 1)

                    def out_transposed(w):
                        pe.wait_ge(o_norm, p.win(w) + 2)
                        srcs = [On[:, 2 * i:2 * i + 2, :].rearrange("p h d -> p (h d)") for i in range(NHP)]
                        transposes(a_unit("oT", w), srcs).then_inc(a_ready, 1)

                    def project_out(w):
                        bank = d_unit("wo", w)
                        a_emptied("oT", w)
                        for i in range(NHP):
                            last = nc.tensor.matmul(bank[:, 0:D], OT[:, i, :], Wo[p.layer_of(w)][:, i, :],
                                                    start=(i == 0), stop=(i == NHP - 1))
                        last.then_inc(d_ready, 1)

                    def hidden(ring, name, w0, m, first, ready):
                        n = rows(m)
                        bank = ring(name, w0, m)
                        for c in range(NC):
                            last = nc.tensor.matmul(bank[0:n, :], W1[p.layer_of(w0)][:, c, first:first + n], ZT[:, c, :],
                                                    start=(c == 0), stop=(c == NC - 1))
                        last.then_inc(ready, 1)

                    def down(w, w0):
                        bank = d_unit("down", w)
                        pe.wait_ge(ht_done, p.it * (NG * NM) + (w0 // WPG + 1) * NM)
                        t0 = (w - w0) * P
                        for m in range(NM):
                            n = rows(m)
                            last = nc.tensor.matmul(bank[:, 0:D], HT[0:n, m, t0:t0 + P], W2[p.layer_of(w)][0:n, m, :],
                                                    start=(m == 0), stop=(m == NM - 1))
                        last.then_inc(d_ready, 1)

                    def feed_forward(step, half):
                        quarter, w0 = MLP_STEPS[step]
                        if not p.has(w0):
                            return
                        turned, gates, ups, downs = MLP_WORK[quarter, half]
                        for i in turned:
                            w = w0 + i
                            pe.wait_ge(z_done, p.win(w) + 1)
                            transposes(a_unit("zT", w), [Z[:, w % NW, c * P:(c + 1) * P] for c in range(NC)]).then_inc(a_ready, 1)
                        for m in gates:
                            if m == 0:
                                a_emptied("zT", w0 + WPG - 1)
                            hidden(a_unit, "gate", w0, m, HID + m * P, a_ready)
                        for m in ups:
                            hidden(d_unit, "up", w0, m, m * P, d_ready)
                        for i in downs:
                            down(w0 + i, w0)

                    if p.has(0):
                        if p.layer != p.layer_prev:
                            pe.wait_ge(s_wqkv[p.layer], 16)
                        x_transposed(0)
                        x_transposed(1)
                    if p.has(-OUT_LAG):
                        out_transposed(-OUT_LAG)
                    if p.has(0):
                        project_qk(0)
                        project_v(0)
                    if p.has(-OUT_LAG):
                        attention(-1, -OUT_LAG)
                    if p.has(0):
                        project_qk(1)
                        project_v(1)
                    feed_forward(0, 0)
                    if p.has(0) and p.layer != p.layer_prev:
                        pe.wait_ge(s_wt[p.layer], 4 * 16)
                    for s in range(NW):
                        if p.has(0):
                            qk_transposed(s)
                        if ahead(s):
                            feed_forward(s, 0 if s else 1)
                        if p.has(0) and ahead(s):
                            x_transposed(s + 2)
                        if s and p.has(s - OUT_LAG):
                            out_transposed(s - OUT_LAG)
                        if p.has(0):
                            scores(s, 0)
                        if not ahead(s):
                            feed_forward(s, 0)
                        if p.has(0) and ahead(s):
                            project_qk(s + 2)
                        if p.has(0):
                            scores(s, 1)
                        if s and p.has(0):
                            attention(s - 1, s - OUT_LAG if p.has(s - OUT_LAG) else None)
                        elif s and p.has(s - OUT_LAG):
                            project_out(s - OUT_LAG)
                        if p.has(0) and ahead(s):
                            project_v(s + 2)
                        if s:
                            feed_forward(s, 1)

                passes(pe, body)

            @block.scalar
            def _(act):
                act.sem_inc(a_free, 2)
                act.sem_inc(v_copied, 1)
                for w in range(NW):
                    act.sem_inc(s_st[w], 16)
                act.wait_ge(s_wqkv[0], 16)
                act.wait_ge(s_x[NW - OUT_LAG - 1], 16)
                for i in range(DEPTH):
                    if i:
                        act.dma_start(Wqkv[i][:], wqkv[i].rearrange("(c p) n -> p c n", p=P)).then_inc(s_wqkv[i], 16)
                    act.dma_start(Wo[i][:], wo[i].rearrange("(c p) n -> p c n", p=P)).then_inc(s_wt[i], 16)
                    act.dma_start(W1[i][:], w1[i].rearrange("(c p) n -> p c n", p=P)).then_inc(s_wt[i], 16)
                    full = (NM - 1) * P
                    act.dma_start(W2[i][:, 0:NM - 1, :], w2[i, 0:full].rearrange("(c p) n -> p c n", p=P)).then_inc(s_wt[i], 16)
                    act.dma_start(W2[i][0:HID - full, NM - 1, :], w2[i, full:HID]).then_inc(s_wt[i], 16)
                act.wait_ge(s_cst, 7 * 16)
                act.wait_ge(s_set, 3)

                def body(p):
                    def a_full(*key):
                        act.wait_ge(a_ready, p.a_base + (p.A[key] + 1))
                        return a_ps[:, p.A[key] % 2, :]

                    def evacuate(dst, bank):
                        nc.scalar.activation(dst, bank, ACT.Copy).then_inc(a_free, 1)

                    def x_evacuated(w):
                        evacuate(XT[:, :, 1 + w * P:1 + (w + 1) * P], a_full("xT", w)[:, 0:D].rearrange("p (c t) -> p c t", c=NC))

                    def squares(w):
                        act.wait_ge(qk_ready, p.win(w) + 1)
                        act.wait_ge(ssum_done, p.win(w) + 1)
                        nc.scalar.activation(Sq[:], qkv_ps[:, 0:2, :].rearrange("p a (h d) -> p (a h) d", d=DH),
                                             ACT.Square).then_inc(sq_done, 1)

                    def v_copy(w):
                        act.wait_ge(v_ready, p.win(w) + 1)
                        nc.scalar.activation(V[:, w % 4, :], qkv_ps[:, 2, :], ACT.Copy).then_inc(v_copied, 1)

                    def exponentials(w, u):
                        act.wait_ge(nb_done, p.win(w, NHP) + u + 1)
                        for i in range(2):
                            head = head_of(u, i)
                            s = SM[:, w % 2, u, i, :, :] if w else SM[:, w % 2, u, i, 1:2, :]
                            last = nc.scalar.activation(s, s, ACT.Exp, bias=Nb[:, w % 2, 2 * u + i:2 * u + i + 1], scale=QK_SCALE,
                                                        accum_out=Rs[:, w % 2, head:head + 1])
                        last.then_inc(exp_done, 1)

                    def probs_evacuated(w, u):
                        bank = a_full("pT", w, u).rearrange("p (h k t) -> p h k t", h=2, k=2)
                        k = slice(0, 2) if w % NW else slice(1, 2)
                        evacuate(PT[:, u, :, k, :], bank[:, :, k, :])

                    def out_evacuated(w):
                        evacuate(OT[:], a_full("oT", w).rearrange("p (a t) -> p a t", a=NHP))

                    def feed_forward(step, half):
                        quarter, w0 = MLP_STEPS[step]
                        if not p.has(w0):
                            return
                        turned, gates, _, _ = MLP_WORK[quarter, half]
                        layer = p.layer_of(w0)
                        for i in turned:
                            bank = a_full("zT", w0 + i)
                            for c in range(NC):
                                g = 2 * NM + c
                                last = nc.scalar.activation(ZT[:, c, i * P:(i + 1) * P], bank[:, c * P:(c + 1) * P], ACT.Identity,
                                                            scale=Pv[:, layer, g:g + 1], bias=Pv[:, layer, g + NC:g + NC + 1])
                            last.then_inc(a_free, 1)
                        for m in gates:
                            n = rows(m)
                            nc.scalar.activation(HT[0:n, m, :], a_full("gate", w0, m)[0:n, :], ACT.Gelu,
                                                 bias=Pv[0:n, layer, NM + m:NM + m + 1]).then_inc(a_free, 1)
                            if m == NM - 1:
                                act.wait_ge(a_free, p.a_base + (p.A["gate", w0, m] + 3))
                                act.sem_inc(gelu_done, 1)

                    def store(w):
                        act.wait_ge(fin_done, p.win(w) + 1)
                        v = w % NW
                        act.dma_start(stages[p.layer_of(w)][1][p.seq_of(w), v * P:(v + 1) * P, :], Z[:, v, :]).then_inc(s_st[v], 16)

                    if p.has(0):
                        x_evacuated(0)
                        x_evacuated(1)
                    if p.has(-OUT_LAG):
                        out_evacuated(-OUT_LAG)
                    if p.has(0):
                        squares(0)
                        v_copy(0)
                    if p.has(-1):
                        for u in range(NHP):
                            probs_evacuated(-1, u)
                    if p.has(0):
                        squares(1)
                        v_copy(1)
                    feed_forward(0, 0)
                    for s in range(NW):
                        if p.has(0):
                            for name, dst in (("qT", QT[:]), ("kT", KT[:, s % 4])):
                                evacuate(dst, a_full(name, s).rearrange("p (a t) -> p a t", a=NHP))
                        if ahead(s):
                            feed_forward(s, 0 if s else 1)
                        if p.has(0) and ahead(s):
                            x_evacuated(s + 2)
                        if s and p.has(s - OUT_LAG):
                            out_evacuated(s - OUT_LAG)
                        if not ahead(s):
                            feed_forward(s, 0)
                        if p.has(0):
                            exponentials(s, 0)
                            exponentials(s, 1)
                        if p.has(0) and ahead(s):
                            squares(s + 2)
                        lag = s and p.has(0)
                        for u in range(NHP):
                            if lag:
                                probs_evacuated(s - 1, u)
                            if p.has(0) and u % 2:
                                exponentials(s, 2 + u // 2)
                        if p.has(0) and ahead(s):
                            v_copy(s + 2)
                        quarter, w0 = MLP_STEPS[(s - 1) % NW]
                        if s and p.has(w0):
                            for i in chain(MLP_WORK[quarter, 0][3], MLP_WORK[quarter, 1][3]):
                                store(w0 + i)
                        if s:
                            feed_forward(s, 1)

                passes(act, body)
                for w in range(NW):
                    act.wait_ge(s_st[w], (DEPTH * B + 1) * 16)

            @block.gpsimd
            def _(pool):
                nc.gpsimd.memset(Half[:], -0.5).then_inc(s_set, 1)
                nc.gpsimd.memset(XT[:, 1, 0:1], 0.0).then_inc(s_set, 1)
                nc.gpsimd.memset(XS[0:1, 0, :], 0.0).then_inc(s_set, 1)
                pool.sem_inc(qk_rot, 1)
                pool.wait_ge(s_set, 3)
                pool.wait_ge(s_cst, 7 * 16)

                def body(p):
                    def rotate(w):
                        pool.wait_ge(ssum_done, p.win(w) + 2)
                        nc.gpsimd.tensor_tensor(Rn[:], Ssum[:], Half[:], ALU.pow).then_inc(rn_done, 1)
                        pool.wait_ge(rot_terms, p.win(w) + 1)
                        q = QKr[:, w % 2].rearrange("p a h d -> p (a h) d")
                        nc.gpsimd.tensor_tensor(q, q, T2[:].rearrange("p a h d -> p (a h) d"), ALU.add).then_inc(qkr_sum, 1)
                        pool.wait_ge(qkr_sum, p.win(w) + 1)
                        pool.wait_ge(rn_done, p.win(w) + 1)
                        nc.gpsimd.tensor_tensor(q, q, bcast(Rn[:], 1, DH), ALU.mult).then_inc(qk_rot, 1)

                    def rsqrt_var(w):
                        v = w % NW
                        pool.wait_ge(ve_done, p.win(w) + 1)
                        nc.gpsimd.tensor_tensor(Rd[:, v:v + 1], Ve[:, v:v + 1], Half[:, 0:1], ALU.pow).then_inc(rd_done, 1)

                    def residuals(w0):
                        layer = p.layer_of(w0)
                        for w in range(w0, w0 + WPG):
                            v = w % NW
                            pool.wait_ge(z_done, p.win(w) + 1)
                            for x in (v, v + 1):
                                if x < NW:
                                    n = 32 if x else 16
                                    pool.wait_ge(s_sh[x], (p.it + (1 if w >= 0 else 0)) * n)
                            if layer == DEPTH - 1:
                                i = w - w0
                                pool.wait_ge(s_x1[i], (p.it * NG + (w0 // WPG + 1 - (DEPTH - 1) * B * NG)) * 16)
                                nc.gpsimd.tensor_tensor(XM[:, v, :], XM[:, v, :], X1[:, i, :], ALU.add).then_inc(x1_added, 1)
                                pool.wait_ge(x1_added, p.win(w) + 1 - (DEPTH - 1) * B * NW)
                            nc.gpsimd.tensor_tensor(XM[:, v, :], XM[:, v, :], B2[:, layer, :], ALU.add).then_inc(b2_added, 1)

                    if p.has(0):
                        rotate(0)
                        rotate(1)
                    for s in range(NW):
                        if p.has(s - NORM_LAG):
                            rsqrt_var(s - NORM_LAG)
                        if p.has(0) and ahead(s):
                            rotate(s + 2)
                        quarter, w0 = MLP_STEPS[s]
                        if quarter == 1 and p.has(w0):
                            residuals(w0)

                passes(pool, body)

            @block.vector
            def _(dve):
                dve.sem_inc(d_free, 2)
                dve.sem_inc(qk_read, 1)
                dve.sem_inc(ssum_done, 1)
                dve.sem_inc(o_norm, 1)
                dve.wait_ge(s_cst, 7 * 16)

                def scaled_tables(layer):
                    for swap, (dst, tab) in enumerate(((Cs, TabC), (Ss, TabS))):
                        nc.vector.tensor_tensor(dst[:], tab[:], bcast(Qs[:, layer, swap], 0, NW), ALU.mult).then_inc(tabs_done, 1)
                    dve.wait_ge(tabs_done, 2 * (layer + 1))

                def body(p):
                    def d_full(*key):
                        dve.wait_ge(d_ready, p.d_base + (p.D[key] + 1))
                        return d_ps[:, p.D[key] % 2, :]

                    def d_written(*key):
                        dve.wait_ge(d_free, p.d_base + (p.D[key] + 3))

                    def rotary_terms(w):
                        dve.wait_ge(qk_rot, p.win(w) + 1)
                        dve.wait_ge(sq_done, p.win(w) + 1)
                        qk = qkv_ps[:, 0:2, :].rearrange("p a (h d) -> p a h d", d=DH)
                        nc.vector.tensor_tensor(QKr[:, w % 2], qk, bcast(Cs[:, w], 1, HEADS), ALU.mult)
                        lo, hi = slice(0, DH // 2), slice(DH // 2, DH)
                        nc.vector.tensor_tensor(T2[:, :, :, lo], qk[:, :, :, hi], bcast(Ss[:, w, :, lo], 1, HEADS), ALU.mult)
                        nc.vector.tensor_tensor(T2[:, :, :, hi], qk[:, :, :, lo], bcast(Ss[:, w, :, hi], 1, HEADS),
                                                ALU.mult).then_inc(rot_terms, 1)
                        dve.wait_ge(rot_terms, p.win(w) + 1)
                        dve.sem_inc(qk_read, 1)
                        nc.vector.reduce_sum(Ssum[:], Sq[:], AX).then_inc(sums_done, 1)
                        dve.wait_ge(sums_done, p.win(w) + 1)
                        nc.vector.tensor_scalar(Ssum[:], Ssum[:], 1e-24, None, ALU.max).then_inc(ssum_done, 1)

                    def mask_and_max(w, u):
                        bank = d_full("sim", w, u).rearrange("p (h k t) -> p h k t", h=2, k=2)
                        k = slice(0, 2) if w else slice(1, 2)
                        s = SM[:, w % 2, u, :, k, :]
                        nc.vector.tensor_tensor(s, bank[:, :, k, :], bcast(Mk[:, k, :], 0, 2), ALU.add).then_inc(d_free, 1)
                        d_written("sim", w, u)
                        nc.vector.reduce_max(Mx[:, 2 * u:2 * u + 2], s.rearrange("p h k t -> p h (k t)"), AX).then_inc(max_done, 1)
                        dve.wait_ge(max_done, p.win(w, NHP) + u + 1)
                        nc.vector.tensor_scalar(Nb[:, w % 2, 2 * u:2 * u + 2], Mx[:, 2 * u:2 * u + 2], -QK_SCALE, None,
                                                ALU.mult).then_inc(nb_done, 1)

                    def normalise(w):
                        dve.wait_ge(exp_done, p.win(w, NHP) + NHP)
                        nc.vector.reciprocal(Ri[:, w % 2, :], Rs[:, w % 2, :]).then_inc(recip_done, 1)
                        dve.wait_ge(recip_done, p.win(w) + 1)
                        dve.wait_ge(o_ready, p.win(w) + 1)
                        nc.vector.tensor_tensor(On[:], o_ps[:].rearrange("p (h d) -> p h d", d=DH), bcast(Ri[:, w % 2, :], 1, DH),
                                                ALU.mult).then_inc(o_norm, 1)

                    def add_attention(w):
                        v = w % NW
                        bank = d_full("wo", w)
                        nc.vector.tensor_tensor(XM[:, v, :], bank[:, 0:D], X[:, v, :], ALU.add).then_inc(d_free, 1)
                        d_written("wo", w)
                        dve.sem_inc(xmid, 1)

                    def variance(w):
                        v = w % NW
                        dve.wait_ge(s_sh[v], (p.it + (1 if w >= 0 else 0)) * (32 if v else 16))
                        nc.vector.bn_stats(Bn[:, 0, :], XM[:, v, 0:P])
                        nc.vector.bn_stats(Bn[:, 1, :], XS[:, v, :]).then_inc(bn_done, 1)
                        dve.wait_ge(bn_done, p.win(w) + 1)
                        dve.sem_inc(bn_seen, 1)
                        nc.vector.bn_aggr(Mv[:, v, :], Bn[:].rearrange("p a b -> p (a b)")).then_inc(mv_done, 1)
                        dve.wait_ge(mv_done, p.win(w) + 1)
                        nc.vector.tensor_scalar(Ve[:, v:v + 1], Mv[:, v, 1:2], LN_EPS, None, ALU.add).then_inc(ve_done, 1)

                    def layernorm(w):
                        v = w % NW
                        dve.wait_ge(rd_done, p.win(w) + 1)
                        dve.wait_ge(s_st[v], (p.it + (1 if w >= 0 else 0)) * 16)
                        nc.vector.tensor_scalar(Z[:, v, 0:P], XM[:, v, 0:P], Mv[:, v, 0:1], Rd[:, v:v + 1], ALU.subtract, ALU.mult)
                        nc.vector.tensor_scalar(Z[:, v, P:D], XS[:, v, :], Mv[:, v, 0:1], Rd[:, v:v + 1],
                                                ALU.subtract, ALU.mult).then_inc(z_done, 1)

                    def hidden_product(w0, m):
                        n = rows(m)
                        bank = d_full("up", w0, m)
                        if m == 0:
                            dve.wait_ge(gelu_done, p.it * NG + (w0 // WPG + 1))
                        nc.vector.scalar_tensor_tensor(HT[0:n, m, :], bank[0:n, :], Pv[0:n, p.layer_of(w0), m:m + 1],
                                                       HT[0:n, m, :], ALU.add, ALU.mult).then_inc(ht_done, 1)
                        dve.wait_ge(ht_done, p.it * (NG * NM) + (w0 // WPG * NM + m + 1))
                        dve.sem_inc(d_free, 1)

                    def finish(w):
                        v = w % NW
                        bank = d_full("down", w)
                        dve.wait_ge(b2_added, p.win(w) + 1)
                        nc.vector.tensor_tensor(Z[:, v, :], bank[:, 0:D], XM[:, v, :], ALU.add).then_inc(d_free, 1)
                        d_written("down", w)
                        dve.sem_inc(fin_done, 1)

                    def feed_forward(step, half):
                        quarter, w0 = MLP_STEPS[step]
                        if not p.has(w0):
                            return
                        _, _, ups, downs = MLP_WORK[quarter, half]
                        for m in ups:
                            hidden_product(w0, m)
                        for i in downs:
                            finish(w0 + i)

                    if p.has(0) and p.layer != p.layer_prev:
                        scaled_tables(p.layer)
                    if p.has(0):
                        rotary_terms(0)
                    if p.has(-OUT_LAG):
                        add_attention(-OUT_LAG)
                        normalise(-1)
                    if p.has(0):
                        rotary_terms(1)
                    feed_forward(0, 0)
                    for s in range(NW):
                        if ahead(s):
                            feed_forward(s, 0 if s else 1)
                        if p.has(0):
                            mask_and_max(s, 0)
                            mask_and_max(s, 1)
                        if not ahead(s):
                            feed_forward(s, 0)
                        if p.has(s - NORM_LAG):
                            variance(s - NORM_LAG)
                        if p.has(0):
                            mask_and_max(s, 2)
                            mask_and_max(s, 3)
                        if p.has(s - NORM_LAG):
                            layernorm(s - NORM_LAG)
                        if p.has(0) and ahead(s):
                            rotary_terms(s + 2)
                        if s and p.has(s - OUT_LAG):
                            add_attention(s - OUT_LAG)
                        if s and p.has(0):
                            normalise(s - 1)
                        if s:
                            feed_forward(s, 1)

                passes(dve, body)


def ffn_constants():
    f = np.float32
    half = np.arange(0, DH, 2, dtype=f)
    inv = (f(1.0) / np.power(f(10000.0), half / f(DH))).astype(f)
    t = np.arange(T, dtype=f)
    fr = (t[:, None] * inv[None]).astype(f)
    fr = np.concatenate([fr, fr], -1)
    base = ((half + f(0.4 * DH)) / f(1.4 * DH)).astype(f)
    power = ((t - T // 2) / f(P // 2)).astype(f)
    sc = (base[None].astype(f) ** power[:, None]).astype(f)
    sc = np.concatenate([sc, sc], -1)
    sign = np.where(np.arange(DH) < DH // 2, f(-1), f(1))
    cos, sin = np.cos(fr), np.sin(fr) * sign
    tabc = np.stack([cos * sc, cos / sc], 1).astype(f)
    tabs = np.stack([sin * sc, sin / sc], 1).astype(f)
    i, j = np.arange(P)[:, None], np.arange(P)[None]
    mask = np.stack([np.where(j >= i, 0, MASKED), np.where(j <= i, 0, MASKED)], 1).astype(f)
    return tabc, tabs, np.eye(P, dtype=f), mask


def ffn_arrays(inp):
    f = np.float32
    b1, lg, lb = inp["L0_ffn_b1"], inp["L0_ffn_ln_g"], inp["L0_ffn_ln_b"]
    pv = np.zeros((P, DEPTH, 2 * NM + 2 * NC), f)
    for i in range(DEPTH):
        for m in range(NM):
            pv[:rows(m), i, m] = b1[i, m * P:m * P + rows(m)]
            pv[:rows(m), i, NM + m] = b1[i, HID + m * P:HID + m * P + rows(m)]
        for c in range(NC):
            pv[:, i, 2 * NM + c] = lg[i, c * P:(c + 1) * P]
            pv[:, i, 2 * NM + NC + c] = lb[i, c * P:(c + 1) * P]
    qk = np.stack([inp["L0_ffn_q_scale"], inp["L0_ffn_k_scale"]], 1)
    swapped = np.concatenate([qk[..., DH // 2:], qk[..., :DH // 2]], -1)
    qs = np.broadcast_to(np.stack([qk, swapped], 1)[None], (P, DEPTH, 2, 2, DH))
    b2 = np.broadcast_to(inp["L0_ffn_b2"][None], (P, DEPTH, D))
    tabc, tabs, ident, mask = ffn_constants()
    return {"wqkv": inp["L0_ffn_wqkv"], "wo": inp["L0_ffn_wo"], "w1": inp["L0_ffn_w1"], "w2": inp["L0_ffn_w2"],
            "pvec": pv, "qs2": qs, "b2": b2, "tabc": tabc, "tabs": tabs, "ident": ident, "maskd": mask}



F16 = mybir.dt.float16
K = 4
H, BITS, BUCKETS, ASSOC = 2, 9, 128, 2
KD = 32
CONV_K = 4
UP = 4 * D
NU = UP // P
ZR, ZW, ZQ, ZK = 0, H * BITS, 2 * H * BITS, 2 * H * BITS + KD
ZG = ZK + 2 * KD
NZ = ZG + 3
RMS_EPS = 1e-6
SCALE = float(np.float32(1.0 / np.sqrt(KD)))
PAD = CONV_K - 1
ZW3 = 2


def bcast1(ap, n):
    return ap.to_broadcast([P, n])


def z_windows(i):
    return range(i * ZW3, min((i + 1) * ZW3, NW))


NZU = -(-NW // ZW3)


LONG_AFTER = {(0, 0): 0, (0, 1): 1, (0, 2): 2, (0, 3): 3, (1, 0): 4, (1, 1): 5}
LONG_LAST = range(len(LONG_AFTER), NW)


def attn_units(prev, cur):
    order = []
    for g in range(NG):
        if prev:
            order += [("A", "up", g, m) for m in range(NU)]
        if cur and g == 0:
            order += [("A", "xnT", w) for w in range(NW)]
            order += [("A", "gate", c, h) for h in range(NG) for c in range(NC)]
        if cur and g == NG - 1:
            order += [("A", "rows", w) for w in range(NW)]
            order += [("A", "keep", h) for h in range(NG)]
        if prev:
            order += [("D", "down", w) for w in range(g * WPG, (g + 1) * WPG)]
        if cur and g == 0:
            order += [("A", "z", i) for i in range(NZU)]
    if cur:
        for h in range(H):
            order += [("D", "slot_row", h, g) for g in range(NG)] + [("D", "slot_col", h)]
        order += [("A", "long", w) for w in range(NW)]
        order += [("A", "rvT", g) for g in range(NG)]
        order += [("D", "mem", w) for w in range(NW)]
        order += [("A", "ynT", w) for w in range(NW)]
    index = {"A": {}, "D": {}}
    for ring, *key in order:
        index[ring][tuple(key)] = len(index[ring])
    return index["A"], index["D"]


AV_STEPS = 1 + 1 + (CONV_K - 1) * NC + 2 + 2 * H + 2 * H + 3 * H * NW + 8
LV_STEPS = 2 * NG
AP_STEPS = 5


def build_attn(nc, x, x1, x2, gate_wt, conv_w, cols, wcat, state_in, state_out_t, mem_out_t, up_wt, down_wt, rowsv, ident):
    FIRST, FULL, LAST = attn_units(False, True), attn_units(True, True), attn_units(True, False)
    NA1, ND1, NAF, NDF = len(FIRST[0]), len(FIRST[1]), len(FULL[0]), len(FULL[1])
    assert NA1 % 2 == ND1 % 2 == NAF % 2 == NDF % 2 == 0
    PRE = 2 * K
    with ExitStack() as ctx:
        def sb(name, shape, dt=F32):
            return ctx.enter_context(nc.sbuf_tensor(name, shape, dt))

        def psum(name, shape):
            return ctx.enter_context(nc.psum_tensor(name, shape, F32))

        def sem(name):
            return ctx.enter_context(nc.semaphore("m_" + name))

        GateT = sb("GateT", [P, NC, D])
        ConvW = sb("ConvW", [P, NC, CONV_K])
        Cols = sb("Cols", [P, NC + NU])
        Wcat = sb("Wcat", [P, NC, NZ])
        Comb = sb("Comb", [P, K, NC, D])
        MemO = sb("MemO", [KD, D])
        UpT = sb("UpT", [P, NC, UP])
        DownT = sb("DownT", [P, NU, D])
        Rv = sb("Rv", [P, 2 * H * BITS + K + 3 + D + 1])
        Pow = Rv[:, 0:2 * H * BITS]
        r0 = 2 * H * BITS
        DecL, GateB, DownB, Iota = Rv[:, r0:r0 + K], Rv[:, r0 + K:r0 + K + 3], Rv[:, r0 + K + 3:r0 + K + 3 + D], Rv[:, r0 + K + 3 + D:r0 + K + 4 + D]
        Id = sb("Id_", [P, P])
        Ones = sb("Ones", [P, P])
        OnesH = sb("OnesH", [P, P], F16)
        Half = sb("Half_", [P, NW])
        Dec = sb("Dec", [P, K])
        Eps = sb("Eps", [P, 2, NW])

        X = sb("X_", [P, NW, D])
        XA = sb("XA", [P, NW, D])
        XN = sb("XN", [P, NW, D])
        XNT = sb("XNT", [P, NC, PAD + T])
        Bn = sb("Bn_", [P, NW, 6])
        Mv = sb("Mv_", [P, NW, 2])
        Rd = sb("Rd_", [P, NW])
        Rr = sb("Rr", [P, NW])
        YNT = sb("YNT", [P, NC, T])
        Y = sb("Y", [P, NW, D])
        X2 = sb("X2", [P, WPG, D])
        Bn1 = sb("Bn1", [P, WPG, 6])
        Mv1 = sb("Mv1", [P, WPG, 2])
        Rd1 = sb("Rd1", [P, WPG])
        HC = sb("HC", [P, NC, T])
        UT = sb("UT", [P, NC, T])
        Z = sb("Z_", [P, NW, NZ])
        Idx = sb("Idx", [P, NW, 2 * H])
        Gt = sb("Gt", [P, 3, NW])
        Keep = sb("Keep", [P, NW])
        DG = sb("DG", [P, 2, 2 * H, P], F16)
        DO = sb("DO", [P, 2, P])
        Row = sb("Row", [P, 2 * H, T])
        KeepRow = sb("KeepRow", [P, T])
        OW = sb("OW", [P, T])
        OWP = sb("OWP", [P, H, T], F16)
        SlotC = sb("SlotC", [P, H, 2, NW])
        CellC = sb("CellC", [P, H, NW])
        KVM = sb("KVM", [P, H, NW, ASSOC, 2 * KD])
        A0 = OW
        Bits = OW[:, 0:NW * 2 * H * BITS].rearrange("p (w n) -> p w n", w=NW)
        Rdv = OW[:, 0:NW * KD].rearrange("p (w d) -> p w d", w=NW)
        D1 = sb("D1", [P, T])
        S = sb("S", [P, 1 + T])
        Par = S[:, 1:1 + T]
        W = sb("W", [P, 2, T])
        RD = HC[:].rearrange("p c t -> p (c t)").rearrange("p (w a d) -> p w a d", w=NW, d=2 * KD)
        Sc = sb("Sc", [P, NW, H * ASSOC])
        Sm = sb("Sm", [P, NW])
        At = sb("At", [P, NW, H * ASSOC])
        RVT = KeepRow[0:KD]
        SS = sb("SS", [P, K, NC, T])
        flat = SS[:].rearrange("p k c t -> p (k c t)")
        StIn = flat[:, 0:2 * K * D].rearrange("p (a n) -> p a n", n=D)
        StOut = flat[:, 2 * K * D:4 * K * D].rearrange("p (a n) -> p a n", n=D)
        PR = UT[:].rearrange("p c t -> p (c t)")[:, 0:NW * H * ASSOC * KD].rearrange("p (w a d) -> p w a d", w=NW, d=KD)
        SG = Row[:].rearrange("p a t -> p (a t)")[:, 0:NG * NC * GT].rearrange("p (i t) -> p i t", t=GT)
        Sq = SG[:, 0, 0:D]
        Hm = sb("Hm", [P, NU, GT])

        a_ps = psum("a_ps_", [P, 2, 512])
        d_ps = psum("d_ps_", [P, 2, 512])
        rd_ps = psum("rd_ps", [P, H, NW, P])

        s_c = sem("const"); s_w0 = sem("state_maps"); s_set = sem("set")
        s_x = [sem(f"x{w}") for w in range(NW)]
        a_ready, a_free, d_ready, d_free = sem("a_ready"), sem("a_free"), sem("d_ready"), sem("d_free")
        dec_done = sem("dec_done"); mv_done = sem("mv_done"); rr_done = sem("rr_done")
        xn_done = sem("xn_done"); conv_done = sem("conv_done"); silu_done = sem("silu_done"); sg_done = sem("sg_done")
        ut_done = sem("ut_done"); z_copied = sem("z_copied"); idx_done = sem("idx_done"); gt_done = sem("gt_done")
        keep_done = sem("keep_done"); dg_done = sem("dg_done"); do_done = sem("do_done")
        ss_done = sem("ss_done"); owp_done = sem("owp_done"); slotc_done = sem("slotc_done"); kvm_done = sem("kvm_done")
        w_done = sem("w_done"); w_used = sem("w_used"); rd_ready = sem("rd_ready"); rd_copied = sem("rd_copied")
        sc_done = sem("sc_done"); ex_done = sem("ex_done"); rdv_done = sem("rdv_done")
        long_done = sem("long_done"); yl_added = sem("yl_added"); y_done = sem("y_done"); ysq_done = sem("ysq_done")
        yv_done = sem("yv_done"); yr_done = sem("yr_done"); yn_done = sem("yn_done"); res_done = sem("res_done")
        x1_done = sem("x1_done"); mv1_done = sem("mv1_done"); rd1_done = sem("rd1_done"); x2_done = sem("x2_done")
        x1_st, x2_st = [sem(f"x1st{w}") for w in range(NW)], [sem(f"x2st{i}") for i in range(WPG)]
        v_chain, l_chain, p_chain, seen = sem("v_chain"), sem("l_chain"), sem("p_chain"), sem("seen")
        seen_bn = sem("seen_bn")
        biased, y_biased = sem("biased"), sem("y_biased")

        class Pass:

            def __init__(self, it, cur, prev, units, a_base, d_base):
                self.it, self.cur, self.prev = it, cur, prev
                (self.A, self.D), self.a_base, self.d_base = units, a_base, d_base

            def a(self, *key):
                return self.a_base + self.A[key]

        def passes(eng, body):
            body(Pass(0, True, False, FIRST, PRE, 0))
            with eng.Fori(1, B) as b:
                body(Pass(b, True, True, FULL, b * NAF + (PRE + NA1 - NAF), b * NDF + (ND1 - NDF)))
            body(Pass(B, False, True, LAST, B * NAF + (PRE + NA1 - NAF), B * NDF + (ND1 - NDF)))

        with nc.Block() as block:

            @block.sync
            def _(sp):
                sp.dma_start(StIn, state_in.rearrange("(a p) n -> p a n", p=P)).then_inc(s_w0, 16)
                sp.dma_start(StOut, state_out_t.rearrange("(a p) n -> p a n", p=P)).then_inc(s_w0, 16)
                for dst, src in ((Rv[:], rowsv), (Id[:], ident), (ConvW[:], conv_w), (Cols[:], cols),
                                 (GateT[:], gate_wt.rearrange("(c p) n -> p c n", p=P)),
                                 (Wcat[:], wcat.rearrange("(c p) n -> p c n", p=P)), (MemO[:], mem_out_t),
                                 (UpT[:], up_wt.rearrange("(c p) n -> p c n", p=P)),
                                 (DownT[:], down_wt.rearrange("(c p) n -> p c n", p=P))):
                    sp.dma_start(dst, src).then_inc(s_c, 16)

                def body(p):
                    if p.cur:
                        for w in range(NW):
                            sp.wait_ge(res_done, p.it * NW + (w + 1))
                            sp.dma_start(X[:, w, :], x[p.it, w * P:(w + 1) * P, :]).then_inc(s_x[w], 16)
                    if p.prev:
                        b = p.it - 1
                        for g in range(NG):
                            for w in range(g * WPG, (g + 1) * WPG):
                                sp.wait_ge(x1_done, p.it * NW + (w + 1 - NW))
                                sp.dma_start(x1[b, w * P:(w + 1) * P, :], Y[:, w, :]).then_inc(x1_st[w], 16)
                            for w in range(g * WPG, (g + 1) * WPG):
                                sp.wait_ge(x2_done, p.it * NW + (w + 1 - NW))
                                sp.dma_start(x2[b, w * P:(w + 1) * P, :], X2[:, w % WPG, :]).then_inc(x2_st[w % WPG], 16)

                for w in range(NW):
                    sp.sem_inc(x1_st[w], 16)
                for i in range(WPG):
                    sp.sem_inc(x2_st[i], 16)
                passes(sp, body)
                for w in range(NW):
                    sp.wait_ge(x1_st[w], (B + 1) * 16)
                for i in range(WPG):
                    sp.wait_ge(x2_st[i], (B * NG + 1) * 16)

            @block.tensor
            def _(pe):
                pe.wait_ge(s_w0, 32)
                for i in range(PRE):
                    k, c = divmod(i, NC)
                    pe.wait_ge(a_free, i + 1)
                    for dt in range(NC):
                        last = nc.tensor.matmul(a_ps[:, i % 2, 0:D], StIn[:, k * NC + dt, c * P:(c + 1) * P],
                                                StOut[:, k * NC + dt, :], start=(dt == 0), stop=(dt == NC - 1))
                    last.then_inc(a_ready, 1)
                pe.wait_ge(s_c, 9 * 16)
                pe.wait_ge(s_set, 8)

                def body(p):
                    def a_unit(*key):
                        pe.wait_ge(a_free, p.a(*key) + 1)
                        return a_ps[:, p.A[key] % 2, :]

                    def a_emptied(*key):
                        pe.wait_ge(a_free, p.a(*key) + 3)

                    def d_unit(*key):
                        pe.wait_ge(d_free, p.d_base + (p.D[key] + 1))
                        return d_ps[:, p.D[key] % 2, :]

                    def transposed(name, w, src, done, n):
                        pe.wait_ge(done, n)
                        bank = a_unit(name, w)
                        for c in range(NC):
                            last = nc.tensor.transpose(bank[:, c * P:(c + 1) * P], src[:, w, c * P:(c + 1) * P], Id[:])
                        last.then_inc(a_ready, 1)

                    def mlp_up(g):
                        for m in range(NU):
                            bank = a_unit("up", g, m)
                            for c in range(NC):
                                last = nc.tensor.matmul(bank, UpT[:, c, m * P:(m + 1) * P], YNT[:, c, g * GT:(g + 1) * GT],
                                                        start=(c == 0), stop=(c == NC - 1))
                            last.then_inc(a_ready, 1)

                    def mlp_down(g):
                        a_emptied("up", g, NU - 1)
                        for w in range(g * WPG, (g + 1) * WPG):
                            bank = d_unit("down", w)
                            t0 = (w % WPG) * P
                            for m in range(NU):
                                last = nc.tensor.matmul(bank[:, 0:D], Hm[:, m, t0:t0 + P], DownT[:, m, :],
                                                        start=(m == 0), stop=(m == NU - 1))
                            last.then_inc(d_ready, 1)

                    def gates(g):
                        a_emptied("xnT", (g + 1) * WPG - 1)
                        for c in range(NC):
                            bank = a_unit("gate", c, g)
                            for ci in range(NC):
                                last = nc.tensor.matmul(bank, GateT[:, ci, c * P:(c + 1) * P],
                                                        XNT[:, ci, PAD + g * GT:PAD + (g + 1) * GT],
                                                        start=(ci == 0), stop=(ci == NC - 1))
                            last.then_inc(a_ready, 1)

                    def projections():
                        pe.wait_ge(ut_done, p.it * (NG * NC) + (NG * NC + 1))
                        for i in range(NZU):
                            bank = a_unit("z", i)
                            for j, w in enumerate(z_windows(i)):
                                for c in range(NC):
                                    last = nc.tensor.matmul(bank[:, j * NZ:(j + 1) * NZ], UT[:, c, w * P:(w + 1) * P],
                                                            Wcat[:, c, :], start=(c == 0), stop=(c == NC - 1))
                            last.then_inc(a_ready, 1)

                    def rows_of_buckets():
                        for w in range(NW):
                            pe.wait_ge(dg_done, p.it * NW + (w + 1))
                            nc.tensor.matmul(a_unit("rows", w), OnesH[:], DG[:, w % 2].rearrange("p a t -> p (a t)"),
                                             start=True, stop=True).then_inc(a_ready, 1)

                    def rows_kept():
                        for g in range(NG):
                            bank = a_unit("keep", g)
                            for i in range(WPG):
                                w = g * WPG + i
                                pe.wait_ge(do_done, p.it * NW + (w + 1))
                                nc.tensor.matmul(bank[:, i * P:(i + 1) * P], Ones[:], DO[:, w % 2, :],
                                                 start=True, stop=True).then_inc(a_ready if i == WPG - 1 else seen, 1)

                    def slots(h):
                        pe.wait_ge(owp_done, p.it * H + (h + 1))
                        for g in range(NG):
                            nc.tensor.matmul(d_unit("slot_row", h, g), OnesH[:], OWP[:, h, g * GT:(g + 1) * GT],
                                             start=True, stop=True).then_inc(d_ready, 1)
                        bank = d_unit("slot_col", h)
                        for w in range(NW):
                            last = nc.tensor.matmul(bank[:, w:w + 1], OWP[:, h, w * P:(w + 1) * P], OnesH[:, 0:1],
                                                    start=True, stop=True)
                        last.then_inc(d_ready, 1)

                    def long(w):
                        bank = a_unit("long", w)
                        for i in range(K * NC):
                            k, c = divmod(i, NC)
                            last = nc.tensor.matmul(bank[:, 0:D], SS[:, k, c, w * P:(w + 1) * P], Comb[:, k, c, :],
                                                    start=(i == 0), stop=(i == K * NC - 1))
                        last.then_inc(a_ready, 1)

                    def memory_read(h, i):
                        pe.wait_ge(w_done, p.it * (H * NW) + (h * NW + i + 1))
                        for w in range(i, NW):
                            last = nc.tensor.matmul(rd_ps[:, h, w, :], W[:, i % 2, (w - i) * P:(w - i + 1) * P],
                                                    KVM[:, h, i].rearrange("p a d -> p (a d)"),
                                                    start=(i == 0 and w % 4 == 0), stop=(i == w), skip_group_check=True)
                        last.then_inc(w_used, 1)

                    if p.prev:
                        mlp_up(0)
                    if p.cur:
                        for w in range(NW):
                            transposed("xnT", w, XN, xn_done, p.it * NW + (w + 1))
                        for g in range(NG):
                            gates(g)
                    if p.prev:
                        mlp_down(0)
                    if p.cur:
                        projections()
                    if p.prev:
                        mlp_up(1)
                    if p.cur:
                        rows_of_buckets()
                        rows_kept()
                    if p.prev:
                        mlp_down(1)
                    if not p.cur:
                        return
                    for h in range(H):
                        slots(h)
                    pe.wait_ge(ss_done, p.it * (K * NC) + K * NC)
                    for h in range(H):
                        pe.wait_ge(kvm_done, p.it * (H * ASSOC) + (h + 1) * ASSOC)
                        pe.wait_ge(rd_copied, p.it * H + (h + 1))
                        for i in range(NW):
                            memory_read(h, i)
                            if (h, i) in LONG_AFTER:
                                long(LONG_AFTER[h, i])
                        pe.wait_ge(w_used, p.it * (H * NW) + (h + 1) * NW)
                        pe.sem_inc(rd_ready, 1)
                    for w in LONG_LAST:
                        long(w)
                    pe.wait_ge(rdv_done, p.it + 1)
                    for g in range(NG):
                        bank = a_unit("rvT", g)
                        for i in range(WPG):
                            last = nc.tensor.transpose(bank[0:KD, i * P:(i + 1) * P], Rdv[:, g * WPG + i, :], Id[:])
                        last.then_inc(a_ready, 1)
                    for w in range(NW):
                        bank = d_unit("mem", w)
                        if w % WPG == 0:
                            a_emptied("rvT", w // WPG)
                        nc.tensor.matmul(bank[:, 0:D], RVT[:, w * P:(w + 1) * P], MemO[:], start=True, stop=True).then_inc(d_ready, 1)
                    for w in range(NW):
                        transposed("ynT", w, XN, yn_done, p.it * NW + (w + 1))

                passes(pe, body)

            @block.scalar
            def _(act):
                act.sem_inc(a_free, 2)
                act.sem_inc(rd_copied, 1)
                for i in range(PRE):
                    k, c = divmod(i, NC)
                    act.wait_ge(a_ready, i + 1)
                    nc.scalar.activation(Comb[:, k, c, :], a_ps[:, i % 2, 0:D], ACT.Copy).then_inc(a_free, 1)
                act.wait_ge(s_c, 9 * 16)
                act.wait_ge(s_set, 8)
                nc.scalar.activation(Dec[:], DecL, ACT.Sigmoid).then_inc(dec_done, 1)

                def body(p):
                    def a_full(*key):
                        act.wait_ge(a_ready, p.a(*key) + 1)
                        return a_ps[:, p.A[key] % 2, :]

                    def evacuate(dst, bank, func=ACT.Copy, **kw):
                        return nc.scalar.activation(dst, bank, func, **kw).then_inc(a_free, 1)

                    def mlp_hidden(g):
                        if g:
                            act.wait_ge(d_ready, p.d_base + (p.D["down", g * WPG - 1] + 1))
                        for m in range(NU):
                            evacuate(Hm[:, m, :], a_full("up", g, m), ACT.Silu, bias=Cols[:, NC + m:NC + m + 1])

                    def long(w):
                        evacuate(XN[:, w, :], a_full("long", w)[:, 0:D], ACT.Copy, scale=Gt[:, 1, w:w + 1])

                    if p.prev:
                        mlp_hidden(0)
                    if p.cur:
                        for w in range(NW):
                            evacuate(XNT[:, :, PAD + w * P:PAD + (w + 1) * P],
                                     a_full("xnT", w)[:, 0:D].rearrange("p (c t) -> p c t", c=NC))
                        if p.prev:
                            act.wait_ge(w_done, p.it * (H * NW))
                        for g in range(NG):
                            for c in range(NC):
                                i = g * NC + c
                                evacuate(SG[:, i, :], a_full("gate", c, g), ACT.Sigmoid, bias=Cols[:, c:c + 1])
                                act.wait_ge(a_free, p.a("gate", c, g) + 3)
                                act.sem_inc(sg_done, 1)
                        for g in range(NG):
                            for c in range(NC):
                                toks = slice(g * GT, (g + 1) * GT)
                                act.wait_ge(conv_done, p.it * NC + NC)
                                nc.scalar.activation(UT[:, c, toks], HC[:, c, toks], ACT.Silu).then_inc(silu_done, 1)
                        for i in range(NZU):
                            ws = z_windows(i)
                            evacuate(Z[:, ws[0]:ws[-1] + 1, :],
                                     a_full("z", i)[:, 0:len(ws) * NZ].rearrange("p (w n) -> p w n", n=NZ))
                        act.wait_ge(a_free, p.a("z", NZU - 1) + 3)
                        act.sem_inc(z_copied, 1)
                        for j in range(3):
                            nc.scalar.activation(Gt[:, j, :], Z[:, :, ZG + j], ACT.Sigmoid, bias=GateB[:, j:j + 1]).then_inc(gt_done, 1)
                    if p.prev:
                        mlp_hidden(1)
                    if not p.cur:
                        return
                    for w in range(NW):
                        evacuate(Row[:, :, w * P:(w + 1) * P], a_full("rows", w).rearrange("p (a t) -> p a t", t=P))
                    for g in range(NG):
                        evacuate(KeepRow[:, g * GT:(g + 1) * GT], a_full("keep", g))
                    act.wait_ge(gt_done, p.it * 3 + 3)
                    for h in range(H):
                        for i in range(NW):
                            if (h, i) in LONG_AFTER:
                                long(LONG_AFTER[h, i])
                        act.wait_ge(rd_ready, p.it * H + (h + 1))
                        nc.scalar.activation(RD[:, :, h * ASSOC:(h + 1) * ASSOC, :],
                                             rd_ps[:, h].rearrange("p w (a d) -> p w a d", a=ASSOC), ACT.Copy).then_inc(rd_copied, 1)
                    for w in LONG_LAST:
                        long(w)
                        if w == LONG_LAST[0]:
                            act.wait_ge(sc_done, p.it + 1)
                            nc.scalar.activation(At[:], Sc[:], ACT.Exp, scale=SCALE).then_inc(ex_done, 1)
                    for g in range(NG):
                        evacuate(RVT[:, g * GT:(g + 1) * GT], a_full("rvT", g)[0:KD, :])
                    for w in range(NW):
                        act.wait_ge(y_done, p.it * NW + (w + 1))
                        nc.scalar.activation(Sq, XA[:, w, :], ACT.Square, accum_out=Rr[:, w:w + 1]).then_inc(ysq_done, 1)
                        act.wait_ge(ysq_done, p.it * NW + (w + 1))
                    for w in range(NW):
                        evacuate(YNT[:, :, w * P:(w + 1) * P],
                                 a_full("ynT", w)[:, 0:D].rearrange("p (c t) -> p c t", c=NC))

                passes(act, body)

            @block.gpsimd
            def _(pool):
                nc.gpsimd.memset(Half[:], -0.5).then_inc(s_set, 1)
                nc.gpsimd.memset(XNT[:, :, 0:PAD], 0.0).then_inc(s_set, 1)
                nc.gpsimd.memset(D1[:], 0.0).then_inc(s_set, 1)
                nc.gpsimd.memset(S[:, 0:1], 0.0).then_inc(s_set, 1)
                nc.gpsimd.memset(Ones[:], 1.0).then_inc(s_set, 1)
                nc.gpsimd.memset(OnesH[:], 1.0).then_inc(s_set, 1)
                nc.gpsimd.memset(Eps[:, 0, :], LN_EPS).then_inc(s_set, 1)
                nc.gpsimd.memset(Eps[:, 1, :], RMS_EPS).then_inc(s_set, 1)
                pool.sem_inc(res_done, NW)
                pool.wait_ge(s_set, 8)
                pool.wait_ge(s_c, 9 * 16)

                def body(p):
                    steps = [0]

                    def written(ins):
                        steps[0] += 1
                        ins.then_inc(p_chain, 1)
                        pool.wait_ge(p_chain, p.it * AP_STEPS + steps[0])

                    def rsqrt_var1(g):
                        pool.wait_ge(mv1_done, p.it * NG + (g + 1 - NG))
                        nc.gpsimd.tensor_tensor(Rd1[:], Rd1[:], Half[:, 0:WPG], ALU.pow).then_inc(rd1_done, 1)

                    if p.cur:
                        pool.wait_ge(mv_done, p.it + 1)
                        var = Mv[:, :, 1]
                        written(nc.gpsimd.tensor_tensor(Rr[:], var, Eps[:, 0, :], ALU.add))
                        written(nc.gpsimd.tensor_tensor(Rd[:], Rr[:], Half[:], ALU.pow))
                        written(nc.gpsimd.tensor_tensor(Rr[:], Rd[:], Rd[:], ALU.mult))
                        written(nc.gpsimd.tensor_tensor(Rr[:], Rr[:], var, ALU.mult))
                        written(nc.gpsimd.tensor_tensor(Rr[:], Rr[:], Eps[:, 1, :], ALU.add))
                        nc.gpsimd.tensor_tensor(Rr[:], Rr[:], Half[:], ALU.pow).then_inc(rr_done, 1)
                    if p.prev:
                        rsqrt_var1(0)
                    if p.cur:
                        pool.wait_ge(idx_done, p.it + 1)
                        for w in range(NW):
                            if w >= 2:
                                pool.wait_ge(a_ready, p.a("rows", w - 2) + 1)
                            nc.gpsimd.tensor_tensor(DG[:, w % 2], bcast(Id[:], 0, 2 * H), bcast(Idx[:, w, :], 1, P),
                                                    ALU.mult).then_inc(dg_done, 1)
                        pool.wait_ge(keep_done, p.it + 1)
                        for w in range(NW):
                            if w >= 2:
                                g, i = divmod(w - 2, WPG)
                                if i == WPG - 1:
                                    pool.wait_ge(a_ready, p.a("keep", g) + 1)
                                else:
                                    pool.wait_ge(seen, p.it * (NG * (WPG - 1)) + (g * (WPG - 1) + i + 1))
                            nc.gpsimd.tensor_tensor(DO[:, w % 2, :], Id[:], bcast1(Keep[:, w:w + 1], P), ALU.mult).then_inc(do_done, 1)
                        for h in range(H):
                            pool.wait_ge(slotc_done, p.it * H + (h + 1))
                            for a in range(ASSOC):
                                nc.gpsimd.tensor_tensor(KVM[:, h, :, a, :], Z[:, :, ZK:ZK + 2 * KD], bcast(SlotC[:, h, a, :], 1, 2 * KD),
                                                        ALU.mult).then_inc(kvm_done, 1)
                    if p.prev:
                        rsqrt_var1(1)
                    if not p.cur:
                        return
                    for w in range(NW):
                        pool.wait_ge(a_free, p.a("long", w) + 3)
                        nc.gpsimd.tensor_tensor(XA[:, w, :], XA[:, w, :], XN[:, w, :], ALU.add).then_inc(yl_added, 1)
                    for g in range(NG):
                        ws = slice(g * WPG, (g + 1) * WPG)
                        pool.wait_ge(yv_done, p.it * NG + (g + 1))
                        nc.gpsimd.tensor_tensor(Rd[:, ws], Rd[:, ws], Half[:, ws], ALU.pow).then_inc(yr_done, 1)
                    if p.prev:
                        pool.wait_ge(x2_done, p.it * NW)
                    for w in range(NW):
                        pool.wait_ge(y_done, p.it * NW + (w + 1))
                        pool.wait_ge(x1_st[w], p.it * 16 + 16)
                        nc.gpsimd.tensor_tensor(Y[:, w, :], XA[:, w, :], X[:, w, :], ALU.add).then_inc(res_done, 1)
                        pool.wait_ge(res_done, p.it * NW + (NW + w + 1))
                        nc.gpsimd.tensor_tensor(Y[:, w, :], Y[:, w, :], DownB, ALU.add).then_inc(y_biased, 1)
                    assert steps[0] == AP_STEPS, steps[0]

                passes(pool, body)

            @block.vector
            def _(dve):
                dve.sem_inc(d_free, 2)
                dve.sem_inc(ut_done, 1)
                dve.wait_ge(s_c, 9 * 16)
                dve.wait_ge(s_set, 8)
                dve.wait_ge(dec_done, 1)
                dve.wait_ge(a_free, PRE + 2)

                def body(p):
                    steps, lag_steps = [0], [0]

                    def written(ins):
                        steps[0] += 1
                        ins.then_inc(v_chain, 1)
                        dve.wait_ge(v_chain, p.it * AV_STEPS + steps[0])

                    def lag_written(ins):
                        lag_steps[0] += 1
                        ins.then_inc(l_chain, 1)
                        dve.wait_ge(l_chain, p.it * LV_STEPS + (lag_steps[0] - LV_STEPS))

                    def d_full(*key):
                        dve.wait_ge(d_ready, p.d_base + (p.D[key] + 1))
                        return d_ps[:, p.D[key] % 2, :]

                    def d_written(*key):
                        dve.wait_ge(d_free, p.d_base + (p.D[key] + 3))

                    def a_emptied(*key):
                        dve.wait_ge(a_free, p.a(*key) + 3)

                    def x1_finished(w):
                        bank = d_full("down", w)
                        dve.wait_ge(y_biased, p.it * NW + (w + 1 - NW))
                        nc.vector.tensor_tensor(Y[:, w, :], bank[:, 0:D], Y[:, w, :], ALU.add).then_inc(d_free, 1)
                        d_written("down", w)
                        dve.sem_inc(x1_done, 1)

                    def x1_normalised(g):
                        for i in range(WPG):
                            last = nc.vector.bn_stats(Bn1[:, i, :], Y[:, g * WPG + i, :])
                        lag_written(last)
                        dve.sem_inc(seen_bn, 1)
                        for i in range(WPG):
                            last = nc.vector.bn_aggr(Mv1[:, i, :], Bn1[:, i, :])
                        lag_written(last)
                        nc.vector.tensor_scalar(Rd1[:], Mv1[:, :, 1], LN_EPS, None, ALU.add).then_inc(mv1_done, 1)
                        dve.wait_ge(rd1_done, p.it * NG + (g + 1 - NG))
                        for i in range(WPG):
                            dve.wait_ge(x2_st[i], p.it * (NG * 16) + (g + 1 - NG) * 16)
                            nc.vector.tensor_scalar(X2[:, i, :], Y[:, g * WPG + i, :], Mv1[:, i, 0:1], Rd1[:, i:i + 1],
                                                    ALU.subtract, ALU.mult).then_inc(x2_done, 1)

                    if p.cur:
                        for w in range(NW):
                            dve.wait_ge(s_x[w], p.it * 16 + 16)
                            last = nc.vector.bn_stats(Bn[:, w, :], X[:, w, :])
                        written(last)
                        dve.sem_inc(seen_bn, 1)
                        for w in range(NW):
                            last = nc.vector.bn_aggr(Mv[:, w, :], Bn[:, w, :])
                        last.then_inc(mv_done, 1)
                        dve.wait_ge(rr_done, p.it + 1)
                        for w in range(NW):
                            last = nc.vector.tensor_scalar(XA[:, w, :], X[:, w, :], Mv[:, w, 0:1], Rd[:, w:w + 1], ALU.subtract, ALU.mult)
                            if w == NW - 1:
                                written(last)
                        dve.wait_ge(a_free, p.a_base + 2)
                        for w in range(NW):
                            nc.vector.tensor_scalar(XN[:, w, :], XA[:, w, :], Rr[:, w:w + 1], None, ALU.mult).then_inc(xn_done, 1)
                        a_emptied("xnT", NW - 1)
                        for j in range(CONV_K):
                            for c in range(NC):
                                src = XNT[:, c, j:j + T]
                                if j == 0:
                                    last = nc.vector.tensor_scalar(HC[:, c, :], src, ConvW[:, c, 0:1], None, ALU.mult)
                                else:
                                    last = nc.vector.scalar_tensor_tensor(HC[:, c, :], src, ConvW[:, c, j:j + 1], HC[:, c, :], ALU.mult, ALU.add)
                                if j == CONV_K - 1:
                                    last.then_inc(conv_done, 1)
                                else:
                                    written(last)
                        for g in range(NG):
                            for c in range(NC):
                                i = g * NC + c
                                toks = slice(g * GT, (g + 1) * GT)
                                dve.wait_ge(silu_done, p.it * (NG * NC) + (i + 1))
                                dve.wait_ge(sg_done, p.it * (NG * NC) + (i + 1))
                                nc.vector.tensor_tensor(UT[:, c, toks], UT[:, c, toks], SG[:, i, :], ALU.mult).then_inc(ut_done, 1)
                    if p.prev:
                        for w in range(WPG):
                            x1_finished(w)
                    if p.cur:
                        dve.wait_ge(z_copied, p.it + 1)
                        written(nc.vector.scalar_tensor_tensor(Bits, Z[:, :, 0:2 * H * BITS], 0.0, bcast(Pow, 0, NW), ALU.is_gt, ALU.mult))
                        written(nc.vector.reduce_sum(Idx[:].rearrange("p w a -> p (w a)"), Bits.rearrange("p w (a n) -> p (w a) n", n=BITS), AX))
                        nc.vector.tensor_scalar(Idx[:, :, 0:H], Idx[:, :, 0:H], float(BUCKETS - 1), None, ALU.min).then_inc(idx_done, 1)
                        dve.wait_ge(gt_done, p.it * 3 + 3)
                        nc.vector.tensor_scalar(Keep[:], Gt[:, 0, :], -1.0, 1.0, ALU.mult, ALU.add).then_inc(keep_done, 1)
                        dve.wait_ge(ut_done, p.it * (NG * NC) + (NG * NC) + 1)
                        for k in range(K):
                            for c in range(NC):
                                nc.vector.tensor_tensor_scan(SS[:, k, c, :], bcast1(Dec[:, k:k + 1], T), UT[:, c, :], 0.0,
                                                             ALU.mult, ALU.add).then_inc(ss_done, 1)
                    if p.prev:
                        x1_normalised(0)
                    if not p.cur:
                        for w in range(WPG, NW):
                            x1_finished(w)
                        x1_normalised(1)
                        return
                    dve.wait_ge(idx_done, p.it + 1)
                    a_emptied("keep", NG - 1)
                    for h in range(H):
                        if h:
                            dve.wait_ge(owp_done, p.it * H + h)
                            if p.prev:
                                x1_finished(WPG)
                        written(nc.vector.tensor_scalar(OW[:], Row[:, H + h, :], Iota, None, ALU.is_equal))
                        written(nc.vector.tensor_tensor_scan(Par, OW[:], bcast1(S[:, 0:1], T), 0.0, ALU.not_equal, ALU.add))
                        nc.vector.tensor_tensor(OWP[:, h, :], OW[:], Par, ALU.mult).then_inc(owp_done, 1)
                    if p.prev:
                        for w in range(WPG + 1, NW):
                            x1_finished(w)
                    for h in range(H):
                        for g in range(NG):
                            row = Row[:, H + h, g * GT:(g + 1) * GT]
                            nc.vector.scalar_tensor_tensor(row, row, 2.0, d_full("slot_row", h, g), ALU.mult, ALU.add).then_inc(d_free, 1)
                        written(nc.vector.tensor_copy(SlotC[:, h, 0, :], d_full("slot_col", h)[:, 0:NW]))
                        dve.sem_inc(d_free, 1)
                        nc.vector.tensor_scalar(SlotC[:, h, 1, :], SlotC[:, h, 0, :], -1.0, 1.0, ALU.mult, ALU.add).then_inc(slotc_done, 1)
                        written(nc.vector.scalar_tensor_tensor(CellC[:, h, :], Idx[:, :, H + h], 2.0, SlotC[:, h, 0, :], ALU.mult, ALU.add))
                    d_written("slot_col", H - 1)
                    for h in range(H):
                        if h and p.prev:
                            x1_normalised(1)
                        for i in range(NW):
                            n = T - i * P
                            t0 = i * P
                            nc.vector.tensor_scalar(D1[:, 0:P], Id[:], Gt[:, 0, i:i + 1], None, ALU.mult)
                            written(nc.vector.scalar_tensor_tensor(A0[:, 0:n], Row[:, H + h, t0:T], CellC[:, h, i:i + 1], KeepRow[:, t0:T],
                                                                   ALU.not_equal, ALU.max))
                            written(nc.vector.tensor_tensor_scan(S[:, 1:1 + n], A0[:, 0:n], D1[:, 0:n], 0.0, ALU.mult, ALU.add))
                            j = h * NW + i
                            if j >= 2:
                                dve.wait_ge(w_used, p.it * (H * NW) + (j - 1))
                            written(nc.vector.scalar_tensor_tensor(W[:, i % 2, 0:n], Row[:, h, t0:T], Idx[:, i, H + h:H + h + 1], S[:, 0:n],
                                                                   ALU.is_equal, ALU.mult))
                            dve.sem_inc(w_done, 1)
                    dve.wait_ge(rd_copied, p.it * H + (H + 1))
                    written(nc.vector.tensor_tensor(PR, RD[:, :, :, 0:KD], bcast(Z[:, :, ZQ:ZQ + KD], 1, H * ASSOC), ALU.mult))
                    written(nc.vector.reduce_sum(Sc[:], PR, AX))
                    written(nc.vector.reduce_max(Sm[:], Sc[:], AX))
                    nc.vector.tensor_tensor(Sc[:], Sc[:], bcast(Sm[:], 1, H * ASSOC), ALU.subtract).then_inc(sc_done, 1)
                    dve.wait_ge(ex_done, p.it + 1)
                    written(nc.vector.reduce_sum(Sm[:], At[:], AX))
                    written(nc.vector.reciprocal(Sm[:], Sm[:]))
                    written(nc.vector.tensor_tensor(Sm[:], Sm[:], Gt[:, 2, :], ALU.mult))
                    written(nc.vector.tensor_tensor(At[:], At[:], bcast(Sm[:], 1, H * ASSOC), ALU.mult))
                    written(nc.vector.tensor_tensor(PR, RD[:, :, :, KD:2 * KD], bcast(At[:], 2, KD), ALU.mult))
                    nc.vector.reduce_sum(Rdv, PR.rearrange("p w a d -> p w d a"), AX).then_inc(rdv_done, 1)
                    for w in range(NW):
                        dve.wait_ge(yl_added, p.it * NW + (w + 1))
                        nc.vector.tensor_tensor(XA[:, w, :], d_full("mem", w)[:, 0:D], XA[:, w, :], ALU.add).then_inc(d_free, 1)
                        d_written("mem", w)
                        dve.sem_inc(y_done, 1)
                    for g in range(NG):
                        ws = slice(g * WPG, (g + 1) * WPG)
                        dve.wait_ge(ysq_done, p.it * NW + (g + 1) * WPG)
                        nc.vector.tensor_scalar(Rd[:, ws], Rr[:, ws], 1.0 / D, RMS_EPS, ALU.mult, ALU.add).then_inc(yv_done, 1)
                    for g in range(NG):
                        dve.wait_ge(yr_done, p.it * NG + (g + 1))
                        for w in range(g * WPG, (g + 1) * WPG):
                            nc.vector.tensor_scalar(XN[:, w, :], XA[:, w, :], Rd[:, w:w + 1], None, ALU.mult).then_inc(yn_done, 1)
                    assert steps[0] == AV_STEPS, steps[0]

                passes(dve, body)


def attn_arrays(inp):
    f = np.float32
    g = lambda n: inp["L0_attn_" + n]
    convw = np.ascontiguousarray(g("conv_w").reshape(NC, P, CONV_K).transpose(1, 0, 2))
    cols = np.concatenate([g("gate_b").reshape(NC, P).T, g("mlp_up_b").reshape(NU, P).T], 1)
    wcat = np.concatenate([g("read_bits_w"), g("write_bits_w"), g("qkey_w"), g("wkey_w"), g("value_w"),
                           g("write_gate_w"), g("gate_long_w"), g("gate_mem_w")], 0).T
    pw = np.tile(2.0 ** np.arange(BITS), 2 * H).astype(f)
    row = np.concatenate([pw, g("state_decay_logit"), g("write_gate_b"), g("gate_long_b"), g("gate_mem_b"), g("mlp_down_b")])
    rv = np.concatenate([np.broadcast_to(row[None], (P, row.size)), np.arange(P, dtype=f)[:, None]], 1)
    return {"gate_wt": g("gate_w").T, "conv_w": convw, "cols": cols, "wcat": wcat, "state_in": g("state_in_w"),
            "state_out_t": g("state_out_w").T, "mem_out_t": g("mem_out_w").T, "up_wt": g("mlp_up_w").T,
            "down_wt": g("mlp_down_w").T, "rowsv": rv}


def build(nc, d, x1, x2, y0, out):
    build_attn(nc, d["x"], x1, x2, *(d[n] for n in ATTN_NAMES), d["ident"])
    build_ffn(nc, x2, x1, y0, out, *(d[n] for n in FFN_NAMES))


ATTN_NAMES = ("gate_wt", "conv_w", "cols", "wcat", "state_in", "state_out_t", "mem_out_t", "up_wt", "down_wt", "rowsv")
FFN_NAMES = ("wqkv", "wo", "w1", "w2", "pvec", "qs2", "b2", "tabc", "tabs", "ident", "maskd")


def kernel(**inputs):
    import numpy as _np
    import concourse.bacc as _bacc
    from concourse.bass_utils import run_bass_kernel_spmd as _run

    inp = {k: _np.asarray(v) for k, v in inputs.items()}
    arrays = {**attn_arrays(inp), **ffn_arrays(inp), "x": inp["L0_attn_x"]}
    arrays = {k: _np.ascontiguousarray(v) for k, v in arrays.items()}
    nc = _bacc.Bacc("TRN2", target_bir_lowering=False, num_devices=1)
    d = {k: nc.dram_tensor(k, v.shape, F32, kind="ExternalInput").ap() for k, v in arrays.items()}
    scratch = [nc.dram_tensor(n, (B, T, D), F32, kind="Internal").ap() for n in ("x1", "x2", "y0")]
    out = nc.dram_tensor("out", (B, T, D), F32, kind="ExternalOutput").ap()
    build(nc, d, *scratch, out)
    r = _run(nc, [arrays], core_ids=[0])
    return r.results[0]["out"]
```

```python
from contextlib import ExitStack
from itertools import chain

import numpy as np

import concourse.bass as bass
from concourse import mybir

F32 = mybir.dt.float32
F32R = mybir.dt.float32r
ALU = mybir.AluOpType
ACT = mybir.ActivationFunctionType
AX = mybir.AxisListType.X

P = 128
B, T, D = 4, 1024, 256
NW = T // P
NC = D // P
DEPTH, HEADS, DH = 2, 8, 64
INNER = HEADS * DH
NHP = HEADS // 2
HID = int(D * 4 * 2 / 3)
NM = -(-HID // P)
QK_SCALE = 8.0
LN_EPS = 1e-5
MASKED = -1e30
GT = 512
WPG = GT // P
NG = T // GT


OUT_LAG = 2
NORM_LAG = 3
MLP_STEPS = {0: (1, -NW), 1: (2, -NW), 2: (3, -NW), 3: (0, -WPG), 4: (1, -WPG), 5: (2, -WPG), 6: (3, -WPG), 7: (0, 0)}
NONE = range(0)
MLP_WORK = {(0, 0): (range(2, WPG), NONE, NONE, NONE), (0, 1): (NONE, range(NM), NONE, NONE),
            (1, 0): (NONE, NONE, range(0, 2), NONE), (1, 1): (NONE, NONE, range(2, 4), NONE),
            (2, 0): (NONE, NONE, range(4, NM), NONE), (2, 1): (NONE, NONE, NONE, range(0, 1)),
            (3, 0): (range(WPG, WPG + 2), NONE, NONE, range(1, 3)), (3, 1): (NONE, NONE, NONE, range(3, WPG))}


def rows(m):
    return min(P, HID - m * P)


def head_of(unit, i):
    return 4 * (unit // 2) + 2 * i + unit % 2


def bcast(ap, at, n):
    names = [f"d{i}" for i in range(len(ap.shape) - 1)]
    out = names[:at] + ["o"] + names[at:]
    src = names[:at] + [f"(o {names[at]})"] + names[at + 1:] if at < len(names) else names[:-1] + [f"({names[-1]} o)"]
    r = ap.rearrange(f"p {' '.join(src)} -> p {' '.join(out)}", o=1)
    shape = list(r.shape)
    shape[at + 1] = n
    return r.to_broadcast(shape)


def ahead(s):
    return s + 2 < NW


RING_A, RING_D = 3, 2
HIGH_LOW = [(0, 0), (0, 1), (1, 0)]


def mlp_units(step, half, has):
    quarter, w0 = MLP_STEPS[step]
    turned, gates, ups, downs = MLP_WORK[quarter, half]
    units = [("A", "zT", w0 + i) for i in turned if has(w0 + i)]
    if not has(w0):
        return units
    return (units + [("A", "gate", w0, m) for m in gates]
            + [("D", "up", w0, m) for m in ups] + [("D", "down", w0 + i) for i in downs])


def ffn_units(prev, cur):
    def has(w):
        return cur if w >= 0 else prev

    order = []
    if cur:
        order += [("A", "xT", 0), ("A", "xT", 1)]
    if prev:
        order.append(("A", "oT", -OUT_LAG))
    if cur:
        order.append(("A", "v", 0))
    if prev:
        order.append(("D", "wo", -OUT_LAG))
        order += [("A", "pT", -1, u) for u in range(NHP)]
    if cur:
        order.append(("A", "v", 1))
    if prev:
        order += mlp_units(0, 0, has)
    for s in range(NW):
        if cur:
            order += [("A", "qT", s), ("A", "kT", s)]
        if ahead(s):
            order += mlp_units(s, 0 if s else 1, has)
        if cur and ahead(s):
            order.append(("A", "xT", s + 2))
        if s and has(s - OUT_LAG):
            order.append(("A", "oT", s - OUT_LAG))
        if cur:
            order += [("D", "sim", s, 0), ("D", "sim", s, 1)]
        if not ahead(s):
            order += mlp_units(s, 0, has)
        if cur:
            order += [("D", "sim", s, 2), ("D", "sim", s, 3)]
        if s and has(s - OUT_LAG):
            order.append(("D", "wo", s - OUT_LAG))
        if s and cur:
            order += [("A", "pT", s - 1, u) for u in range(NHP)]
        if cur and ahead(s):
            order.append(("A", "v", s + 2))
        if s:
            order += mlp_units(s, 1, has)
    if cur:
        order += [("A", "end", i) for i in range(-sum(unit[0] == "A" for unit in order) % RING_A)]
    index = {"A": {}, "D": {}}
    for ring, *key in order:
        index[ring][tuple(key)] = len(index[ring])
    return index["A"], index["D"]


def build_ffn(nc, x2, x1, y0, out, wqkv, wo, w1, w2, pvec, qs2, b2, tabc, tabs, ident, maskd):
    FIRST, FULL, LAST = ffn_units(False, True), ffn_units(True, True), ffn_units(True, False)
    with ExitStack() as ctx:
        def sb(name, shape, dt=F32):
            return ctx.enter_context(nc.sbuf_tensor(name, shape, dt))

        def psum(name, shape):
            return ctx.enter_context(nc.psum_tensor(name, shape, F32))

        def sem(name):
            return ctx.enter_context(nc.semaphore(name))

        Wqkv = [sb(f"Wqkv{i}", [P, NC, 3 * INNER], F32R) for i in range(2)]
        W1 = [sb(f"W1{i}", [P, NC, 2 * HID], F32R) for i in range(2)]
        Stage = sb("Stage", [P, NC * 3 * INNER])
        Wo = [sb(f"Wo{i}", [P, NHP, D]) for i in range(DEPTH)]
        W2 = [sb(f"W2{i}", [P, NM, D]) for i in range(DEPTH)]
        Pv = sb("Pv", [P, DEPTH, 2 * NM + 2 * NC])
        Qs = sb("Qs", [P, DEPTH, 2, 2, DH])
        B2 = sb("B2", [P, DEPTH, D])
        Cs = sb("Cs", [P, NW, 2, DH])
        Ss = sb("Ss", [P, NW, 2, DH])
        Id = sb("Id", [P, P])
        Mk = sb("Mk", [P, 2, P])
        Half = sb("Half", [P, 2 * HEADS])
        Zero = sb("Zero", [P, 1])
        Warm, End = sb("Warm", [P, 1]), sb("End", [P, RING_A])
        X = sb("X", [P, NW, D])
        XM = sb("XM", [P, NW, D])
        X1 = sb("X1", [P, 2, D])
        XS = sb("XS", [P, NW, P])
        XTf = sb("XTf", [P, 2, NC, P])
        XT = [sb(f"XT{i}", [P, NC, 2 * P + 1], F32R) for i in range(2)]
        QKr = sb("QKr", [P, 2, 2, HEADS, DH])
        T2 = sb("T2", [P, 2, HEADS, DH])
        Sq = sb("Sq", [P, 2 * HEADS, DH])
        Ssum = sb("Ssum", [P, 2 * HEADS])
        Rn = sb("Rn", [P, 2 * HEADS])
        V = sb("V", [P, 4, INNER])
        KT = sb("KT", [P, 2, NHP, P])
        QT = sb("QT", [P, NHP, P])
        SM = sb("SM", [P, 2, NHP, 2, 2, P])
        Nb = sb("Nb", [P, 2, HEADS])
        Rs = sb("Rs", [P, 2, HEADS])
        Ri = sb("Ri", [P, 2, HEADS])
        PT = sb("PT", [P, NHP, 2, 2, P])
        On = sb("On", [P, HEADS, DH])
        OT = sb("OT", [P, NHP, P])
        Bn = sb("Bn", [P, 2, 6])
        Mv = sb("Mv", [P, NW, 2])
        Ve = sb("Ve", [P, NW])
        Rd = sb("Rd", [P, NW])
        Z = sb("Z", [P, NW, D])
        ZTf = sb("ZTf", [P, 2, NC, P])
        ZT = [sb(f"ZT{i}", [P, NC, GT], F32R) for i in range(2)]
        HT = sb("HT", [P, NM, GT])

        qk_ps = psum("qk_ps", [P, 2, 512])
        a_ps = psum("a_ps", [P, RING_A, 512])
        d_ps = psum("d_ps", [P, RING_D, 512])
        o_ps = psum("o_ps", [P, 512])

        s_wt = sem("wt")
        staged, split_hi, split = sem("staged"), sem("split_hi"), sem("split")
        x_edge = sem("x_edge")
        x_low, z_low = sem("x_low"), sem("z_low")
        s_tab = sem("tab")
        s_cst = sem("cst")
        s_set = sem("set")
        s_x = [sem(f"x_in{w}") for w in range(NW)]
        s_x1 = [sem(f"x1_in{i}") for i in range(2)]
        s_sh = [sem(f"shift{w}") for w in range(NW)]
        s_st = [sem(f"stored{w}") for w in range(NW)]
        a_ready, a_free = sem("a_ready"), sem("a_free")
        d_ready, d_free = sem("d_ready"), sem("d_free")
        qk_ready, qk_read = sem("qk_ready"), sem("qk_read")
        sq_done, sums_done, ssum_done = sem("sq_done"), sem("sums_done"), sem("ssum_done")
        rot_terms, rn_done, qkr_sum, qk_rot = sem("rot_terms"), sem("rn_done"), sem("qkr_sum"), sem("qk_rot")
        tabs_done = sem("tabs_done")
        exp_done, warmed = sem("exp_done"), sem("warmed")
        sim_seen, fin_seen, bn_seen = sem("sim_seen"), sem("fin_seen"), sem("bn_seen")
        recip_done, o_ready, o_norm = sem("recip_done"), sem("o_ready"), sem("o_norm")
        xmid = sem("xmid")
        bn_done, mv_done, ve_done, rd_done, z_done = (sem("bn_done"), sem("mv_done"), sem("ve_done"), sem("rd_done"),
                                                      sem("z_done"))
        x1_added, b2_added = sem("x1_added"), sem("b2_added")
        gelu_done, ht_done, fin_done = sem("gelu_done"), sem("ht_done"), sem("fin_done")

        stages = [(x2, y0), (y0, out)]

        class Pass:

            def __init__(self, it, b, layer, b_prev, layer_prev, units, a_base, d_base):
                self.it, self.b, self.layer, self.b_prev, self.layer_prev = it, b, layer, b_prev, layer_prev
                (self.A, self.D), self.a_base, self.d_base = units, a_base, d_base
                self.kind = (FIRST, FULL, LAST).index(units)

            def has(self, w):
                return (self.layer if w >= 0 else self.layer_prev) is not None

            def present(self, windows):
                return [w for w in windows if self.has(w)]

            def layer_of(self, w):
                return self.layer if w >= 0 else self.layer_prev

            def prev_empty(self):
                return self.layer_prev is None

            def first_of_layer(self):
                return self.layer is not None and self.layer != self.layer_prev

            def seq_of(self, w):
                return self.b if w >= 0 else self.b_prev

            def win(self, w, n=1):
                return self.it * (NW * n) + w * n

        NA1, ND1 = len(FIRST[0]), len(FIRST[1])
        NAF, NDF = len(FULL[0]), len(FULL[1])
        ends = [sum(key[0] == "end" for key in units[0]) for units in (FIRST, FULL, LAST)]
        assert NA1 % RING_A == NAF % RING_A == ND1 % RING_D == NDF % RING_D == 0

        def passes(eng, body):
            body(Pass(0, 0, 0, None, None, FIRST, 0, 0))
            for layer in range(DEPTH):
                if layer:
                    n = layer * B - 1
                    body(Pass(layer * B, 0, layer, B - 1, layer - 1, FULL, NA1 + n * NAF, ND1 + n * NDF))
                n = layer * B - 1
                with eng.Fori(1, B) as b:
                    body(Pass(b + layer * B, b, layer, b - 1, layer, FULL, b * NAF + (NA1 + n * NAF), b * NDF + (ND1 + n * NDF)))
            n = DEPTH * B - 1
            body(Pass(DEPTH * B, None, None, B - 1, DEPTH - 1, LAST, NA1 + n * NAF, ND1 + n * NDF))

        with nc.Block() as block:

            @block.sync
            def _(sp):
                sp.dma_start(Stage[:].rearrange("p (c n) -> p c n", c=NC), wqkv[0].rearrange("(c p) n -> p c n", p=P)).then_inc(staged, 16)
                for dst, src in ((Id[:], ident), (Mk[:], maskd),
                                 (Pv[:], pvec), (Qs[:], qs2), (B2[:], b2)):
                    sp.dma_start(dst, src).then_inc(s_cst, 16)

                def body(p):
                    def load_x(w):
                        if p.layer_prev is not None:
                            sp.wait_ge(xmid, p.win(w - NW) + 1)
                        sp.dma_start(X[:, w, :], stages[p.layer][0][p.b, w * P:(w + 1) * P, :]).then_inc(s_x[w], 16)

                    def store(w):
                        sp.wait_ge(fin_done, p.win(w) + 1)
                        sp.sem_inc(fin_seen, 1)
                        v = w % NW
                        sp.dma_start(stages[p.layer_of(w)][1][p.seq_of(w), v * P:(v + 1) * P, :], Z[:, v, :]).then_inc(s_st[v], 16)

                    if p.has(0):
                        for w in range(NW - OUT_LAG):
                            load_x(w)
                    if p.first_of_layer():
                        if p.layer:
                            sp.wait_ge(rot_terms, p.win(0))
                        for dst, src in ((Cs, tabc), (Ss, tabs)):
                            sp.dma_start(dst[:], src.rearrange("(w p) a d -> p w a d", p=P)).then_inc(s_tab, 16)
                    if p.prev_empty():
                        for i in range(DEPTH):
                            sp.dma_start(Wo[i][:], wo[i].rearrange("(c p) n -> p c n", p=P)).then_inc(s_wt, 16)
                            full = (NM - 1) * P
                            sp.dma_start(W2[i][:, 0:NM - 1, :], w2[i, 0:full].rearrange("(c p) n -> p c n", p=P)).then_inc(s_wt, 16)
                            sp.dma_start(W2[i][0:HID - full, NM - 1, :], w2[i, full:HID]).then_inc(s_wt, 16)
                    for s in range(NW):
                        quarter, w0 = MLP_STEPS[(s - 1) % NW]
                        if s and p.has(w0):
                            for i in chain(MLP_WORK[quarter, 0][3], MLP_WORK[quarter, 1][3]):
                                store(w0 + i)
                        w = s - OUT_LAG
                        if p.has(w):
                            v = w % NW
                            sp.wait_ge(xmid, p.win(w) + 1)
                            sp.dma_start(XS[1:P, v, :], XM[0:P - 1, v, P:D]).then_inc(s_sh[v], 16)
                            if v + 1 < NW:
                                sp.dma_start(XS[0:1, v + 1, :], XM[P - 1:P, v, P:D]).then_inc(s_sh[v + 1], 16)
                        if s < OUT_LAG and p.has(0):
                            load_x(NW - OUT_LAG + s)
                        quarter, w0 = MLP_STEPS[s]
                        if quarter < 2 and p.has(w0) and p.layer_of(w0) == DEPTH - 1:
                            for w in range(w0 + 2 * quarter, w0 + 2 * quarter + 2):
                                if p.layer_prev == DEPTH - 1 or w > 1:
                                    sp.wait_ge(x1_added, p.win(w) - 1 - (DEPTH - 1) * B * NW)
                                t0 = w % NW * P
                                sp.dma_start(X1[:, w % 2, :], x1[p.seq_of(w0), t0:t0 + P, :]).then_inc(s_x1[w % 2], 16)

                passes(sp, body)
                for w in range(NW):
                    sp.wait_ge(s_st[w], (DEPTH * B + 1) * 16)

            @block.tensor
            def _(pe):
                pe.wait_ge(s_cst, 5 * 16)
                pe.wait_ge(s_set, 3)

                def body(p):
                    def a_unit(*key):
                        pe.wait_ge(a_free, p.a_base + (p.A[key] + 1))
                        return a_ps[:, p.A[key] % RING_A, :]

                    def a_emptied(*key):
                        pe.wait_ge(a_free, p.a_base + (p.A[key] + 1 + RING_A))

                    def d_unit(*key):
                        pe.wait_ge(d_free, p.d_base + (p.D[key] + 1))
                        return d_ps[:, p.D[key] % RING_D, :]

                    def transposes(bank, srcs):
                        for i, src in enumerate(srcs):
                            last = nc.tensor.transpose(bank[:, i * P:(i + 1) * P], src, Id[:])
                        return last

                    def x_transposed(w):
                        pe.wait_ge(s_x[w], p.it * 16 + 16)
                        transposes(a_unit("xT", w), [X[:, w, c * P:(c + 1) * P] for c in range(NC)]).then_inc(a_ready, 1)

                    def project(w, part, bank):
                        t0 = w % 2 * P
                        lhs = [[x[:, 0, 1 + t0:1 + t0 + P], x[:, 1, t0:t0 + P]] for x in XT]
                        for c in range(NC):
                            for x, y in HIGH_LOW:
                                last = nc.tensor.matmul(bank, lhs[x][c], Wqkv[y][:, c, part * INNER:(part + 1) * INNER],
                                                        start=(c == 0 and (x, y) == HIGH_LOW[0]),
                                                        stop=(c == NC - 1 and (x, y) == HIGH_LOW[-1]))
                        return last

                    def project_qk(w):
                        pe.wait_ge(x_low, p.win(w) + 1)
                        pe.wait_ge(qk_read, p.win(w) + 1)
                        project(w, 0, qk_ps[:, 0, :])
                        project(w, 1, qk_ps[:, 1, :]).then_inc(qk_ready, 1)

                    def project_v(w):
                        project(w, 2, a_unit("v", w)).then_inc(a_ready, 1)

                    def qk_transposed(w):
                        pe.wait_ge(qk_rot, p.win(w) + 2)
                        for a, name in enumerate(("qT", "kT")):
                            srcs = [QKr[:, w % 2, a, 2 * i:2 * i + 2, :].rearrange("p h d -> p (h d)") for i in range(NHP)]
                            transposes(a_unit(name, w), srcs).then_inc(a_ready, 1)

                    def scores(w, a):
                        banks = [d_unit("sim", w, 2 * a + r) for r in range(2)]
                        if a == 0:
                            a_emptied("kT", w)
                        own = [(i, blk) for i in range(2) for blk in range(2) if w or blk]
                        for i, blk in own:
                            for r in range(2):
                                half = slice(r * DH, (r + 1) * DH)
                                mm = nc.tensor.matmul(banks[r][:, (2 * i + blk) * P:(2 * i + blk + 1) * P],
                                                      QT[half, 2 * a + i, :], KT[half, (w - 1 + blk) % 2, 2 * a + i, :],
                                                      start=True, stop=True)
                                if (i, blk) == own[-1]:
                                    mm.then_inc(d_ready, 1)

                    def blocks(w):
                        return (0, 1) if w % NW else (1,)

                    def probs_transposed(w, u):
                        pe.wait_ge(exp_done, p.win(w, NHP) + u + 1)
                        bank = a_unit("pT", w, u)
                        for i in range(2):
                            for blk in blocks(w):
                                j = 2 * i + blk
                                last = nc.tensor.transpose(bank[:, j * P:(j + 1) * P], SM[:, w % 2, u, i, blk, :], Id[:])
                        last.then_inc(a_ready, 1)

                    def attend(w, u):
                        if u == 0:
                            pe.wait_ge(o_norm, p.win(w) + 1)
                        a_emptied("pT", w, u)
                        for i in range(2):
                            head = head_of(u, i)
                            cols = slice(head * DH, (head + 1) * DH)
                            for blk in blocks(w):
                                last = nc.tensor.matmul(o_ps[:, cols], PT[:, u, i, blk, :], V[:, (w - 1 + blk) % 4, cols],
                                                        start=(blk == blocks(w)[0]), stop=(blk == 1))
                        if u == NHP - 1:
                            last.then_inc(o_ready, 1)

                    def attention(w, w_out=None):
                        for u in range(RING_A):
                            probs_transposed(w, u)
                        if w_out is not None:
                            project_out(w_out)
                        for u in range(NHP):
                            if u and u + RING_A - 1 < NHP:
                                probs_transposed(w, u + RING_A - 1)
                            attend(w, u)

                    def out_transposed(w):
                        pe.wait_ge(o_norm, p.win(w) + 2)
                        srcs = [On[:, 2 * i:2 * i + 2, :].rearrange("p h d -> p (h d)") for i in range(NHP)]
                        transposes(a_unit("oT", w), srcs).then_inc(a_ready, 1)

                    def project_out(w):
                        bank = d_unit("wo", w)
                        a_emptied("oT", w)
                        for i in range(NHP):
                            last = nc.tensor.matmul(bank[:, 0:D], OT[:, i, :], Wo[p.layer_of(w)][:, i, :],
                                                    start=(i == 0), stop=(i == NHP - 1))
                        last.then_inc(d_ready, 1)

                    def hidden(ring, name, w0, m, first, ready):
                        n = rows(m)
                        bank = ring(name, w0, m)
                        for c in range(NC):
                            for x, y in HIGH_LOW:
                                last = nc.tensor.matmul(bank[0:n, :], W1[y][:, c, first:first + n], ZT[x][:, c, :],
                                                        start=(c == 0 and (x, y) == HIGH_LOW[0]),
                                                        stop=(c == NC - 1 and (x, y) == HIGH_LOW[-1]))
                        last.then_inc(ready, 1)

                    def down(w, w0):
                        bank = d_unit("down", w)
                        pe.wait_ge(ht_done, p.it * (NG * NM) + (w0 // WPG + 1) * NM)
                        t0 = (w - w0) * P
                        for m in range(NM):
                            n = rows(m)
                            last = nc.tensor.matmul(bank[:, 0:D], HT[0:n, m, t0:t0 + P], W2[p.layer_of(w)][0:n, m, :],
                                                    start=(m == 0), stop=(m == NM - 1))
                        last.then_inc(d_ready, 1)

                    def feed_forward(step, half):
                        quarter, w0 = MLP_STEPS[step]
                        turned, gates, ups, downs = MLP_WORK[quarter, half]
                        for w in p.present(w0 + i for i in turned):
                            pe.wait_ge(z_done, p.win(w) + 1)
                            transposes(a_unit("zT", w), [Z[:, w % NW, c * P:(c + 1) * P] for c in range(NC)]).then_inc(a_ready, 1)
                        if not p.has(w0):
                            return
                        for m in gates:
                            if m == 0:
                                pe.wait_ge(z_low, p.win(w0 + WPG) + 2)
                            hidden(a_unit, "gate", w0, m, HID + m * P, a_ready)
                        for m in ups:
                            hidden(d_unit, "up", w0, m, m * P, d_ready)
                        for i in downs:
                            down(w0 + i, w0)

                    if p.has(0):
                        x_transposed(0)
                        x_transposed(1)
                    if p.has(-OUT_LAG):
                        out_transposed(-OUT_LAG)
                    if p.has(0):
                        if p.first_of_layer():
                            pe.wait_ge(split, 2 * p.layer + 1)
                        project_qk(0)
                        project_v(0)
                    if p.has(-OUT_LAG):
                        attention(-1, -OUT_LAG)
                    if p.has(0):
                        project_qk(1)
                        project_v(1)
                    feed_forward(0, 0)
                    if p.prev_empty():
                        pe.wait_ge(s_wt, DEPTH * 3 * 16)
                    for s in range(NW):
                        if s == NW - 1 and p.first_of_layer():
                            pe.wait_ge(split, 2 * p.layer + 2)
                        if p.has(0):
                            qk_transposed(s)
                        if ahead(s):
                            feed_forward(s, 0 if s else 1)
                        if p.has(0) and ahead(s):
                            x_transposed(s + 2)
                        if s and p.has(s - OUT_LAG):
                            out_transposed(s - OUT_LAG)
                        if p.has(0):
                            scores(s, 0)
                        if not ahead(s):
                            feed_forward(s, 0)
                        if p.has(0) and ahead(s):
                            project_qk(s + 2)
                        if p.has(0):
                            scores(s, 1)
                        if s and p.has(0):
                            attention(s - 1, s - OUT_LAG if p.has(s - OUT_LAG) else None)
                        elif s and p.has(s - OUT_LAG):
                            project_out(s - OUT_LAG)
                        if p.has(0) and ahead(s):
                            project_v(s + 2)
                        if s:
                            feed_forward(s, 1)
                    for i in range(ends[p.kind]):
                        transposes(a_unit("end", i), [Id[:]]).then_inc(a_ready, 1)

                passes(pe, body)

            @block.scalar
            def _(act):
                act.sem_inc(a_free, RING_A)
                for w in range(NW):
                    act.sem_inc(s_st[w], 16)
                act.wait_ge(s_cst, 5 * 16)
                act.wait_ge(s_set, 3)

                def body(p):
                    def a_full(*key):
                        act.wait_ge(a_ready, p.a_base + (p.A[key] + 1))
                        return a_ps[:, p.A[key] % RING_A, :]

                    def evacuate(dst, bank):
                        nc.scalar.activation(dst, bank, ACT.Copy).then_inc(a_free, 1)

                    def x_evacuated(w):
                        bank = a_full("xT", w)[:, 0:D].rearrange("p (c t) -> p c t", c=NC)
                        t0 = 1 + w % 2 * P
                        nc.scalar.activation(XT[0][:, :, t0:t0 + P], bank, ACT.Copy)
                        evacuate(XTf[:, w % 2], bank)

                    def squares(w):
                        act.wait_ge(qk_ready, p.win(w) + 1)
                        act.wait_ge(ssum_done, p.win(w) + 1)
                        nc.scalar.activation(Sq[:], qk_ps[:].rearrange("p a (h d) -> p (a h) d", d=DH),
                                             ACT.Square).then_inc(sq_done, 1)

                    def v_copy(w):
                        evacuate(V[:, w % 4, :], a_full("v", w))

                    def exponentials(w, u):
                        act.wait_ge(d_free, p.d_base + (p.D["sim", w, u] + 1 + RING_D))
                        for i in range(2):
                            head = head_of(u, i)
                            s = SM[:, w % 2, u, i, :, :] if w else SM[:, w % 2, u, i, 1:2, :]
                            last = nc.scalar.activation(s, s, ACT.Exp, bias=Nb[:, w % 2, 2 * u + i:2 * u + i + 1], scale=-1.0,
                                                        accum_out=Rs[:, w % 2, head:head + 1])
                        last.then_inc(exp_done, 1)

                    def probs_evacuated(w, u):
                        bank = a_full("pT", w, u).rearrange("p (h k t) -> p h k t", h=2, k=2)
                        k = slice(0, 2) if w % NW else slice(1, 2)
                        evacuate(PT[:, u, :, k, :], bank[:, :, k, :])

                    def out_evacuated(w):
                        evacuate(OT[:], a_full("oT", w).rearrange("p (a t) -> p a t", a=NHP))

                    def feed_forward(step, half):
                        quarter, w0 = MLP_STEPS[step]
                        turned, gates, _, _ = MLP_WORK[quarter, half]
                        for w in p.present(w0 + i for i in turned):
                            bank = a_full("zT", w)
                            layer, t0 = p.layer_of(w), w % WPG * P
                            act.wait_ge(z_low, p.win(w) + 1)
                            for c in range(NC):
                                g = 2 * NM + c
                                for dst in (ZT[0][:, c, t0:t0 + P], ZTf[:, w % 2, c, :]):
                                    last = nc.scalar.activation(dst, bank[:, c * P:(c + 1) * P], ACT.Identity,
                                                                scale=Pv[:, layer, g:g + 1], bias=Pv[:, layer, g + NC:g + NC + 1])
                            last.then_inc(a_free, 1)
                        if not p.has(w0):
                            return
                        layer = p.layer_of(w0)
                        if gates:
                            nc.scalar.activation(Warm[:], Zero[:], ACT.Gelu).then_inc(warmed, 1)
                        for m in gates:
                            n = rows(m)
                            nc.scalar.activation(HT[0:n, m, :], a_full("gate", w0, m)[0:n, :], ACT.Gelu,
                                                 bias=Pv[0:n, layer, NM + m:NM + m + 1]).then_inc(a_free, 1)
                            if m == NM - 1:
                                act.wait_ge(a_free, p.a_base + (p.A["gate", w0, m] + 1 + RING_A))
                                act.sem_inc(gelu_done, 1)

                    if p.has(0):
                        x_evacuated(0)
                        x_evacuated(1)
                    if p.has(-OUT_LAG):
                        out_evacuated(-OUT_LAG)
                    if p.has(0):
                        squares(0)
                        v_copy(0)
                    if p.has(-1):
                        for u in range(NHP):
                            probs_evacuated(-1, u)
                    if p.has(0):
                        squares(1)
                        v_copy(1)
                    feed_forward(0, 0)
                    for s in range(NW):
                        if p.has(0):
                            for name, dst in (("qT", QT[:]), ("kT", KT[:, s % 2])):
                                evacuate(dst, a_full(name, s).rearrange("p (a t) -> p a t", a=NHP))
                        if ahead(s):
                            feed_forward(s, 0 if s else 1)
                        if p.has(0) and ahead(s):
                            x_evacuated(s + 2)
                        if s and p.has(s - OUT_LAG):
                            out_evacuated(s - OUT_LAG)
                        if not ahead(s):
                            feed_forward(s, 0)
                        if p.has(0):
                            exponentials(s, 0)
                            exponentials(s, 1)
                        if p.has(0) and ahead(s):
                            squares(s + 2)
                        lag = s and p.has(0)
                        for u in range(NHP):
                            if lag:
                                probs_evacuated(s - 1, u)
                            if p.has(0) and u % 2:
                                exponentials(s, 2 + u // 2)
                        if p.has(0) and ahead(s):
                            v_copy(s + 2)
                        if p.first_of_layer() and s == 2:
                            act.wait_ge(split, 2 * p.layer + 1)
                            act.dma_start(Stage[:, 0:NC * 2 * HID].rearrange("p (c n) -> p c n", c=NC),
                                          w1[p.layer].rearrange("(c p) n -> p c n", p=P)).then_inc(staged, 16)
                        if s:
                            feed_forward(s, 1)
                    for i in range(ends[p.kind]):
                        evacuate(End[:, i:i + 1], a_full("end", i)[:, 0:1])
                    if p.first_of_layer() and p.layer + 1 < DEPTH:
                        act.wait_ge(split, 2 * p.layer + 2)
                        act.dma_start(Stage[:].rearrange("p (c n) -> p c n", c=NC),
                                      wqkv[p.layer + 1].rearrange("(c p) n -> p c n", p=P)).then_inc(staged, 16)

                passes(act, body)

            @block.gpsimd
            def _(pool):
                nc.gpsimd.memset(Half[:], -0.5).then_inc(s_set, 1)
                nc.gpsimd.memset(Zero[:], 0.0).then_inc(s_set, 1)
                nc.gpsimd.memset(XS[0:1, 0, :], 0.0).then_inc(s_set, 1)
                pool.sem_inc(qk_rot, 1)
                pool.wait_ge(s_set, 3)
                pool.wait_ge(s_cst, 5 * 16)

                def body(p):
                    def rotate(w):
                        pool.wait_ge(rot_terms, p.win(w) + 1)
                        q = QKr[:, w % 2].rearrange("p a h d -> p (a h) d")
                        nc.gpsimd.tensor_tensor(q, q, T2[:].rearrange("p a h d -> p (a h) d"), ALU.add).then_inc(qkr_sum, 1)
                        pool.wait_ge(ssum_done, p.win(w) + 2)
                        nc.gpsimd.tensor_tensor(Rn[:], Ssum[:], Half[:], ALU.pow).then_inc(rn_done, 1)
                        pool.wait_ge(qkr_sum, p.win(w) + 1)
                        pool.wait_ge(rn_done, p.win(w) + 1)
                        nc.gpsimd.tensor_tensor(q, q, bcast(Rn[:], 1, DH), ALU.mult).then_inc(qk_rot, 1)

                    def rsqrt_var(w):
                        v = w % NW
                        pool.wait_ge(ve_done, p.win(w) + 1)
                        nc.gpsimd.tensor_tensor(Rd[:, v:v + 1], Ve[:, v:v + 1], Half[:, 0:1], ALU.pow).then_inc(rd_done, 1)

                    def residuals(w0):
                        layer = p.layer_of(w0)
                        for w in range(w0, w0 + WPG):
                            v = w % NW
                            pool.wait_ge(z_done, p.win(w) + 1)
                            for x in (v, v + 1):
                                if x < NW:
                                    n = 32 if x else 16
                                    pool.wait_ge(s_sh[x], (p.it + (1 if w >= 0 else 0)) * n)
                            if layer == DEPTH - 1:
                                i = w % 2
                                pool.wait_ge(s_x1[i], (p.it * (NW // 2) + (w // 2 + 1 - (DEPTH - 1) * B * NW // 2)) * 16)
                                nc.gpsimd.tensor_tensor(XM[:, v, :], XM[:, v, :], X1[:, i, :], ALU.add).then_inc(x1_added, 1)
                                pool.wait_ge(x1_added, p.win(w) + 1 - (DEPTH - 1) * B * NW)
                            nc.gpsimd.tensor_tensor(XM[:, v, :], XM[:, v, :], B2[:, layer, :], ALU.add).then_inc(b2_added, 1)

                    if p.has(0):
                        rotate(0)
                        rotate(1)
                    for s in range(NW):
                        if p.has(s - NORM_LAG):
                            rsqrt_var(s - NORM_LAG)
                        if p.has(0) and ahead(s):
                            rotate(s + 2)
                        quarter, w0 = MLP_STEPS[s]
                        if quarter == 1 and p.has(w0):
                            residuals(w0)

                passes(pool, body)

            @block.vector
            def _(dve):
                dve.sem_inc(d_free, RING_D)
                dve.sem_inc(qk_read, 1)
                dve.sem_inc(ssum_done, 1)
                dve.sem_inc(o_norm, 1)
                dve.sem_inc(z_low, 2)
                dve.wait_ge(s_cst, 5 * 16)
                dve.wait_ge(s_set, 3)
                for x in XT:
                    nc.vector.tensor_copy(x[:, 1, 0:1], Zero[:])

                def split_weights(n, parts, length):
                    dve.wait_ge(staged, (n + 1) * 16)
                    high, low = [x[:].rearrange("p c n -> p (c n)") for x in parts]
                    nc.vector.tensor_copy(high, Stage[:, 0:length]).then_inc(split_hi, 1)
                    dve.wait_ge(split_hi, n + 1)
                    nc.vector.tensor_tensor(low, Stage[:, 0:length], high, ALU.subtract).then_inc(split, 1)

                def scaled_tables(layer):
                    dve.wait_ge(s_tab, 2 * (layer + 1) * 16)
                    for swap, tab in enumerate((Cs, Ss)):
                        nc.vector.tensor_tensor(tab[:], tab[:], bcast(Qs[:, layer, swap], 0, NW), ALU.mult).then_inc(tabs_done, 1)
                    dve.wait_ge(tabs_done, 2 * (layer + 1))

                def body(p):
                    def d_full(*key):
                        dve.wait_ge(d_ready, p.d_base + (p.D[key] + 1))
                        return d_ps[:, p.D[key] % RING_D, :]

                    def d_written(*key):
                        dve.wait_ge(d_free, p.d_base + (p.D[key] + 1 + RING_D))

                    def x_low_part(w):
                        dve.wait_ge(a_free, p.a_base + (p.A["xT", w] + 1 + RING_A))
                        t0 = 1 + w % 2 * P
                        last = nc.vector.tensor_tensor(XT[1][:, :, t0:t0 + P], XTf[:, w % 2], XT[0][:, :, t0:t0 + P], ALU.subtract)
                        if w % 2 == 0:
                            last.then_inc(x_low, 1)
                            return
                        last.then_inc(x_edge, 1)
                        dve.wait_ge(x_edge, p.it * (NW // 2) + (w // 2 + 1))
                        dve.wait_ge(a_ready, p.a_base + (p.A["v", w - 1] + 1))
                        for x in XT:
                            last = nc.vector.tensor_copy(x[:, 1, 0:1], x[:, 1, 2 * P:2 * P + 1] if w < NW - 1 else Zero[:])
                        last.then_inc(x_low, 1)

                    def z_low_part(w):
                        dve.wait_ge(a_free, p.a_base + (p.A["zT", w] + 1 + RING_A))
                        t0 = w % WPG * P
                        nc.vector.tensor_tensor(ZT[1][:, :, t0:t0 + P], ZTf[:, w % 2], ZT[0][:, :, t0:t0 + P],
                                                ALU.subtract).then_inc(z_low, 1)

                    def rotary_terms(w):
                        dve.wait_ge(qk_rot, p.win(w) + 1)
                        dve.wait_ge(sq_done, p.win(w) + 1)
                        qk = qk_ps[:].rearrange("p a (h d) -> p a h d", d=DH)
                        nc.vector.tensor_tensor(QKr[:, w % 2], qk, bcast(Cs[:, w], 1, HEADS), ALU.mult)
                        lo, hi = slice(0, DH // 2), slice(DH // 2, DH)
                        nc.vector.tensor_tensor(T2[:, :, :, lo], qk[:, :, :, hi], bcast(Ss[:, w, :, lo], 1, HEADS), ALU.mult)
                        nc.vector.tensor_tensor(T2[:, :, :, hi], qk[:, :, :, lo], bcast(Ss[:, w, :, hi], 1, HEADS),
                                                ALU.mult).then_inc(rot_terms, 1)
                        dve.wait_ge(rot_terms, p.win(w) + 1)
                        dve.sem_inc(qk_read, 1)
                        nc.vector.reduce_sum(Ssum[:], Sq[:], AX).then_inc(sums_done, 1)
                        dve.wait_ge(sums_done, p.win(w) + 1)
                        nc.vector.tensor_scalar(Ssum[:], Ssum[:], 1e-24, None, ALU.max).then_inc(ssum_done, 1)

                    def mask_and_max(w, u):
                        bank = d_full("sim", w, u).rearrange("p (h k t) -> p h k t", h=2, k=2)
                        k = slice(0, 2) if w else slice(1, 2)
                        dve.sem_inc(sim_seen, 1)
                        for i in range(2):
                            last = nc.vector.tensor_tensor_reduce(SM[:, w % 2, u, i, k, :], bank[:, i, k, :], Mk[:, k, :], -QK_SCALE,
                                                                  -MASKED * 100, ALU.add, ALU.min,
                                                                  Nb[:, w % 2, 2 * u + i:2 * u + i + 1])
                        last.then_inc(d_free, 1)

                    def normalise(w):
                        dve.wait_ge(exp_done, p.win(w, NHP) + NHP)
                        nc.vector.reciprocal(Ri[:, w % 2, :], Rs[:, w % 2, :]).then_inc(recip_done, 1)
                        dve.wait_ge(recip_done, p.win(w) + 1)
                        dve.wait_ge(o_ready, p.win(w) + 1)
                        nc.vector.tensor_tensor(On[:], o_ps[:].rearrange("p (h d) -> p h d", d=DH), bcast(Ri[:, w % 2, :], 1, DH),
                                                ALU.mult).then_inc(o_norm, 1)

                    def add_attention(w):
                        v = w % NW
                        bank = d_full("wo", w)
                        nc.vector.tensor_tensor(XM[:, v, :], bank[:, 0:D], X[:, v, :], ALU.add).then_inc(d_free, 1)
                        d_written("wo", w)
                        dve.sem_inc(xmid, 1)

                    def variance(w):
                        v = w % NW
                        dve.wait_ge(s_sh[v], (p.it + (1 if w >= 0 else 0)) * (32 if v else 16))
                        nc.vector.bn_stats(Bn[:, 0, :], XM[:, v, 0:P])
                        nc.vector.bn_stats(Bn[:, 1, :], XS[:, v, :]).then_inc(bn_done, 1)
                        dve.wait_ge(bn_done, p.win(w) + 1)
                        dve.sem_inc(bn_seen, 1)
                        nc.vector.bn_aggr(Mv[:, v, :], Bn[:].rearrange("p a b -> p (a b)")).then_inc(mv_done, 1)
                        dve.wait_ge(mv_done, p.win(w) + 1)
                        nc.vector.tensor_scalar(Ve[:, v:v + 1], Mv[:, v, 1:2], LN_EPS, None, ALU.add).then_inc(ve_done, 1)

                    def layernorm(w):
                        v = w % NW
                        dve.wait_ge(rd_done, p.win(w) + 1)
                        dve.wait_ge(s_st[v], (p.it + (1 if w >= 0 else 0)) * 16)
                        nc.vector.tensor_scalar(Z[:, v, 0:P], XM[:, v, 0:P], Mv[:, v, 0:1], Rd[:, v:v + 1], ALU.subtract, ALU.mult)
                        nc.vector.tensor_scalar(Z[:, v, P:D], XS[:, v, :], Mv[:, v, 0:1], Rd[:, v:v + 1],
                                                ALU.subtract, ALU.mult).then_inc(z_done, 1)

                    def hidden_product(w0, m):
                        n = rows(m)
                        bank = d_full("up", w0, m)
                        if m == 0:
                            dve.wait_ge(gelu_done, p.it * NG + (w0 // WPG + 1))
                        nc.vector.scalar_tensor_tensor(HT[0:n, m, :], bank[0:n, :], Pv[0:n, p.layer_of(w0), m:m + 1],
                                                       HT[0:n, m, :], ALU.add, ALU.mult).then_inc(ht_done, 1)
                        dve.wait_ge(ht_done, p.it * (NG * NM) + (w0 // WPG * NM + m + 1))
                        dve.sem_inc(d_free, 1)

                    def finish(w):
                        v = w % NW
                        bank = d_full("down", w)
                        dve.wait_ge(b2_added, p.win(w) + 1)
                        nc.vector.tensor_tensor(Z[:, v, :], bank[:, 0:D], XM[:, v, :], ALU.add).then_inc(d_free, 1)
                        d_written("down", w)
                        dve.sem_inc(fin_done, 1)

                    def feed_forward(step, half):
                        quarter, w0 = MLP_STEPS[step]
                        turned, _, ups, downs = MLP_WORK[quarter, half]
                        for w in p.present(w0 + i for i in turned):
                            z_low_part(w)
                        if not p.has(w0):
                            return
                        for m in ups:
                            hidden_product(w0, m)
                        for i in downs:
                            finish(w0 + i)

                    if p.first_of_layer():
                        if p.layer:
                            dve.wait_ge(a_ready, p.a_base)
                        split_weights(2 * p.layer, Wqkv, NC * 3 * INNER)
                    if p.has(0):
                        x_low_part(0)
                        if p.first_of_layer():
                            scaled_tables(p.layer)
                        rotary_terms(0)
                        x_low_part(1)
                    if p.has(-OUT_LAG):
                        add_attention(-OUT_LAG)
                        normalise(-1)
                    if p.has(0):
                        rotary_terms(1)
                    feed_forward(0, 0)
                    for s in range(NW):
                        if ahead(s):
                            feed_forward(s, 0 if s else 1)
                            if p.has(0):
                                x_low_part(s + 2)
                        if p.first_of_layer() and s == NW - OUT_LAG:
                            split_weights(2 * p.layer + 1, W1, NC * 2 * HID)
                        if p.has(0):
                            mask_and_max(s, 0)
                            mask_and_max(s, 1)
                        if not ahead(s):
                            feed_forward(s, 0)
                        if p.has(s - NORM_LAG):
                            variance(s - NORM_LAG)
                        if p.has(0):
                            mask_and_max(s, 2)
                            mask_and_max(s, 3)
                        if p.has(s - NORM_LAG):
                            layernorm(s - NORM_LAG)
                        if p.has(0) and ahead(s):
                            rotary_terms(s + 2)
                        if s and p.has(0):
                            normalise(s - 1)
                        if s and p.has(s - OUT_LAG):
                            add_attention(s - OUT_LAG)
                        if s:
                            feed_forward(s, 1)

                passes(dve, body)


def ffn_constants():
    f = np.float32
    half = np.arange(0, DH, 2, dtype=f)
    inv = (f(1.0) / np.power(f(10000.0), half / f(DH))).astype(f)
    t = np.arange(T, dtype=f)
    fr = (t[:, None] * inv[None]).astype(f)
    fr = np.concatenate([fr, fr], -1)
    base = ((half + f(0.4 * DH)) / f(1.4 * DH)).astype(f)
    power = ((t - T // 2) / f(P // 2)).astype(f)
    sc = (base[None].astype(f) ** power[:, None]).astype(f)
    sc = np.concatenate([sc, sc], -1)
    sign = np.where(np.arange(DH) < DH // 2, f(-1), f(1))
    cos, sin = np.cos(fr), np.sin(fr) * sign
    tabc = np.stack([cos * sc, cos / sc], 1).astype(f)
    tabs = np.stack([sin * sc, sin / sc], 1).astype(f)
    i, j = np.arange(P)[:, None], np.arange(P)[None]
    mask = np.stack([np.where(j >= i, 0, MASKED), np.where(j <= i, 0, MASKED)], 1).astype(f)
    return tabc, tabs, np.eye(P, dtype=f), mask


def ffn_arrays(inp):
    f = np.float32
    b1, lg, lb = inp["L0_ffn_b1"], inp["L0_ffn_ln_g"], inp["L0_ffn_ln_b"]
    pv = np.zeros((P, DEPTH, 2 * NM + 2 * NC), f)
    for i in range(DEPTH):
        for m in range(NM):
            pv[:rows(m), i, m] = b1[i, m * P:m * P + rows(m)]
            pv[:rows(m), i, NM + m] = b1[i, HID + m * P:HID + m * P + rows(m)]
        for c in range(NC):
            pv[:, i, 2 * NM + c] = lg[i, c * P:(c + 1) * P]
            pv[:, i, 2 * NM + NC + c] = lb[i, c * P:(c + 1) * P]
    qk = np.stack([inp["L0_ffn_q_scale"], inp["L0_ffn_k_scale"]], 1)
    swapped = np.concatenate([qk[..., DH // 2:], qk[..., :DH // 2]], -1)
    qs = np.broadcast_to(np.stack([qk, swapped], 1)[None], (P, DEPTH, 2, 2, DH))
    b2 = np.broadcast_to(inp["L0_ffn_b2"][None], (P, DEPTH, D))
    tabc, tabs, ident, mask = ffn_constants()
    return {"wqkv": inp["L0_ffn_wqkv"], "wo": inp["L0_ffn_wo"], "w1": inp["L0_ffn_w1"], "w2": inp["L0_ffn_w2"],
            "pvec": pv, "qs2": qs, "b2": b2, "tabc": tabc, "tabs": tabs, "ident": ident, "maskd": mask}



F16 = mybir.dt.float16
K = 4
H, BITS, BUCKETS, ASSOC = 2, 9, 128, 2
KD = 32
CONV_K = 4
UP = 4 * D
NU = UP // P
ZQ = 2 * H * BITS
ZK = ZQ + KD
ZG = ZK + 2 * KD
NZ = ZG + 3
RMS_EPS = 1e-6
SCALE = float(np.float32(1.0 / np.sqrt(KD)))
PAD = CONV_K - 1
Z_PER_BANK = 2


def bcast1(ap, n):
    return ap.to_broadcast([P, n])


def z_windows(i):
    return range(i * Z_PER_BANK, min((i + 1) * Z_PER_BANK, NW))


N_Z_UNITS = -(-NW // Z_PER_BANK)


LONG_AFTER = {(0, 0): 0, (0, 2): 1, (0, 5): 2, (0, 7): 3, (1, 0): 4, (1, 3): 5}
LONG_LAST = range(6, NW)
UP_FIRST = range(0, NU // 2)
DOWN_FIRST, DOWN_AFTER_KEEP, DOWN_LAST = range(1), [range(WPG, WPG + 1), range(WPG + 1, WPG + 2)], range(WPG + 2, NW)
ROWS_BEFORE = {m: range((m - NU // 2) * 2, (m - NU // 2) * 2 + 2) for m in range(NU // 2, NU)}


def attn_units(prev, cur):
    order = []
    if prev:
        order += [("A", "up", 0, m) for m in range(NU)]
        order += [("D", "down", w) for w in DOWN_FIRST]
    if cur:
        order += [("A", "xnT", w) for w in range(NW)]
        order += [("A", "gate", c, h) for h in range(NG) for c in range(NC)]
    if prev:
        order += [("D", "down", w) for w in range(DOWN_FIRST.stop, WPG)]
    if cur:
        order += [("A", "z", i) for i in range(N_Z_UNITS)]
    if prev:
        order += [("A", "up", 1, m) for m in UP_FIRST]
    for m, windows in ROWS_BEFORE.items():
        if cur:
            order += [("A", "rows", w) for w in windows]
        if prev:
            order.append(("A", "up", 1, m))
    for g in range(NG):
        if cur:
            order.append(("A", "keep", g))
        if prev:
            order += [("D", "down", w) for w in DOWN_AFTER_KEEP[g]]
    if cur:
        for h in range(H):
            order += [("D", "slot_row", h, g) for g in range(NG)] + [("D", "slot_col", h)]
    if prev:
        order += [("D", "down", w) for w in DOWN_LAST]
    if cur:
        order += [("A", "long", w) for w in range(NW)]
        order += [("A", "rvT", g) for g in range(NG)]
        order += [("D", "mem", w) for w in range(NW)]
        order += [("A", "ynT", w) for w in range(NW)]
    index = {"A": {}, "D": {}}
    for ring, *key in order:
        index[ring][tuple(key)] = len(index[ring])
    return index["A"], index["D"]


V_OWN_RESULTS = 1 + 1 + (CONV_K - 1) * NC + 2 + 2 * H + 2 * H + 3 * H * NW + 8
V_OWN_STATISTICS = NG
P_OWN_RESULTS = 5


def build_attn(nc, x, x1, x2, gate_wt, conv_w, cols, wcat, state_in, state_out_t, mem_out_t, up_wt, down_wt, rowsv, ident):
    FIRST, FULL, LAST = attn_units(False, True), attn_units(True, True), attn_units(True, False)
    NA1, ND1, NAF, NDF = len(FIRST[0]), len(FIRST[1]), len(FULL[0]), len(FULL[1])
    assert NA1 % 2 == ND1 % 2 == NAF % 2 == NDF % 2 == 0
    PRE = 2 * K
    with ExitStack() as ctx:
        def sb(name, shape, dt=F32):
            return ctx.enter_context(nc.sbuf_tensor(name, shape, dt))

        def psum(name, shape):
            return ctx.enter_context(nc.psum_tensor(name, shape, F32))

        def sem(name):
            return ctx.enter_context(nc.semaphore("m_" + name))

        GateT = sb("GateT", [P, NC, D])
        ConvW = sb("ConvW", [P, NC, CONV_K])
        Cols = sb("Cols", [P, NC + NU])
        Wcat = sb("Wcat", [P, NC, NZ])
        Comb = sb("Comb", [P, K, NC, D])
        MemO = sb("MemO", [KD, D])
        UpT = sb("UpT", [P, NC, UP])
        DownT = sb("DownT", [P, NU, D])
        Rv = sb("Rv", [P, 2 * H * BITS + K + 3 + D + 1])
        Pow = Rv[:, 0:2 * H * BITS]
        r0 = 2 * H * BITS
        DecL, GateB = Rv[:, r0:r0 + K], Rv[:, r0 + K:r0 + K + 3]
        r0 += K + 3
        DownB, Iota = Rv[:, r0:r0 + D], Rv[:, r0 + D:r0 + D + 1]
        Id = sb("Id_", [P, P])
        Ones = sb("Ones", [P, P])
        OnesH = sb("OnesH", [P, P], F16)
        Half = sb("Half_", [P, NW])
        Dec = sb("Dec", [P, K])
        Eps = sb("Eps", [P, 2, NW])

        X = sb("X_", [P, NW, D])
        XA = sb("XA", [P, NW, D])
        XN = sb("XN", [P, NW, D])
        XNT = sb("XNT", [P, NC, PAD + T])
        Bn = sb("Bn_", [P, NW, 6])
        Mv = sb("Mv_", [P, NW, 2])
        Rd = sb("Rd_", [P, NW])
        Rr = sb("Rr", [P, NW])
        YNT = sb("YNT", [P, NC, T])
        Y = sb("Y", [P, NW, D])
        X2 = sb("X2", [P, WPG, D])
        Bn1 = sb("Bn1", [P, WPG, 6])
        Mv1 = sb("Mv1", [P, WPG, 2])
        Rd1 = sb("Rd1", [P, WPG])
        HC = sb("HC", [P, NC, T])
        UT = sb("UT", [P, NC, T])
        Z = sb("Z_", [P, NW, NZ])
        Idx = sb("Idx", [P, NW, 2 * H])
        Gt = sb("Gt", [P, 3, NW])
        Keep = sb("Keep", [P, NW])
        DG = sb("DG", [P, 2, 2 * H, P], F16)
        DO = sb("DO", [P, 2, P])
        Row = sb("Row", [P, 2 * H, T])
        KeepRow = sb("KeepRow", [P, T])
        OW = sb("OW", [P, T])
        OWP = sb("OWP", [P, H, T], F16)
        SlotC = sb("SlotC", [P, H, 2, NW])
        CellC = sb("CellC", [P, H, NW])
        KVM = sb("KVM", [P, H, NW, ASSOC, 2 * KD])
        A0 = OW
        Bits = OW[:, 0:NW * 2 * H * BITS].rearrange("p (w n) -> p w n", w=NW)
        Rdv = OW[:, 0:NW * KD].rearrange("p (w d) -> p w d", w=NW)
        D1 = sb("D1", [P, T])
        S = sb("S", [P, 1 + T])
        Par = S[:, 1:1 + T]
        W = sb("W", [P, 2, T])
        RD = HC[:].rearrange("p c t -> p (c t)").rearrange("p (w a d) -> p w a d", w=NW, d=2 * KD)
        Sc = sb("Sc", [P, NW, H * ASSOC])
        Sm = sb("Sm", [P, NW])
        At = sb("At", [P, NW, H * ASSOC])
        RVT = KeepRow[0:KD]
        SS = sb("SS", [P, K, NC, T])
        flat = SS[:].rearrange("p k c t -> p (k c t)")
        StIn = flat[:, 0:2 * K * D].rearrange("p (a n) -> p a n", n=D)
        StOut = flat[:, 2 * K * D:4 * K * D].rearrange("p (a n) -> p a n", n=D)
        PR = UT[:].rearrange("p c t -> p (c t)")[:, 0:NW * H * ASSOC * KD].rearrange("p (w a d) -> p w a d", w=NW, d=KD)
        SG = Row[:].rearrange("p a t -> p (a t)")[:, 0:NG * NC * GT].rearrange("p (i t) -> p i t", t=GT)
        Sq = SG[:, 0, 0:D]
        Hm = sb("Hm", [P, NU, GT])

        a_ps = psum("a_ps_", [P, 2, 512])
        d_ps = psum("d_ps_", [P, 2, 512])
        rd_ps = psum("rd_ps", [P, H, NW, P])

        s_c, s_w0, s_w = sem("const"), sem("state_maps"), sem("weights")
        s_set = sem("set")
        s_x = [sem(f"x{w}") for w in range(NW)]
        x1_st = [sem(f"x1st{w}") for w in range(NW)]
        x2_st = [sem(f"x2st{i}") for i in range(WPG)]
        a_ready, a_free, d_ready, d_free = sem("a_ready"), sem("a_free"), sem("d_ready"), sem("d_free")
        dec_done = sem("dec_done")
        mv_done, rr_done, xn_done = sem("mv_done"), sem("rr_done"), sem("xn_done")
        conv_done, silu_done, sg_done, ut_done = sem("conv_done"), sem("silu_done"), sem("sg_done"), sem("ut_done")
        z_copied, idx_done, gt_done, keep_done = sem("z_copied"), sem("idx_done"), sem("gt_done"), sem("keep_done")
        dg_done, do_done = sem("dg_done"), sem("do_done")
        do_used = sem("do_used")
        ss_done, owp_done, slotc_done, kvm_done = sem("ss_done"), sem("owp_done"), sem("slotc_done"), sem("kvm_done")
        w_done, w_used, rd_ready, rd_copied = sem("w_done"), sem("w_used"), sem("rd_ready"), sem("rd_copied")
        sc_done, ex_done, rdv_done = sem("sc_done"), sem("ex_done"), sem("rdv_done")
        yl_added, y_done, ysq_done, yv_done = sem("yl_added"), sem("y_done"), sem("ysq_done"), sem("yv_done")
        yr_done, yn_done = sem("yr_done"), sem("yn_done")
        res_done, y_biased = sem("res_done"), sem("y_biased")
        x1_done, bn1_done, mv1_done, rd1_done, x2_done = (sem("x1_done"), sem("bn1_done"), sem("mv1_done"), sem("rd1_done"),
                                                          sem("x2_done"))
        v_own_result, v_own_statistics, p_own_result = sem("v_own_result"), sem("v_own_statistics"), sem("p_own_result")
        bn_taken = sem("bn_taken")

        class Pass:

            def __init__(self, it, cur, prev, units, a_base, d_base):
                self.it, self.cur, self.prev = it, cur, prev
                (self.A, self.D), self.a_base, self.d_base = units, a_base, d_base

            def a(self, *key):
                return self.a_base + self.A[key]

        def passes(eng, body):
            body(Pass(0, True, False, FIRST, PRE, 0))
            with eng.Fori(1, B) as b:
                body(Pass(b, True, True, FULL, b * NAF + (PRE + NA1 - NAF), b * NDF + (ND1 - NDF)))
            body(Pass(B, False, True, LAST, B * NAF + (PRE + NA1 - NAF), B * NDF + (ND1 - NDF)))

        with nc.Block() as block:

            @block.sync
            def _(sp):
                sp.dma_start(StIn, state_in.rearrange("(a p) n -> p a n", p=P)).then_inc(s_w0, 16)
                sp.dma_start(StOut, state_out_t.rearrange("(a p) n -> p a n", p=P)).then_inc(s_w0, 16)
                for dst, src in ((Rv[:], rowsv), (Id[:], ident), (ConvW[:], conv_w), (Cols[:], cols)):
                    sp.dma_start(dst, src).then_inc(s_c, 16)

                def body(p):
                    if p.cur:
                        for w in range(NW):
                            sp.wait_ge(res_done, p.it * NW + (w + 1))
                            sp.dma_start(X[:, w, :], x[p.it, w * P:(w + 1) * P, :]).then_inc(s_x[w], 16)
                    if not p.prev:
                        for dst, src in ((GateT[:], gate_wt.rearrange("(c p) n -> p c n", p=P)),
                                         (Wcat[:], wcat.rearrange("(c p) n -> p c n", p=P)), (MemO[:], mem_out_t),
                                         (UpT[:], up_wt.rearrange("(c p) n -> p c n", p=P)),
                                         (DownT[:], down_wt.rearrange("(c p) n -> p c n", p=P))):
                            sp.dma_start(dst, src).then_inc(s_w, 16)
                    if p.prev:
                        b = p.it - 1
                        for g in range(NG):
                            for w in range(g * WPG, (g + 1) * WPG):
                                sp.wait_ge(x1_done, p.it * NW + (w + 1 - NW))
                                sp.dma_start(x1[b, w * P:(w + 1) * P, :], Y[:, w, :]).then_inc(x1_st[w], 16)
                            for w in range(g * WPG, (g + 1) * WPG):
                                sp.wait_ge(x2_done, p.it * NW + (w + 1 - NW))
                                sp.dma_start(x2[b, w * P:(w + 1) * P, :], X2[:, w % WPG, :]).then_inc(x2_st[w % WPG], 16)

                for w in range(NW):
                    sp.sem_inc(x1_st[w], 16)
                for i in range(WPG):
                    sp.sem_inc(x2_st[i], 16)
                passes(sp, body)
                for w in range(NW):
                    sp.wait_ge(x1_st[w], (B + 1) * 16)
                for i in range(WPG):
                    sp.wait_ge(x2_st[i], (B * NG + 1) * 16)

            @block.tensor
            def _(pe):
                pe.wait_ge(s_w0, 32)
                for i in range(PRE):
                    k, c = divmod(i, NC)
                    pe.wait_ge(a_free, i + 1)
                    for dt in range(NC):
                        last = nc.tensor.matmul(a_ps[:, i % 2, 0:D], StIn[:, k * NC + dt, c * P:(c + 1) * P],
                                                StOut[:, k * NC + dt, :], start=(dt == 0), stop=(dt == NC - 1))
                    last.then_inc(a_ready, 1)
                pe.wait_ge(s_c, 4 * 16)
                pe.wait_ge(s_set, 8)

                def body(p):
                    def a_unit(*key):
                        pe.wait_ge(a_free, p.a(*key) + 1)
                        return a_ps[:, p.A[key] % 2, :]

                    def a_emptied(*key):
                        pe.wait_ge(a_free, p.a(*key) + 3)

                    def d_unit(*key):
                        pe.wait_ge(d_free, p.d_base + (p.D[key] + 1))
                        return d_ps[:, p.D[key] % 2, :]

                    def transposed(name, w, src, done, n):
                        pe.wait_ge(done, n)
                        bank = a_unit(name, w)
                        for c in range(NC):
                            last = nc.tensor.transpose(bank[:, c * P:(c + 1) * P], src[:, w, c * P:(c + 1) * P], Id[:])
                        last.then_inc(a_ready, 1)

                    def mlp_up(g, tiles=range(NU)):
                        for m in tiles:
                            bank = a_unit("up", g, m)
                            for c in range(NC):
                                last = nc.tensor.matmul(bank, UpT[:, c, m * P:(m + 1) * P], YNT[:, c, g * GT:(g + 1) * GT],
                                                        start=(c == 0), stop=(c == NC - 1))
                            last.then_inc(a_ready, 1)

                    def mlp_down(g, windows):
                        a_emptied("up", g, NU - 1)
                        for w in windows:
                            bank = d_unit("down", w)
                            t0 = (w % WPG) * P
                            for m in range(NU):
                                last = nc.tensor.matmul(bank[:, 0:D], Hm[:, m, t0:t0 + P], DownT[:, m, :],
                                                        start=(m == 0), stop=(m == NU - 1))
                            last.then_inc(d_ready, 1)

                    def gates(g):
                        a_emptied("xnT", (g + 1) * WPG - 1)
                        for c in range(NC):
                            bank = a_unit("gate", c, g)
                            for ci in range(NC):
                                last = nc.tensor.matmul(bank, GateT[:, ci, c * P:(c + 1) * P],
                                                        XNT[:, ci, PAD + g * GT:PAD + (g + 1) * GT],
                                                        start=(ci == 0), stop=(ci == NC - 1))
                            last.then_inc(a_ready, 1)

                    def projections():
                        pe.wait_ge(ut_done, p.it * (NG * NC) + NG * NC)
                        for i in range(N_Z_UNITS):
                            bank = a_unit("z", i)
                            for j, w in enumerate(z_windows(i)):
                                for c in range(NC):
                                    last = nc.tensor.matmul(bank[:, j * NZ:(j + 1) * NZ], UT[:, c, w * P:(w + 1) * P],
                                                            Wcat[:, c, :], start=(c == 0), stop=(c == NC - 1))
                            last.then_inc(a_ready, 1)

                    def rows_of_buckets(windows):
                        for w in windows:
                            pe.wait_ge(dg_done, p.it * NW + (w + 1))
                            nc.tensor.matmul(a_unit("rows", w), OnesH[:], DG[:, w % 2].rearrange("p a t -> p (a t)"),
                                             start=True, stop=True).then_inc(a_ready, 1)

                    def row_kept(g):
                        bank = a_unit("keep", g)
                        for i in range(WPG):
                            w = g * WPG + i
                            pe.wait_ge(do_done, p.it * NW + (w + 1))
                            nc.tensor.matmul(bank[:, i * P:(i + 1) * P], Ones[:], DO[:, w % 2, :],
                                             start=True, stop=True).then_inc(a_ready if i == WPG - 1 else do_used, 1)

                    def slots(h):
                        pe.wait_ge(owp_done, p.it * H + (h + 1))
                        for g in range(NG):
                            nc.tensor.matmul(d_unit("slot_row", h, g), OnesH[:], OWP[:, h, g * GT:(g + 1) * GT],
                                             start=True, stop=True).then_inc(d_ready, 1)
                        bank = d_unit("slot_col", h)
                        for w in range(NW):
                            last = nc.tensor.matmul(bank[:, w:w + 1], OWP[:, h, w * P:(w + 1) * P], OnesH[:, 0:1],
                                                    start=True, stop=True)
                        last.then_inc(d_ready, 1)

                    def long(w):
                        bank = a_unit("long", w)
                        for i in range(K * NC):
                            k, c = divmod(i, NC)
                            last = nc.tensor.matmul(bank[:, 0:D], SS[:, k, c, w * P:(w + 1) * P], Comb[:, k, c, :],
                                                    start=(i == 0), stop=(i == K * NC - 1))
                        last.then_inc(a_ready, 1)

                    def memory_read(h, i):
                        pe.wait_ge(w_done, p.it * (H * NW) + (h * NW + i + 1))
                        for w in range(i, NW):
                            last = nc.tensor.matmul(rd_ps[:, h, w, :], W[:, i % 2, (w - i) * P:(w - i + 1) * P],
                                                    KVM[:, h, i].rearrange("p a d -> p (a d)"),
                                                    start=(i == 0 and w % 4 == 0), stop=(i == w), skip_group_check=True)
                        last.then_inc(w_used, 1)

                    if p.prev:
                        mlp_up(0)
                        mlp_down(0, DOWN_FIRST)
                    if p.cur:
                        for w in range(NW):
                            transposed("xnT", w, XN, xn_done, p.it * NW + (w + 1))
                        if not p.prev:
                            pe.wait_ge(s_w, 5 * 16)
                        for g in range(NG):
                            gates(g)
                    if p.prev:
                        mlp_down(0, range(DOWN_FIRST.stop, WPG))
                    if p.cur:
                        projections()
                    if p.prev:
                        mlp_up(1, UP_FIRST)
                    for m, windows in ROWS_BEFORE.items():
                        if p.cur:
                            rows_of_buckets(windows)
                        if p.prev:
                            mlp_up(1, [m])
                    for g in range(NG):
                        if p.cur:
                            row_kept(g)
                        if p.prev:
                            mlp_down(1, DOWN_AFTER_KEEP[g])
                    if p.cur:
                        for h in range(H):
                            slots(h)
                    if p.prev:
                        mlp_down(1, DOWN_LAST)
                    if not p.cur:
                        return
                    pe.wait_ge(ss_done, p.it * (K * NC) + K * NC)
                    for h in range(H):
                        pe.wait_ge(kvm_done, p.it * (H * ASSOC) + (h + 1) * ASSOC)
                        pe.wait_ge(rd_copied, p.it * H + (h + 1))
                        for i in range(NW):
                            memory_read(h, i)
                            if (h, i) in LONG_AFTER:
                                long(LONG_AFTER[h, i])
                        pe.wait_ge(w_used, p.it * (H * NW) + (h + 1) * NW)
                        pe.sem_inc(rd_ready, 1)
                    for w in LONG_LAST:
                        long(w)
                    pe.wait_ge(rdv_done, p.it + 1)
                    for g in range(NG):
                        bank = a_unit("rvT", g)
                        for i in range(WPG):
                            last = nc.tensor.transpose(bank[0:KD, i * P:(i + 1) * P], Rdv[:, g * WPG + i, :], Id[:])
                        last.then_inc(a_ready, 1)
                    for w in range(NW):
                        bank = d_unit("mem", w)
                        if w % WPG == 0:
                            a_emptied("rvT", w // WPG)
                        nc.tensor.matmul(bank[:, 0:D], RVT[:, w * P:(w + 1) * P], MemO[:], start=True, stop=True).then_inc(d_ready, 1)
                    for w in range(NW):
                        transposed("ynT", w, XN, yn_done, p.it * NW + (w + 1))

                passes(pe, body)

            @block.scalar
            def _(act):
                act.sem_inc(a_free, 2)
                act.sem_inc(rd_copied, 1)
                for i in range(PRE):
                    k, c = divmod(i, NC)
                    act.wait_ge(a_ready, i + 1)
                    nc.scalar.activation(Comb[:, k, c, :], a_ps[:, i % 2, 0:D], ACT.Copy).then_inc(a_free, 1)
                act.wait_ge(s_c, 4 * 16)
                act.wait_ge(s_set, 8)
                nc.scalar.activation(Dec[:], DecL, ACT.Sigmoid).then_inc(dec_done, 1)

                def body(p):
                    def a_full(*key):
                        act.wait_ge(a_ready, p.a(*key) + 1)
                        return a_ps[:, p.A[key] % 2, :]

                    def evacuate(dst, bank, func=ACT.Copy, **kw):
                        return nc.scalar.activation(dst, bank, func, **kw).then_inc(a_free, 1)

                    def mlp_hidden(g, tiles=range(NU)):
                        if g and tiles[0] == 0:
                            act.wait_ge(d_ready, p.d_base + (p.D["down", g * WPG - 1] + 1))
                        for m in tiles:
                            evacuate(Hm[:, m, :], a_full("up", g, m), ACT.Silu, bias=Cols[:, NC + m:NC + m + 1])

                    def long(w):
                        evacuate(XN[:, w, :], a_full("long", w)[:, 0:D], ACT.Copy, scale=Gt[:, 1, w:w + 1])

                    if p.prev:
                        mlp_hidden(0)
                    if p.cur:
                        for w in range(NW):
                            evacuate(XNT[:, :, PAD + w * P:PAD + (w + 1) * P],
                                     a_full("xnT", w)[:, 0:D].rearrange("p (c t) -> p c t", c=NC))
                        if p.prev:
                            act.wait_ge(w_done, p.it * (H * NW))
                        for g in range(NG):
                            for c in range(NC):
                                i = g * NC + c
                                evacuate(SG[:, i, :], a_full("gate", c, g), ACT.Sigmoid, bias=Cols[:, c:c + 1])
                                act.wait_ge(a_free, p.a("gate", c, g) + 3)
                                act.sem_inc(sg_done, 1)
                        for g in range(NG):
                            for c in range(NC):
                                toks = slice(g * GT, (g + 1) * GT)
                                act.wait_ge(conv_done, p.it * NC + NC)
                                nc.scalar.activation(UT[:, c, toks], HC[:, c, toks], ACT.Silu).then_inc(silu_done, 1)
                        for i in range(N_Z_UNITS):
                            ws = z_windows(i)
                            evacuate(Z[:, ws[0]:ws[-1] + 1, :],
                                     a_full("z", i)[:, 0:len(ws) * NZ].rearrange("p (w n) -> p w n", n=NZ))
                        act.wait_ge(a_free, p.a("z", N_Z_UNITS - 1) + 3)
                        act.sem_inc(z_copied, 1)
                        for j in range(3):
                            nc.scalar.activation(Gt[:, j, :], Z[:, :, ZG + j], ACT.Sigmoid, bias=GateB[:, j:j + 1]).then_inc(gt_done, 1)
                    if p.prev:
                        mlp_hidden(1, UP_FIRST)
                    for m, windows in ROWS_BEFORE.items():
                        if p.cur:
                            for w in windows:
                                evacuate(Row[:, :, w * P:(w + 1) * P], a_full("rows", w).rearrange("p (a t) -> p a t", t=P))
                        if p.prev:
                            mlp_hidden(1, [m])
                    if not p.cur:
                        return
                    for g in range(NG):
                        evacuate(KeepRow[:, g * GT:(g + 1) * GT], a_full("keep", g))
                    act.wait_ge(gt_done, p.it * 3 + 3)
                    for h in range(H):
                        for i in range(NW):
                            if (h, i) in LONG_AFTER:
                                long(LONG_AFTER[h, i])
                        act.wait_ge(rd_ready, p.it * H + (h + 1))
                        nc.scalar.activation(RD[:, :, h * ASSOC:(h + 1) * ASSOC, :],
                                             rd_ps[:, h].rearrange("p w (a d) -> p w a d", a=ASSOC), ACT.Copy).then_inc(rd_copied, 1)
                    for w in LONG_LAST:
                        long(w)
                        if w == LONG_LAST[0]:
                            act.wait_ge(sc_done, p.it + 1)
                            nc.scalar.activation(At[:], Sc[:], ACT.Exp, scale=SCALE).then_inc(ex_done, 1)
                    for g in range(NG):
                        evacuate(RVT[:, g * GT:(g + 1) * GT], a_full("rvT", g)[0:KD, :])
                    for w in range(NW):
                        act.wait_ge(y_done, p.it * NW + (w + 1))
                        nc.scalar.activation(Sq, XA[:, w, :], ACT.Square, accum_out=Rr[:, w:w + 1]).then_inc(ysq_done, 1)
                        act.wait_ge(ysq_done, p.it * NW + (w + 1))
                    for w in range(NW):
                        evacuate(YNT[:, :, w * P:(w + 1) * P],
                                 a_full("ynT", w)[:, 0:D].rearrange("p (c t) -> p c t", c=NC))

                passes(act, body)

            @block.gpsimd
            def _(pool):
                nc.gpsimd.memset(Half[:], -0.5).then_inc(s_set, 1)
                nc.gpsimd.memset(XNT[:, :, 0:PAD], 0.0).then_inc(s_set, 1)
                nc.gpsimd.memset(D1[:], 0.0).then_inc(s_set, 1)
                nc.gpsimd.memset(S[:, 0:1], 0.0).then_inc(s_set, 1)
                nc.gpsimd.memset(Ones[:], 1.0).then_inc(s_set, 1)
                nc.gpsimd.memset(OnesH[:], 1.0).then_inc(s_set, 1)
                nc.gpsimd.memset(Eps[:, 0, :], LN_EPS).then_inc(s_set, 1)
                nc.gpsimd.memset(Eps[:, 1, :], RMS_EPS).then_inc(s_set, 1)
                pool.sem_inc(res_done, NW)
                pool.wait_ge(s_set, 8)
                pool.wait_ge(s_c, 4 * 16)

                def body(p):
                    steps = [0]

                    def written(ins):
                        steps[0] += 1
                        ins.then_inc(p_own_result, 1)
                        pool.wait_ge(p_own_result, p.it * P_OWN_RESULTS + steps[0])

                    def rsqrt_var1(g):
                        pool.wait_ge(mv1_done, p.it * NG + (g + 1 - NG))
                        nc.gpsimd.tensor_tensor(Rd1[:], Rd1[:], Half[:, 0:WPG], ALU.pow).then_inc(rd1_done, 1)

                    if p.cur:
                        pool.wait_ge(mv_done, p.it + 1)
                        var = Mv[:, :, 1]
                        written(nc.gpsimd.tensor_tensor(Rr[:], var, Eps[:, 0, :], ALU.add))
                        written(nc.gpsimd.tensor_tensor(Rd[:], Rr[:], Half[:], ALU.pow))
                        written(nc.gpsimd.tensor_tensor(Rr[:], Rd[:], Rd[:], ALU.mult))
                        written(nc.gpsimd.tensor_tensor(Rr[:], Rr[:], var, ALU.mult))
                        written(nc.gpsimd.tensor_tensor(Rr[:], Rr[:], Eps[:, 1, :], ALU.add))
                        nc.gpsimd.tensor_tensor(Rr[:], Rr[:], Half[:], ALU.pow).then_inc(rr_done, 1)
                    if p.prev:
                        rsqrt_var1(0)
                    if p.cur:
                        pool.wait_ge(idx_done, p.it + 1)
                        for w in range(NW):
                            if w >= 2:
                                pool.wait_ge(a_ready, p.a("rows", w - 2) + 1)
                            nc.gpsimd.tensor_tensor(DG[:, w % 2], bcast(Id[:], 0, 2 * H), bcast(Idx[:, w, :], 1, P),
                                                    ALU.mult).then_inc(dg_done, 1)
                        pool.wait_ge(keep_done, p.it + 1)
                        for w in range(NW):
                            if w >= 2:
                                g, i = divmod(w - 2, WPG)
                                if i == WPG - 1:
                                    pool.wait_ge(a_ready, p.a("keep", g) + 1)
                                else:
                                    pool.wait_ge(do_used, p.it * (NG * (WPG - 1)) + (g * (WPG - 1) + i + 1))
                            nc.gpsimd.tensor_tensor(DO[:, w % 2, :], Id[:], bcast1(Keep[:, w:w + 1], P), ALU.mult).then_inc(do_done, 1)
                        for h in range(H):
                            pool.wait_ge(slotc_done, p.it * H + (h + 1))
                            for a in range(ASSOC):
                                nc.gpsimd.tensor_tensor(KVM[:, h, :, a, :], Z[:, :, ZK:ZK + 2 * KD], bcast(SlotC[:, h, a, :], 1, 2 * KD),
                                                        ALU.mult).then_inc(kvm_done, 1)
                    if p.prev:
                        rsqrt_var1(1)
                    if not p.cur:
                        return
                    for w in range(NW):
                        pool.wait_ge(a_free, p.a("long", w) + 3)
                        nc.gpsimd.tensor_tensor(XA[:, w, :], XA[:, w, :], XN[:, w, :], ALU.add).then_inc(yl_added, 1)
                    for g in range(NG):
                        ws = slice(g * WPG, (g + 1) * WPG)
                        pool.wait_ge(yv_done, p.it * NG + (g + 1))
                        nc.gpsimd.tensor_tensor(Rd[:, ws], Rd[:, ws], Half[:, ws], ALU.pow).then_inc(yr_done, 1)
                    if p.prev:
                        pool.wait_ge(x2_done, p.it * NW)
                    for w in range(NW):
                        pool.wait_ge(y_done, p.it * NW + (w + 1))
                        pool.wait_ge(x1_st[w], p.it * 16 + 16)
                        nc.gpsimd.tensor_tensor(Y[:, w, :], XA[:, w, :], X[:, w, :], ALU.add).then_inc(res_done, 1)
                    for w in range(NW):
                        pool.wait_ge(res_done, p.it * NW + (NW + w + 1))
                        nc.gpsimd.tensor_tensor(Y[:, w, :], Y[:, w, :], DownB, ALU.add).then_inc(y_biased, 1)
                    assert steps[0] == P_OWN_RESULTS, steps[0]

                passes(pool, body)

            @block.vector
            def _(dve):
                dve.sem_inc(d_free, 2)
                dve.wait_ge(s_c, 4 * 16)
                dve.wait_ge(s_set, 8)

                def body(p):
                    steps, lag_steps = [0], [0]

                    def written(ins):
                        steps[0] += 1
                        ins.then_inc(v_own_result, 1)
                        dve.wait_ge(v_own_result, p.it * V_OWN_RESULTS + steps[0])

                    def lag_written(ins):
                        lag_steps[0] += 1
                        ins.then_inc(v_own_statistics, 1)
                        dve.wait_ge(v_own_statistics, p.it * V_OWN_STATISTICS + (lag_steps[0] - V_OWN_STATISTICS))

                    def d_full(*key):
                        dve.wait_ge(d_ready, p.d_base + (p.D[key] + 1))
                        return d_ps[:, p.D[key] % 2, :]

                    def d_written(*key):
                        dve.wait_ge(d_free, p.d_base + (p.D[key] + 3))

                    def a_emptied(*key):
                        dve.wait_ge(a_free, p.a(*key) + 3)

                    def x1_finished(w):
                        bank = d_full("down", w)
                        dve.wait_ge(y_biased, p.it * NW + (w + 1 - NW))
                        nc.vector.tensor_tensor(Y[:, w, :], bank[:, 0:D], Y[:, w, :], ALU.add).then_inc(d_free, 1)
                        d_written("down", w)
                        dve.sem_inc(x1_done, 1)
                        nc.vector.bn_stats(Bn1[:, w % WPG, :], Y[:, w, :]).then_inc(bn1_done, 1)

                    def x1_normalised(g):
                        dve.wait_ge(bn1_done, p.it * NW + ((g + 1) * WPG - NW))
                        dve.sem_inc(bn_taken, 1)
                        for i in range(WPG):
                            last = nc.vector.bn_aggr(Mv1[:, i, :], Bn1[:, i, :])
                        lag_written(last)
                        nc.vector.tensor_scalar(Rd1[:], Mv1[:, :, 1], LN_EPS, None, ALU.add).then_inc(mv1_done, 1)
                        dve.wait_ge(rd1_done, p.it * NG + (g + 1 - NG))
                        for i in range(WPG):
                            dve.wait_ge(x2_st[i], p.it * (NG * 16) + (g + 1 - NG) * 16)
                            nc.vector.tensor_scalar(X2[:, i, :], Y[:, g * WPG + i, :], Mv1[:, i, 0:1], Rd1[:, i:i + 1],
                                                    ALU.subtract, ALU.mult).then_inc(x2_done, 1)

                    def y_mean_squares(g):
                        ws = slice(g * WPG, (g + 1) * WPG)
                        dve.wait_ge(ysq_done, p.it * NW + (g + 1) * WPG)
                        nc.vector.tensor_scalar(Rd[:, ws], Rr[:, ws], 1.0 / D, RMS_EPS, ALU.mult, ALU.add).then_inc(yv_done, 1)

                    if p.cur:
                        for w in range(NW):
                            dve.wait_ge(s_x[w], p.it * 16 + 16)
                            last = nc.vector.bn_stats(Bn[:, w, :], X[:, w, :])
                        written(last)
                        dve.sem_inc(bn_taken, 1)
                        for w in range(NW):
                            last = nc.vector.bn_aggr(Mv[:, w, :], Bn[:, w, :])
                        last.then_inc(mv_done, 1)
                        dve.wait_ge(rr_done, p.it + 1)
                        for w in range(NW):
                            last = nc.vector.tensor_scalar(XA[:, w, :], X[:, w, :], Mv[:, w, 0:1], Rd[:, w:w + 1], ALU.subtract, ALU.mult)
                            if w == NW - 1:
                                written(last)
                        dve.wait_ge(a_free, p.a_base + 2)
                        for w in range(NW):
                            nc.vector.tensor_scalar(XN[:, w, :], XA[:, w, :], Rr[:, w:w + 1], None, ALU.mult).then_inc(xn_done, 1)
                        if p.prev:
                            for w in DOWN_FIRST:
                                x1_finished(w)
                        a_emptied("xnT", NW - 1)
                        for j in range(CONV_K):
                            for c in range(NC):
                                src = XNT[:, c, j:j + T]
                                if j == 0:
                                    last = nc.vector.tensor_scalar(HC[:, c, :], src, ConvW[:, c, 0:1], None, ALU.mult)
                                else:
                                    last = nc.vector.scalar_tensor_tensor(HC[:, c, :], src, ConvW[:, c, j:j + 1], HC[:, c, :], ALU.mult, ALU.add)
                                if j == CONV_K - 1:
                                    last.then_inc(conv_done, 1)
                                else:
                                    written(last)
                        for g in range(NG):
                            for c in range(NC):
                                i = g * NC + c
                                toks = slice(g * GT, (g + 1) * GT)
                                dve.wait_ge(silu_done, p.it * (NG * NC) + (i + 1))
                                dve.wait_ge(sg_done, p.it * (NG * NC) + (i + 1))
                                nc.vector.tensor_tensor(UT[:, c, toks], UT[:, c, toks], SG[:, i, :], ALU.mult).then_inc(ut_done, 1)
                    if p.prev:
                        for w in range(DOWN_FIRST.stop if p.cur else 0, WPG):
                            x1_finished(w)
                        x1_normalised(0)
                    if p.cur:
                        dve.wait_ge(z_copied, p.it + 1)
                        written(nc.vector.scalar_tensor_tensor(Bits, Z[:, :, 0:2 * H * BITS], 0.0, bcast(Pow, 0, NW), ALU.is_gt, ALU.mult))
                        written(nc.vector.reduce_sum(Idx[:].rearrange("p w a -> p (w a)"), Bits.rearrange("p w (a n) -> p (w a) n", n=BITS), AX))
                        nc.vector.tensor_scalar(Idx[:, :, 0:H], Idx[:, :, 0:H], float(BUCKETS - 1), None, ALU.min).then_inc(idx_done, 1)
                        dve.wait_ge(gt_done, p.it * 3 + 3)
                        nc.vector.tensor_scalar(Keep[:], Gt[:, 0, :], -1.0, 1.0, ALU.mult, ALU.add).then_inc(keep_done, 1)
                        dve.wait_ge(ut_done, p.it * (NG * NC) + NG * NC)
                        if not p.prev:
                            dve.wait_ge(dec_done, 1)
                            dve.wait_ge(a_free, PRE + 2)
                        for k in range(K):
                            for c in range(NC):
                                nc.vector.tensor_tensor_scan(SS[:, k, c, :], bcast1(Dec[:, k:k + 1], T), UT[:, c, :], 0.0,
                                                             ALU.mult, ALU.add).then_inc(ss_done, 1)
                    if not p.cur:
                        for w in range(WPG, NW):
                            x1_finished(w)
                        x1_normalised(1)
                        return
                    dve.wait_ge(idx_done, p.it + 1)
                    a_emptied("rows", NW - 1)
                    for h in range(H):
                        if h:
                            dve.wait_ge(owp_done, p.it * H + h)
                        written(nc.vector.tensor_scalar(OW[:], Row[:, H + h, :], Iota, None, ALU.is_equal))
                        written(nc.vector.tensor_tensor_scan(Par, OW[:], bcast1(S[:, 0:1], T), 0.0, ALU.not_equal, ALU.add))
                        nc.vector.tensor_tensor(OWP[:, h, :], OW[:], Par, ALU.mult).then_inc(owp_done, 1)
                    if p.prev:
                        for w in range(WPG, DOWN_LAST.start):
                            x1_finished(w)
                    for h in range(H):
                        for g in range(NG):
                            row = Row[:, H + h, g * GT:(g + 1) * GT]
                            nc.vector.scalar_tensor_tensor(row, row, 2.0, d_full("slot_row", h, g), ALU.mult, ALU.add).then_inc(d_free, 1)
                        written(nc.vector.tensor_copy(SlotC[:, h, 0, :], d_full("slot_col", h)[:, 0:NW]))
                        dve.sem_inc(d_free, 1)
                        nc.vector.tensor_scalar(SlotC[:, h, 1, :], SlotC[:, h, 0, :], -1.0, 1.0, ALU.mult, ALU.add).then_inc(slotc_done, 1)
                        written(nc.vector.scalar_tensor_tensor(CellC[:, h, :], Idx[:, :, H + h], 2.0, SlotC[:, h, 0, :], ALU.mult, ALU.add))
                    d_written("slot_col", H - 1)
                    a_emptied("keep", NG - 1)
                    for h in range(H):
                        if h and p.prev:
                            x1_normalised(1)
                        for i in range(NW):
                            n = T - i * P
                            t0 = i * P
                            nc.vector.tensor_scalar(D1[:, 0:P], Id[:], Gt[:, 0, i:i + 1], None, ALU.mult)
                            written(nc.vector.scalar_tensor_tensor(A0[:, 0:n], Row[:, H + h, t0:T], CellC[:, h, i:i + 1], KeepRow[:, t0:T],
                                                                   ALU.not_equal, ALU.max))
                            written(nc.vector.tensor_tensor_scan(S[:, 1:1 + n], A0[:, 0:n], D1[:, 0:n], 0.0, ALU.mult, ALU.add))
                            j = h * NW + i
                            if j >= 2:
                                dve.wait_ge(w_used, p.it * (H * NW) + (j - 1))
                            written(nc.vector.scalar_tensor_tensor(W[:, i % 2, 0:n], Row[:, h, t0:T], Idx[:, i, H + h:H + h + 1], S[:, 0:n],
                                                                   ALU.is_equal, ALU.mult))
                            dve.sem_inc(w_done, 1)
                            if h == i == 0 and p.prev:
                                for w in DOWN_LAST:
                                    x1_finished(w)
                    dve.wait_ge(rd_copied, p.it * H + (H + 1))
                    written(nc.vector.tensor_tensor(PR, RD[:, :, :, 0:KD], bcast(Z[:, :, ZQ:ZQ + KD], 1, H * ASSOC), ALU.mult))
                    written(nc.vector.reduce_sum(Sc[:], PR, AX))
                    written(nc.vector.reduce_max(Sm[:], Sc[:], AX))
                    nc.vector.tensor_tensor(Sc[:], Sc[:], bcast(Sm[:], 1, H * ASSOC), ALU.subtract).then_inc(sc_done, 1)
                    dve.wait_ge(ex_done, p.it + 1)
                    written(nc.vector.reduce_sum(Sm[:], At[:], AX))
                    written(nc.vector.reciprocal(Sm[:], Sm[:]))
                    written(nc.vector.tensor_tensor(Sm[:], Sm[:], Gt[:, 2, :], ALU.mult))
                    written(nc.vector.tensor_tensor(At[:], At[:], bcast(Sm[:], 1, H * ASSOC), ALU.mult))
                    written(nc.vector.tensor_tensor(PR, RD[:, :, :, KD:2 * KD], bcast(At[:], 2, KD), ALU.mult))
                    nc.vector.reduce_sum(Rdv, PR.rearrange("p w a d -> p w d a"), AX).then_inc(rdv_done, 1)
                    for w in range(NW):
                        dve.wait_ge(yl_added, p.it * NW + (w + 1))
                        nc.vector.tensor_tensor(XA[:, w, :], d_full("mem", w)[:, 0:D], XA[:, w, :], ALU.add).then_inc(d_free, 1)
                        d_written("mem", w)
                        dve.sem_inc(y_done, 1)
                        if w == WPG + 1:
                            y_mean_squares(0)
                    y_mean_squares(1)
                    for g in range(NG):
                        dve.wait_ge(yr_done, p.it * NG + (g + 1))
                        for w in range(g * WPG, (g + 1) * WPG):
                            nc.vector.tensor_scalar(XN[:, w, :], XA[:, w, :], Rd[:, w:w + 1], None, ALU.mult).then_inc(yn_done, 1)
                    assert steps[0] == V_OWN_RESULTS, steps[0]

                passes(dve, body)


def attn_arrays(inp):
    f = np.float32

    def g(name):
        return inp["L0_attn_" + name]

    convw = np.ascontiguousarray(g("conv_w").reshape(NC, P, CONV_K).transpose(1, 0, 2))
    cols = np.concatenate([g("gate_b").reshape(NC, P).T, g("mlp_up_b").reshape(NU, P).T], 1)
    wcat = np.concatenate([g("read_bits_w"), g("write_bits_w"), g("qkey_w"), g("wkey_w"), g("value_w"),
                           g("write_gate_w"), g("gate_long_w"), g("gate_mem_w")], 0).T
    pw = np.tile(2.0 ** np.arange(BITS), 2 * H).astype(f)
    row = np.concatenate([pw, g("state_decay_logit"), g("write_gate_b"), g("gate_long_b"), g("gate_mem_b"), g("mlp_down_b")])
    rv = np.concatenate([np.broadcast_to(row[None], (P, row.size)), np.arange(P, dtype=f)[:, None]], 1)
    return {"gate_wt": g("gate_w").T, "conv_w": convw, "cols": cols, "wcat": wcat, "state_in": g("state_in_w"),
            "state_out_t": g("state_out_w").T, "mem_out_t": g("mem_out_w").T, "up_wt": g("mlp_up_w").T,
            "down_wt": g("mlp_down_w").T, "rowsv": rv}


def build(nc, d, x1, x2, y0, out):
    build_attn(nc, d["x"], x1, x2, *(d[n] for n in ATTN_NAMES), d["ident"])
    build_ffn(nc, x2, x1, y0, out, *(d[n] for n in FFN_NAMES))


ATTN_NAMES = ("gate_wt", "conv_w", "cols", "wcat", "state_in", "state_out_t", "mem_out_t", "up_wt", "down_wt", "rowsv")
FFN_NAMES = ("wqkv", "wo", "w1", "w2", "pvec", "qs2", "b2", "tabc", "tabs", "ident", "maskd")


def kernel(**inputs):
    import numpy as _np
    import concourse.bacc as _bacc
    from concourse.bass_utils import run_bass_kernel_spmd as _run

    inp = {k: _np.asarray(v) for k, v in inputs.items()}
    arrays = {**attn_arrays(inp), **ffn_arrays(inp), "x": inp["L0_attn_x"]}
    arrays = {k: _np.ascontiguousarray(v) for k, v in arrays.items()}
    nc = _bacc.Bacc("TRN2", target_bir_lowering=False, num_devices=1)
    d = {k: nc.dram_tensor(k, v.shape, F32, kind="ExternalInput").ap() for k, v in arrays.items()}
    scratch = [nc.dram_tensor(n, (B, T, D), F32, kind="Internal").ap() for n in ("x1", "x2", "y0")]
    out = nc.dram_tensor("out", (B, T, D), F32, kind="ExternalOutput").ap()
    build(nc, d, *scratch, out)
    r = _run(nc, [arrays], core_ids=[0])
    return r.results[0]["out"]
```
